# Optimizing a Trainium2 kernel written in Bass

```python
import numpy as np
import jax
import jax.numpy as jnp

def _softmax(x, axis=-1):
    return jax.nn.softmax(x, axis=axis)

def _gelu(x):
    return jax.nn.gelu(x, approximate=True)

def _silu(x):
    return jax.nn.silu(x)

def _sigmoid(x):
    return jax.nn.sigmoid(x)

def _layernorm(x, axis=-1, eps=1e-05):
    m = jnp.mean(x, axis=axis, keepdims=True)
    v = jnp.var(x, axis=axis, keepdims=True)
    return (x - m) / jnp.sqrt(v + eps)

def _scatter_add(tgt, idx, src, axis=0):
    return tgt.at[idx].add(src)

def _segment_sum(src, seg, n):
    return jax.ops.segment_sum(src, seg, n)
kernel_name = 'mk_flamingo_gated_d2_seqx_r8_0cca89'

def setup_inputs(seed: int=0):
    np.random.seed(seed)
    _w = jnp.asarray

    def _rec_inputs():
        import jax
        import jax.numpy as jnp
        _rk = jax.random.key(seed)
        x = 7.22e-05 + 1 * jax.random.normal(jax.random.fold_in(_rk, 1), (2, 512, 128), jnp.float32)
        _lenS = 512 - jax.random.randint(jax.random.fold_in(_rk, 7), (2,), 0, max(1, 512 // 4) + 1, jnp.int32)
        _lenS2 = 32 - jax.random.randint(jax.random.fold_in(_rk, 8), (2,), 0, max(1, 32 // 4) + 1, jnp.int32)
        _ctx_1024P = jax.random.normal(jax.random.fold_in(_rk, 11), (2, 16, 128), jnp.float32)
        _ctx_1024c = jax.random.dirichlet(jax.random.fold_in(_rk, 511), 0.3 * jnp.ones((16,), jnp.float32), (2, 32))
        _ctx_1024t = jnp.einsum('bsk,bkd->bsd', _ctx_1024c, _ctx_1024P)
        _ctx_1024t = _ctx_1024t * jax.lax.rsqrt(jnp.mean(jnp.square(_ctx_1024t)) + 1e-12) * 0.953939
        ctx_1024 = 4.13588e-05 + 0.999923 * (_ctx_1024t + 0.3 * jax.random.normal(jax.random.fold_in(_rk, 611), (2, 32, 128), jnp.float32))
        _validS = jnp.arange(512)[None, :] < _lenS[:, None]
        _validS2 = jnp.arange(32)[None, :] < _lenS2[:, None]
        _causal = jnp.tril(jnp.ones((512, 512), dtype=bool))
        mask_Bx1xSxS2_bk1 = jnp.broadcast_to(_validS2[:, None, None, :], (2, 1, 512, 32))
        _g = jax.random.normal(jax.random.fold_in(_rk, 9001), (2, 2), jnp.float32)
        _g = jnp.sign(_g) * jnp.maximum(jnp.abs(_g), 1.0) + (_g == 0) * 1.0
        g_xattn = _g[0]
        g_ffn = _g[1]
        return (x, ctx_1024, mask_Bx1xSxS2_bk1, g_xattn, g_ffn)
    x, ctx_1024, mask_Bx1xSxS2_bk1, g_xattn, g_ffn = _rec_inputs()

    def _L0_xattn_setup():
        import jax, jax.numpy as jnp
        import numpy as np
        import math
        D_MODEL = 128
        NHEAD = 16
        D_K = D_MODEL // NHEAD
        B, S = (4, 256)

        def _stable_softmax(scores):
            m = jnp.max(scores, axis=-1, keepdims=True)
            e = jnp.exp(scores - m)
            return e / (jnp.sum(e, axis=-1, keepdims=True) + 1e-10)
        key = jax.random.key(seed)
        ks = jax.random.split(key, 11)
        gain = math.sqrt(2.0)
        bound = gain * math.sqrt(6.0 / (2 * D_MODEL))

        def xavier(k):
            return jax.random.uniform(k, (D_MODEL, D_MODEL), jnp.float32, -bound, bound)
        return {'q': jax.random.normal(ks[0], (B, S, D_MODEL), jnp.float32), 'k': jax.random.normal(ks[1], (B, S, D_MODEL), jnp.float32), 'v': jax.random.normal(ks[2], (B, S, D_MODEL), jnp.float32), 'Wq': xavier(ks[3]), 'bq': jnp.zeros((D_MODEL,), jnp.float32), 'Wk': xavier(ks[4]), 'bk': jnp.zeros((D_MODEL,), jnp.float32), 'Wv': xavier(ks[5]), 'bv': jnp.zeros((D_MODEL,), jnp.float32), 'Wo': xavier(ks[6]), 'bo': jnp.zeros((D_MODEL,), jnp.float32)}
    _L0_xattn_all = _L0_xattn_setup()
    _L0_xattn_in = {k: v for k, v in _L0_xattn_all.items() if k in ('Wq', 'bq', 'Wk', 'bk', 'Wv', 'bv', 'Wo', 'bo')}
    del _L0_xattn_all

    def _L0_ffn_setup():
        import jax, jax.numpy as jnp
        import numpy as np
        D = 128
        H = 16
        HD = D // H
        L = 64
        E = 8
        B, T = (4, 256)
        EPS = 1e-06

        def _glorot(k, shape):
            fan_in, fan_out = (shape[-2], shape[-1])
            lim = np.sqrt(6.0 / (fan_in + fan_out)).astype(np.float32)
            return jax.random.uniform(k, shape, jnp.float32, -lim, lim)

        def _rmsnorm(x, gamma):
            return gamma * x * jax.lax.rsqrt(jnp.mean(x * x, axis=-1, keepdims=True) + EPS)
        key = jax.random.key(seed)
        ks = jax.random.split(key, 8)
        return {'x': jax.random.normal(ks[0], (B, T, D), jnp.float32), 'gamma1': jnp.ones((D,), jnp.float32), 'Wq': _glorot(ks[1], (D, D)), 'bq': jnp.zeros((D,), jnp.float32), 'Wdown': _glorot(ks[2], (D, L)), 'bdown': jnp.zeros((L,), jnp.float32), 'Wup': _glorot(ks[3], (L, 2 * D)), 'bup': jnp.zeros((2 * D,), jnp.float32), 'Wo': _glorot(ks[4], (D, D)), 'bo': jnp.zeros((D,), jnp.float32), 'gamma2': jnp.ones((D,), jnp.float32), 'Wg': _glorot(ks[5], (D, E)), 'bg': jnp.zeros((E,), jnp.float32), 'We': _glorot(ks[6], (E, D, D))}
    _L0_ffn_all = _L0_ffn_setup()
    _L0_ffn_in = {k: v for k, v in _L0_ffn_all.items() if k in ('gamma1', 'Wq', 'bq', 'Wdown', 'bdown', 'Wup', 'bup', 'Wo', 'bo', 'gamma2', 'Wg', 'bg', 'We')}
    del _L0_ffn_all

    def _L1_xattn_setup():
        import jax, jax.numpy as jnp
        import numpy as np
        EMBED = 128
        HEADS = 16
        HEAD_DIM = EMBED // HEADS
        B, S = (4, 256)

        def _split_heads(x):
            b, s, _ = x.shape
            return x.reshape(b, s, HEADS, HEAD_DIM).transpose(0, 2, 1, 3)
        key = jax.random.key(seed)
        ks = jax.random.split(key, 13)
        scale = 1.0 / np.sqrt(EMBED)
        inp = {'query': jax.random.normal(ks[0], (B, S, EMBED), dtype=jnp.float32), 'key': jax.random.normal(ks[1], (B, S, EMBED), dtype=jnp.float32), 'value': jax.random.normal(ks[2], (B, S, EMBED), dtype=jnp.float32), 'mask': jax.random.randint(ks[3], (B, 1, S, S), 0, 2) > 0, 'Wq': jax.random.normal(ks[4], (EMBED, EMBED), dtype=jnp.float32) * scale, 'bq': jnp.zeros((EMBED,), dtype=jnp.float32), 'Wk': jax.random.normal(ks[5], (EMBED, EMBED), dtype=jnp.float32) * scale, 'bk': jnp.zeros((EMBED,), dtype=jnp.float32), 'Wv': jax.random.normal(ks[6], (EMBED, EMBED), dtype=jnp.float32) * scale, 'bv': jnp.zeros((EMBED,), dtype=jnp.float32), 'Wo': jax.random.normal(ks[7], (EMBED, EMBED), dtype=jnp.float32) * scale, 'bo': jnp.zeros((EMBED,), dtype=jnp.float32)}
        return inp
    _L1_xattn_all = _L1_xattn_setup()
    _L1_xattn_in = {k: v for k, v in _L1_xattn_all.items() if k in ('Wq', 'bq', 'Wk', 'bk', 'Wv', 'bv', 'Wo', 'bo')}
    del _L1_xattn_all

    def _L1_ffn_setup():
        import jax, jax.numpy as jnp
        import numpy as np
        B, L, D = (1, 256, 128)
        E, H, G, K = (64, 32, 64, 16)

        def _grouped_routing_scores(router_scores):
            T, En = router_scores.shape
            Tq = T // G
            budget = Tq * K
            order = jnp.argsort(-router_scores, axis=0)
            sorted_vals = jnp.take_along_axis(router_scores, order, axis=0)
            group_score = sorted_vals.reshape(Tq, G, En).sum(axis=1)
            _, top_flat = jax.lax.top_k(group_score.reshape(-1), budget)
            gmask = jnp.zeros((Tq * En,), bool).at[top_flat].set(True).reshape(Tq, En)
            mask_sorted = jnp.broadcast_to(gmask[:, None, :], (Tq, G, En)).reshape(T, En)
            mask = jnp.zeros((T, En), bool).at[order, jnp.arange(En)[None, :]].set(mask_sorted)
            fs = jnp.where(mask, router_scores, 0.0)
            return fs / (fs.sum(axis=-1, keepdims=True) + 1e-06)
        key = jax.random.key(seed)
        ks = jax.random.split(key, 6)
        s = lambda k, shape, scale: jax.random.normal(k, shape, jnp.float32) * scale
        return {'x': jax.random.normal(ks[0], (B, L, D), jnp.float32), 'Wr': s(ks[1], (D, E), D ** (-0.5)), 'br': jnp.zeros((E,), jnp.float32), 'Wup': s(ks[2], (E, D, H), D ** (-0.5)), 'bup': jnp.zeros((E, H), jnp.float32), 'Wgate': s(ks[3], (E, D, H), D ** (-0.5)), 'bgate': jnp.zeros((E, H), jnp.float32), 'Wdown': s(ks[4], (E, H, D), H ** (-0.5)), 'bdown': jnp.zeros((E, D), jnp.float32)}
    _L1_ffn_all = _L1_ffn_setup()
    _L1_ffn_in = {k: v for k, v in _L1_ffn_all.items() if k in ('Wr', 'br', 'Wup', 'bup', 'Wgate', 'bgate', 'Wdown', 'bdown')}
    del _L1_ffn_all
    return {'x': x, 'ctx_1024': ctx_1024, 'mask_Bx1xSxS2_bk1': mask_Bx1xSxS2_bk1, 'g_xattn': g_xattn, 'g_ffn': g_ffn, 'L0_xattn_Wq': _L0_xattn_in['Wq'], 'L0_xattn_bq': _L0_xattn_in['bq'], 'L0_xattn_Wk': _L0_xattn_in['Wk'], 'L0_xattn_bk': _L0_xattn_in['bk'], 'L0_xattn_Wv': _L0_xattn_in['Wv'], 'L0_xattn_bv': _L0_xattn_in['bv'], 'L0_xattn_Wo': _L0_xattn_in['Wo'], 'L0_xattn_bo': _L0_xattn_in['bo'], 'L0_ffn_gamma1': _L0_ffn_in['gamma1'], 'L0_ffn_Wq': _L0_ffn_in['Wq'], 'L0_ffn_bq': _L0_ffn_in['bq'], 'L0_ffn_Wdown': _L0_ffn_in['Wdown'], 'L0_ffn_bdown': _L0_ffn_in['bdown'], 'L0_ffn_Wup': _L0_ffn_in['Wup'], 'L0_ffn_bup': _L0_ffn_in['bup'], 'L0_ffn_Wo': _L0_ffn_in['Wo'], 'L0_ffn_bo': _L0_ffn_in['bo'], 'L0_ffn_gamma2': _L0_ffn_in['gamma2'], 'L0_ffn_Wg': _L0_ffn_in['Wg'], 'L0_ffn_bg': _L0_ffn_in['bg'], 'L0_ffn_We': _L0_ffn_in['We'], 'L1_xattn_Wq': _L1_xattn_in['Wq'], 'L1_xattn_bq': _L1_xattn_in['bq'], 'L1_xattn_Wk': _L1_xattn_in['Wk'], 'L1_xattn_bk': _L1_xattn_in['bk'], 'L1_xattn_Wv': _L1_xattn_in['Wv'], 'L1_xattn_bv': _L1_xattn_in['bv'], 'L1_xattn_Wo': _L1_xattn_in['Wo'], 'L1_xattn_bo': _L1_xattn_in['bo'], 'L1_ffn_Wr': _L1_ffn_in['Wr'], 'L1_ffn_br': _L1_ffn_in['br'], 'L1_ffn_Wup': _L1_ffn_in['Wup'], 'L1_ffn_bup': _L1_ffn_in['bup'], 'L1_ffn_Wgate': _L1_ffn_in['Wgate'], 'L1_ffn_bgate': _L1_ffn_in['bgate'], 'L1_ffn_Wdown': _L1_ffn_in['Wdown'], 'L1_ffn_bdown': _L1_ffn_in['bdown']}

def reference(x, ctx_1024, mask_Bx1xSxS2_bk1, g_xattn, g_ffn, L0_xattn_Wq, L0_xattn_bq, L0_xattn_Wk, L0_xattn_bk, L0_xattn_Wv, L0_xattn_bv, L0_xattn_Wo, L0_xattn_bo, L0_ffn_gamma1, L0_ffn_Wq, L0_ffn_bq, L0_ffn_Wdown, L0_ffn_bdown, L0_ffn_Wup, L0_ffn_bup, L0_ffn_Wo, L0_ffn_bo, L0_ffn_gamma2, L0_ffn_Wg, L0_ffn_bg, L0_ffn_We, L1_xattn_Wq, L1_xattn_bq, L1_xattn_Wk, L1_xattn_bk, L1_xattn_Wv, L1_xattn_bv, L1_xattn_Wo, L1_xattn_bo, L1_ffn_Wr, L1_ffn_br, L1_ffn_Wup, L1_ffn_bup, L1_ffn_Wgate, L1_ffn_bgate, L1_ffn_Wdown, L1_ffn_bdown):
    import jax
    import jax.numpy as jnp

    def _L0_xattn_ref(q, k, v, Wq, bq, Wk, bk, Wv, bv, Wo, bo):
        import jax, jax.numpy as jnp
        import numpy as np
        import math
        D_MODEL = 128
        NHEAD = 16
        D_K = D_MODEL // NHEAD
        B, S = (4, 256)

        def _stable_softmax(scores):
            m = jnp.max(scores, axis=-1, keepdims=True)
            e = jnp.exp(scores - m)
            return e / (jnp.sum(e, axis=-1, keepdims=True) + 1e-10)
        b = q.shape[0]
        Q = q @ Wq.T + bq
        K = k @ Wk.T + bk
        V = v @ Wv.T + bv
        Q = Q.reshape(b, -1, NHEAD, D_K).transpose(0, 2, 1, 3)
        K = K.reshape(b, -1, NHEAD, D_K).transpose(0, 2, 1, 3)
        V = V.reshape(b, -1, NHEAD, D_K).transpose(0, 2, 1, 3)
        scores = jnp.einsum('bhqd,bhkd->bhqk', Q / math.sqrt(D_K), K)
        attn_weight = _stable_softmax(scores)
        attn = jnp.einsum('bhqk,bhkd->bhqd', attn_weight, V)
        concat = attn.transpose(0, 2, 1, 3).reshape(b, -1, D_MODEL)
        return concat @ Wo.T + bo

    def _L0_ffn_ref(x, gamma1, Wq, bq, Wdown, bdown, Wup, bup, Wo, bo, gamma2, Wg, bg, We):
        import jax, jax.numpy as jnp
        import numpy as np
        D = 128
        H = 16
        HD = D // H
        L = 64
        E = 8
        B, T = (4, 256)
        EPS = 1e-06

        def _glorot(k, shape):
            fan_in, fan_out = (shape[-2], shape[-1])
            lim = np.sqrt(6.0 / (fan_in + fan_out)).astype(np.float32)
            return jax.random.uniform(k, shape, jnp.float32, -lim, lim)

        def _rmsnorm(x, gamma):
            return gamma * x * jax.lax.rsqrt(jnp.mean(x * x, axis=-1, keepdims=True) + EPS)
        b, t = (x.shape[0], x.shape[1])
        h = _rmsnorm(x, gamma1)
        q = (h @ Wq + bq).reshape(b, t, H, HD)
        kv = ((h @ Wdown + bdown) @ Wup + bup).reshape(b, t, H, 2 * HD)
        k, v = jnp.split(kv, 2, axis=-1)
        att = jnp.einsum('bthd,btgd->bthg', q, k) / np.sqrt(HD).astype(np.float32)
        att = jax.nn.softmax(att, axis=-1)
        out = jnp.einsum('bthg,btgd->bthd', att, v).reshape(b, t, D)
        x = x + (out @ Wo + bo)
        h2 = _rmsnorm(x, gamma2)
        gate = jax.nn.softmax(h2 @ Wg + bg, axis=-1)
        combined = jnp.einsum('btd,edf,bte->btf', h2, We, gate)
        return x + combined

    def _L1_xattn_ref(query, key, value, mask, Wq, bq, Wk, bk, Wv, bv, Wo, bo):
        import jax, jax.numpy as jnp
        import numpy as np
        EMBED = 128
        HEADS = 16
        HEAD_DIM = EMBED // HEADS
        B, S = (4, 256)

        def _split_heads(x):
            b, s, _ = x.shape
            return x.reshape(b, s, HEADS, HEAD_DIM).transpose(0, 2, 1, 3)
        q = _split_heads(query @ Wq.T + bq)
        k = _split_heads(key @ Wk.T + bk)
        v = _split_heads(value @ Wv.T + bv)
        scores = jnp.einsum('bhqd,bhkd->bhqk', q, k) / jnp.sqrt(jnp.float32(HEAD_DIM))
        scores = jnp.where(mask, jnp.float32(-1000000000.0), scores)
        attn = jax.nn.softmax(scores, axis=-1)
        out = jnp.einsum('bhqk,bhkd->bhqd', attn, v)
        out = out.transpose(0, 2, 1, 3).reshape(out.shape[0], -1, EMBED)
        return out @ Wo.T + bo

    def _L1_ffn_ref(x, Wr, br, Wup, bup, Wgate, bgate, Wdown, bdown):
        import jax, jax.numpy as jnp
        import numpy as np
        B, L, D = (1, 256, 128)
        E, H, G, K = (64, 32, 64, 16)

        def _grouped_routing_scores(router_scores):
            T, En = router_scores.shape
            Tq = T // G
            budget = Tq * K
            order = jnp.argsort(-router_scores, axis=0)
            sorted_vals = jnp.take_along_axis(router_scores, order, axis=0)
            group_score = sorted_vals.reshape(Tq, G, En).sum(axis=1)
            _, top_flat = jax.lax.top_k(group_score.reshape(-1), budget)
            gmask = jnp.zeros((Tq * En,), bool).at[top_flat].set(True).reshape(Tq, En)
            mask_sorted = jnp.broadcast_to(gmask[:, None, :], (Tq, G, En)).reshape(T, En)
            mask = jnp.zeros((T, En), bool).at[order, jnp.arange(En)[None, :]].set(mask_sorted)
            fs = jnp.where(mask, router_scores, 0.0)
            return fs / (fs.sum(axis=-1, keepdims=True) + 1e-06)
        Bx, Lx, Dx = x.shape
        xt = x.reshape(-1, Dx)
        router_scores = jax.nn.softmax(xt @ Wr + br, axis=-1)
        fs = _grouped_routing_scores(router_scores)
        up = jnp.einsum('td,edh->teh', xt, Wup) + bup
        gate = jnp.einsum('td,edh->teh', xt, Wgate) + bgate
        h = jax.nn.silu(up) * gate * fs[:, :, None]
        out = jnp.einsum('teh,ehd->td', h, Wdown) + fs @ bdown
        return out.reshape(Bx, Lx, Dx)
    x = x + jnp.tanh(g_xattn[0]) * _L0_xattn_ref(_layernorm(x, axis=-1), ctx_1024, ctx_1024, L0_xattn_Wq, L0_xattn_bq, L0_xattn_Wk, L0_xattn_bk, L0_xattn_Wv, L0_xattn_bv, L0_xattn_Wo, L0_xattn_bo)
    x = x + jnp.tanh(g_ffn[0]) * _L0_ffn_ref(_layernorm(x, axis=-1), L0_ffn_gamma1, L0_ffn_Wq, L0_ffn_bq, L0_ffn_Wdown, L0_ffn_bdown, L0_ffn_Wup, L0_ffn_bup, L0_ffn_Wo, L0_ffn_bo, L0_ffn_gamma2, L0_ffn_Wg, L0_ffn_bg, L0_ffn_We)
    x = x + jnp.tanh(g_xattn[1]) * _L1_xattn_ref(_layernorm(x, axis=-1), ctx_1024, ctx_1024, mask_Bx1xSxS2_bk1, L1_xattn_Wq, L1_xattn_bq, L1_xattn_Wk, L1_xattn_bk, L1_xattn_Wv, L1_xattn_bv, L1_xattn_Wo, L1_xattn_bo)
    x = x + jnp.tanh(g_ffn[1]) * _L1_ffn_ref(_layernorm(x, axis=-1), L1_ffn_Wr, L1_ffn_br, L1_ffn_Wup, L1_ffn_bup, L1_ffn_Wgate, L1_ffn_bgate, L1_ffn_Wdown, L1_ffn_bdown)
    return x

_drawn_inputs = setup_inputs


def setup_inputs(seed=0):
    import zlib

    import numpy as np

    out = dict(_drawn_inputs(seed))
    spreads = {'g_ffn': (-1.0, 0.6),
     'L0_xattn_bq': (0.0, 0.1),
     'L0_xattn_bk': (0.0, 0.8),
     'L0_xattn_bv': (0.0, 0.1),
     'L0_xattn_bo': (0.0, 0.1),
     'L0_ffn_gamma1': (1.0, 0.2),
     'L0_ffn_bq': (0.0, 0.482),
     'L0_ffn_bdown': (0.0, 0.366),
     'L0_ffn_bup': (0.0, 0.1),
     'L0_ffn_bo': (0.0, 0.1),
     'L0_ffn_gamma2': (1.0, 0.2),
     'L0_ffn_bg': (0.0, 0.462),
     'L1_xattn_bq': (0.0, 0.531),
     'L1_xattn_bk': (0.0, 0.8),
     'L1_xattn_bv': (0.0, 0.1),
     'L1_xattn_bo': (0.0, 0.1),
     'L1_ffn_br': (0.0, 0.419),
     'L1_ffn_bup': (0.0, 0.667),
     'L1_ffn_bgate': (0.0, 0.627),
     'L1_ffn_bdown': (0.0, 0.369)}
    factors = {}
    for name, (base, spread) in spreads.items():
        noise = np.random.default_rng([zlib.crc32(name.encode()), seed]).standard_normal(out[name].shape)
        drawn = base * np.exp(spread * noise) if base else spread * noise
        out[name] = jnp.asarray(drawn.astype(out[name].dtype))
    for name, factor in factors.items():
        out[name] = (out[name] * factor).astype(out[name].dtype)
    return out
```

```python
from contextlib import ExitStack

import concourse.bass as bass
from concourse import mybir

ALU = mybir.AluOpType
ACT = mybir.ActivationFunctionType
AX = mybir.AxisListType
F32 = mybir.dt.float32
U8 = mybir.dt.uint8


def at_least(eng, sem, value):
    if value > 0:
        eng.wait_ge(sem, value)


class Steps:

    def __init__(self, eng, sem):
        self.eng, self.sem, self.n = eng, sem, 0

    def mark(self, ins):
        ins.then_inc(self.sem, 1)
        self.n += 1
        return self.n

    def wait(self, n=None):
        self.eng.wait_ge(self.sem, self.n if n is None else n)


def gated_layers(nc, a, out):
    B, S, D = a["x"].shape
    C = a["ctx_1024"].shape[1]
    HD = 8
    H = D // HD
    T = B * S
    P = 128
    NT = T // P
    TB = S // P
    L = a["L0_ffn_Wdown"].shape[1]
    E0 = a["L0_ffn_We"].shape[0]
    E1, _, EH = a["L1_ffn_Wup"].shape
    G = 64
    NG = T // G
    BUDGET = NG * 16
    NC = E1 * EH // P
    EC = P // EH
    CH = P // C
    HC = H // CH
    HC9 = HD + 1
    SC = float(HD) ** -0.5
    HALF = T // 2
    GH = HALF // G
    assert P == D and B == 2 and HALF == S == 512 and 2 * E1 == P and H * C == 512

    with ExitStack() as ctx:
        def sb(name, shape, dt=F32):
            return ctx.enter_context(nc.sbuf_tensor(name, shape, dt))

        def bank(name):
            return ctx.enter_context(nc.psum_tensor(name, [P, 512], F32))

        def sem(name):
            return ctx.enter_context(nc.semaphore(name))

        x = sb("x_tok", [P, NT, D])
        ctx_in = sb("ctx_in", [B * C, D])
        w_in = [sb(f"w_in{l}", [P, 4, D]) for l in (0, 1)]
        bcol = sb("bcol", [P, 4])
        gcol = sb("gcol", [P, 4])
        tg = sb("tg", [P, 4])
        brow = sb("brow", [P, 8 * D + E0 + E1])
        maskt = sb("maskt", [P, NT, C], U8)
        fq_in = sb("fq_in", [P, D])
        fdown_in = sb("fdown_in", [P, L])
        fup_in = sb("fup_in", [L, 2 * D])
        bup_row = sb("bup_row", [1, 2 * D])
        bdown_col = sb("bdown_col", [L, 1])
        gam = sb("gam", [P, 2])
        fo = sb("fo", [P, D])
        wg = sb("wg", [P, E0])
        we = sb("we", [P, E0, D])
        wr = sb("wr", [P, E1])
        wup = sb("wup", [P, E1, EH])
        wgate = sb("wgate", [P, E1, EH])
        wdn = sb("wdn", [P, NC, D])
        bdn = sb("bdn", [P, 2, D])
        bug_in = sb("bug_in", [2 * NC, P])
        bug = sb("bug", [P, 2, NC])

        ident = sb("ident", [P, P])
        row0 = sb("row0", [P, P])
        headmask = sb("headmask", [P, H])
        jmask = sb("jmask", [P, CH])
        eps = sb("eps", [P, 3])
        neg = sb("neg", [P, 1])
        ones = sb("ones", [P, 512])
        swap = sb("swap", [P, P])
        samehalf = sb("samehalf", [P, P])
        low2high = sb("low2high", [P, P])
        upto = sb("upto", [P, P])
        high = sb("high", [P, 1])
        sel = sb("sel", [P, 2, NC, P])

        hg = sb("hg", [P, NC, T])
        early = hg[:, :, :].rearrange("p c t -> p (c t)")
        taken = [0]

        def shared(*dims):
            n = 1
            for d in dims:
                n *= d
            part = early[:, taken[0]:taken[0] + n]
            taken[0] += n
            assert taken[0] <= NC * T
            names = "abc"[:len(dims)]
            return part.rearrange(f"p ({' '.join(names)}) -> p {' '.join(names)}", **dict(zip(names, dims)))

        ctxT = sb("ctxT", [P, B * C])
        ctx4 = sb("ctx4", [P, B, CH, C])
        wT = [sb(f"wT{l}", [P, 4, D]) for l in (0, 1)]
        kT = [sb(f"kT{l}", [P, B * C]) for l in (0, 1)]
        kblk = [shared(B, H, C) for _ in (0, 1)]
        vblk = [sb(f"vblk{l}", [P, B, HC, CH, HC9]) for l in (0, 1)]
        wdT = sb("wdT", [L, D])
        wqkv = sb("wqkv", [P, 3 * D])
        bqs = sb("bqs", [P, 2])

        st6 = sb("st6", [P, TB, 6])
        mv = sb("mv", [P, 4 * NT, 2])
        lnv = sb("lnv", [P, 4 * NT])
        rstd = sb("rstd", [P, 4 * NT])
        lnu = sb("lnu", [P, NT])
        ustd = sb("ustd", [P, NT])
        y = sb("y", [P, 2, D])
        yB = shared(NT, D)
        yT = sb("yT", [P, 2, P])
        yTD = sb("yTD", [P, T])
        qT = sb("qT", [P, 2, P])
        mx = sb("mx", [P, 2, H])
        e = shared(2, 512)
        eT = shared(2, 512)
        den = sb("den", [P, 2, H])
        rec = sb("rec", [P, 2, H])
        o = sb("o", [P, 2, D])
        oT = sb("oT", [P, 2, D])
        qkv = shared(4, 3 * D)
        prod = shared(2, H * H * HD)
        prov = shared(2, H * H * HD)
        sB = sb("sB", [P, 2, H * H])
        eB = sb("eB", [P, 2, H * H])
        oraw = sb("oraw", [P, D])
        xp = sb("xp", [P, 3, D])
        sq = sb("sq", [P, D])
        ssq = sb("ssq", [P, NT])
        lns = sb("lns", [P, NT])
        rms = sb("rms", [P, NT])
        h2 = sb("h2", [P, D])
        h2T = sb("h2T", [P, 2, P])
        gmx = sb("gmx", [P, NT])
        gex = sb("gex", [P, 2, E0])
        gsum = sb("gsum", [P, NT])
        grec = sb("grec", [P, NT])
        gate = sb("gate", [P, 2, E0])
        acc = sb("acc", [P, 2, 2, D])
        rmx = sb("rmx", [P, NT])
        rex = sb("rex", [P, 2, E1])
        rsum = sb("rsum", [P, NT])
        rrec = sb("rrec", [P, NT])
        rsc = sb("rsc", [P, TB, 2, E1])
        rT = sb("rT", [P, HALF])
        sort = [sb(f"sort{i}", [P, HALF]) for i in (0, 1)]
        other = sb("other", [P, HALF])
        gs = sb("gs", [P, GH])
        gmin = sb("gmin", [P, GH])
        diag = sb("diag", [P, GH, P])
        allgs = sb("allgs", [P, 2 * HALF])
        junk = sb("junk", [P, 2, 2 * HALF])
        small = sb("small", [P, 16, GH])
        lmax = sb("lmax", [1, 4])
        st2 = sb("st2", [P, 8])
        gt = sb("gt", [P, HALF])
        eq = sb("eq", [P, HALF])
        fs = sb("fs", [P, HALF])
        silu = sb("silu", [P, 4, HALF])
        fT = sb("fT", [P, T])
        res = allgs[:, :].rearrange("p (t d) -> p t d", t=NT)

        pTA, pTB, pS0, pS1, pE0, pE1, pO, pW = [bank(n) for n in ("pTA", "pTB", "pS0", "pS1", "pE0", "pE1", "pO", "pW")]
        pS, pE = (pS0, pS1), (pE0, pE1)

        ld_x = sem("ld_x")
        ld_ctx = sem("ld_ctx")
        ld_w = [sem("ld_w0"), sem("ld_w1")]
        ld_small = sem("ld_small")
        ld_rows = sem("ld_rows")
        ld_mask = sem("ld_mask")
        ld_ffn0 = sem("ld_ffn0")
        ld_ffn1 = sem("ld_ffn1")
        ld_up = sem("ld_up")
        ld_bug = sem("ld_bug")
        stored = sem("stored")
        rows_zero = sem("rows_zero")
        eps_set = sem("eps_set")
        bdn_zero = sem("bdn_zero")
        consts = sem("consts")
        consts_sel = sem("consts_sel")
        pool_steps = sem("pool_steps")
        vec_steps = sem("vec_steps")
        act_steps = sem("act_steps")
        setup_ps = sem("setup_ps")
        setup_act = sem("setup_act")
        setup_vec = sem("setup_vec")
        kblk_done = sem("kblk_done")
        scaled0 = sem("scaled0")
        stats = sem("stats")
        rstd_done = sem("rstd_done")
        y_done = sem("y_done")
        yT_ps = sem("yT_ps")
        yT_done = sem("yT_done")
        q_ps = sem("q_ps")
        q_done = sem("q_done")
        proj_ps = sem("proj_ps")
        e_shift = sem("e_shift")
        e_done = sem("e_done")
        eT_ps = sem("eT_ps")
        eT_done = sem("eT_done")
        o_ps = sem("o_ps")
        o_done = sem("o_done")
        oT_ps = sem("oT_ps")
        oT_done = sem("oT_done")
        w_ps = sem("w_ps")
        w_read = sem("w_read")
        qkv_done = sem("qkv_done")
        mulqk = sem("mulqk")
        redqk = sem("redqk")
        sB_done = sem("sB_done")
        eB_done = sem("eB_done")
        sumB = sem("sumB")
        mulav = sem("mulav")
        redav = sem("redav")
        rms_done = sem("rms_done")
        h2_done = sem("h2_done")
        h2T_ps = sem("h2T_ps")
        h2T_done = sem("h2T_done")
        gl_ps = sem("gl_ps")
        gmx_done = sem("gmx_done")
        gex_done = sem("gex_done")
        moe_ps = sem("moe_ps")
        moe_read = sem("moe_read")
        rmx_done = sem("rmx_done")
        rex_done = sem("rex_done")
        rsc_done = sem("rsc_done")
        rT_ps = sem("rT_ps")
        rT_done = sem("rT_done")
        up_ps = sem("up_ps")
        gate_ps = sem("gate_ps")
        silu_done = sem("silu_done")
        hg_done = sem("hg_done")
        pick_vec = sem("pick_vec")
        pick_ps = sem("pick_ps")
        allgs_done = sem("allgs_done")
        fs_done = sem("fs_done")
        bc_ps = sem("bc_ps")
        h_done = sem("h_done")
        down_ps = sem("down_ps")
        fT_done = sem("fT_done")
        res_ps = sem("res_ps")
        res_done = sem("res_done")

        BO0, BOF, BO1, BV0, BV1, BQKV = (i * D for i in range(6))
        BG = BQKV + 3 * D
        BR = BG + E0

        SCHEDULE = []
        for stage, last in (("A", NT + 1), ("B", NT + 2), ("C", NT + 1), ("D", NT)):
            new = [(stage, i) for i in range(-2, last + 1)]
            if SCHEDULE:
                new = [SCHEDULE[-2], new[0], SCHEDULE[-1], *new[1:]]
                SCHEDULE = SCHEDULE[:-2]
            SCHEDULE += new

        UNITS = [(c, b) for c in range(NC) for b in range(2)]

        SORT = []
        k = 2
        while k <= HALF:
            SORT.append((k, None))
            j = k // 4
            while j >= 1:
                SORT.append((k, j))
                j //= 2
            k *= 2
        MERGE = [(HALF, HALF // 2), (HALF, HALF // 4), (HALF, HALF // 8)]
        assert MERGE[-1][1] == G

        block = ctx.enter_context(nc.Block())

        @block.sync
        def _(sp):
            xr = a["x"].rearrange("b (t p) d -> p (b t) d", p=P)
            sp.dma_start(ctx_in[:, :], a["ctx_1024"].rearrange("b s d -> (b s) d")).then_inc(ld_ctx, 16)
            for l, pre in enumerate(("L0_xattn_", "L1_xattn_")):
                for i, w in enumerate(("Wq", "Wk", "Wv", "Wo")):
                    sp.dma_start(w_in[l][:, i, :], a[pre + w]).then_inc(ld_w[l], 16)
                if l == 0:
                    sp.dma_start(x[:, 0:TB, :], xr[:, 0:TB, :]).then_inc(ld_x, 16)
                    sp.dma_start(x[:, TB:NT, :], xr[:, TB:NT, :]).then_inc(ld_x, 16)
            for i, w in enumerate(("bup", "bgate")):
                sp.dma_start(bug_in[i * NC:(i + 1) * NC, :], a["L1_ffn_" + w].rearrange("(c j) h -> c (j h)", j=EC)).then_inc(ld_bug, 16)
            sp.dma_start(fdown_in[:, :], a["L0_ffn_Wdown"]).then_inc(ld_ffn0, 16)
            sp.dma_start(fup_in[:, :], a["L0_ffn_Wup"]).then_inc(ld_ffn0, 16)
            sp.dma_start(fq_in[:, :], a["L0_ffn_Wq"]).then_inc(ld_ffn0, 16)
            sp.dma_start(fo[:, :], a["L0_ffn_Wo"]).then_inc(ld_ffn0, 16)
            sp.dma_start(wg[:, :], a["L0_ffn_Wg"]).then_inc(ld_ffn0, 16)
            sp.dma_start(bup_row[:, :], a["L0_ffn_bup"].rearrange("(a n) -> a n", a=1)).then_inc(ld_ffn0, 16)
            sp.dma_start(bdown_col[:, :], a["L0_ffn_bdown"].rearrange("(n a) -> n a", a=1)).then_inc(ld_ffn0, 16)
            sp.dma_start(we[:, :, :], a["L0_ffn_We"].rearrange("e d f -> d e f")).then_inc(ld_ffn0, 16)
            mr = a["mask_Bx1xSxS2_bk1"].rearrange("b o (t p) c -> p (b o t) c", p=P)
            sp.dma_start(maskt[:, :, :], mr).then_inc(ld_mask, 16)
            sp.dma_start(wr[:, :], a["L1_ffn_Wr"]).then_inc(ld_ffn1, 16)
            sp.dma_start(wup[:, :, :], a["L1_ffn_Wup"].rearrange("e d h -> d e h")).then_inc(ld_up, 16)
            sp.dma_start(wgate[:, :, :], a["L1_ffn_Wgate"].rearrange("e d h -> d e h")).then_inc(ld_up, 16)
            sp.dma_start(wdn[:, :, :], a["L1_ffn_Wdown"].rearrange("(c j) h d -> (j h) c d", j=EC)).then_inc(ld_up, 16)
            for b in range(2):
                sp.dma_start(bdn[b * E1:(b + 1) * E1, b, :], a["L1_ffn_bdown"]).then_inc(ld_up, 16)
            orr = out.rearrange("b (t p) d -> p (b t) d", p=P)
            for b in range(2):
                sp.wait_ge(res_done, b + 1)
                sp.dma_start(orr[:, b * TB:(b + 1) * TB, :], res[:, b * TB:(b + 1) * TB, :]).then_inc(stored, 16)
            sp.wait_ge(stored, 32)

        @block.gpsimd
        def _(pool):
            steps = Steps(pool, pool_steps)

            for i in range(2):
                pool.dma_start(gcol[:, 2 * i:2 * i + 2],
                               a[("g_xattn", "g_ffn")[i]].partition_broadcast(P)).then_inc(ld_small, 16)
            for l in range(2):
                for i, w in enumerate(("bq", "bk")):
                    pool.dma_start(bcol[:, 2 * l + i:2 * l + i + 1],
                                   a[f"L{l}_xattn_{w}"].rearrange("(n a) -> n a", a=1)).then_inc(ld_small, 16)
            for i in range(2):
                pool.dma_start(gam[:, i:i + 1],
                               a[f"L0_ffn_gamma{i + 1}"].rearrange("(n a) -> n a", a=1)).then_inc(ld_small, 16)

            def mask_from(tile, value, *selects):
                steps.mark(nc.gpsimd.memset(tile, value))
                for op, fill, base, pattern, mult in selects:
                    steps.wait()
                    steps.mark(nc.gpsimd.affine_select(out=tile, in_=tile, compare_op=op, fill=fill, base=base,
                                                       pattern=pattern, channel_multiplier=mult))

            mask_from(ident[:, :], 0.0, (ALU.not_equal, 1.0, 0, [[-1, P]], 1))
            mask_from(headmask[:, :], 1.0, (ALU.is_ge, 0.0, 0, [[-HD, H]], 1),
                      (ALU.is_ge, 0.0, HD - 1, [[HD, H]], -1))
            mask_from(jmask[:, :], 1.0, (ALU.is_ge, 0.0, 0, [[-C, CH]], 1),
                      (ALU.is_ge, 0.0, C - 1, [[C, CH]], -1))
            mask_from(row0[:, :], 0.0, (ALU.not_equal, 1.0, 0, [[0, P]], 1))
            steps.wait()
            nc.gpsimd.memset(neg[:, :], -1e9).then_inc(consts, 1)

            for l in range(2):
                pool.wait_ge(setup_act, (6, 7)[l])
                for b in range(B):
                    nc.gpsimd.tensor_tensor(
                        kblk[l][:, b, :, :],
                        kT[l][:, b * C:(b + 1) * C].unsqueeze(1).to_broadcast([P, H, C]),
                        headmask[:, :].unsqueeze(2).to_broadcast([P, H, C]), ALU.mult).then_inc(kblk_done, 1)

            pool.wait_ge(ld_small, 16 * 8)
            pool.wait_ge(ld_ffn0, 16 * 8)
            nc.gpsimd.tensor_scalar(wqkv[:, 0:D], fq_in[:, :], gam[:, 0:1], None, ALU.mult).then_inc(scaled0, 1)
            nc.gpsimd.tensor_scalar(wg[:, :], wg[:, :], gam[:, 1:2], None, ALU.mult).then_inc(scaled0, 1)
            nc.gpsimd.tensor_scalar(we[:, :, :].rearrange("p e f -> p (e f)"), we[:, :, :].rearrange("p e f -> p (e f)"),
                                    gam[:, 1:2], None, ALU.mult).then_inc(scaled0, 1)

            mask_from(swap[:, :], 0.0, (ALU.not_equal, 1.0, E1, [[-1, P]], 1), (ALU.not_equal, 1.0, -E1, [[-1, P]], 1))
            v = samehalf[:, :].rearrange("p (b e) -> p b e", b=2)
            mask_from(v, 1.0, (ALU.is_ge, 0.0, 0, [[-E1, 2], [0, E1]], 1),
                      (ALU.is_ge, 0.0, E1 - 1, [[E1, 2], [0, E1]], -1))
            steps.wait()
            v = low2high[:, :].rearrange("p (b e) -> p b e", b=2)
            mask_from(v, 1.0, (ALU.is_ge, 0.0, E1 - 1, [[0, 2], [0, E1]], -1),
                      (ALU.is_ge, 0.0, -1, [[1, 2], [0, E1]], 0))
            mask_from(upto[:, :], 1.0, (ALU.is_ge, 0.0, 0, [[1, P]], -1))
            steps.wait()
            steps.mark(nc.gpsimd.tensor_tensor(upto[:, :], upto[:, :], samehalf[:, :], ALU.mult))
            mask_from(high[:, :], 1.0, (ALU.is_ge, 0.0, -E1, [[0, 1]], 1))
            for b in range(2):
                v = sel[:, b, :, :].rearrange("p c (j h) -> p c j h", j=EC)
                mask_from(v, 0.0, (ALU.not_equal, 1.0, -b * E1, [[-EC, NC], [-1, EC], [0, EH]], 1))
            steps.wait()
            nc.gpsimd.memset(ones[:, :], 1.0).then_inc(consts_sel, 1)

            def mul_qk(t):
                pool.wait_ge(qkv_done, t + 1)
                at_least(pool, redqk, t - 1)
                q = qkv[:, t % 4, 0:D].rearrange("p (h d) -> p h d", h=H)
                k = qkv[:, t % 4, D:2 * D].rearrange("p (h d) -> p h d", h=H)
                nc.gpsimd.tensor_tensor(prod[:, t % 2, :].rearrange("p (h g d) -> p h g d", h=H, g=H),
                                        q.unsqueeze(2).to_broadcast([P, H, H, HD]),
                                        k.unsqueeze(1).to_broadcast([P, H, H, HD]), ALU.mult).then_inc(mulqk, 1)

            def mul_av(t):
                pool.wait_ge(eB_done, t + 1)
                at_least(pool, redav, t - 1)
                w = eB[:, t % 2, :].rearrange("p (h g) -> p h g", h=H)
                v = qkv[:, t % 4, 2 * D:3 * D].rearrange("p (d g) -> p d g", d=HD)
                nc.gpsimd.tensor_tensor(prov[:, t % 2, :].rearrange("p (h d g) -> p h d g", h=H, d=HD),
                                        w.unsqueeze(2).to_broadcast([P, H, HD, H]),
                                        v.unsqueeze(1).to_broadcast([P, H, HD, H]), ALU.mult).then_inc(mulav, 1)

            for t in range(NT + 1):
                if t < NT:
                    mul_qk(t)
                if t >= 1:
                    mul_av(t - 1)

        @block.scalar
        def _(act):
            steps = Steps(act, act_steps)

            act.wait_ge(rows_zero, 1)
            for name, at, n in (("L0_xattn_bo", BO0, D), ("L0_ffn_bo", BOF, D), ("L1_xattn_bo", BO1, D),
                                ("L0_xattn_bv", BV0, D), ("L1_xattn_bv", BV1, D), ("L0_ffn_bg", BG, E0), ("L1_ffn_br", BR, E1),
                                ("L0_ffn_bq", BQKV, D)):
                act.dma_start(brow[0:1, at:at + n], a[name].rearrange("(a n) -> a n", a=1)).then_inc(ld_rows, 16)

            act.wait_ge(setup_ps, 1)
            nc.scalar.activation(ctxT[:, :], pO[:, 0:B * C], ACT.Copy).then_inc(setup_act, 1)
            for b in range(B):
                steps.mark(nc.scalar.activation(ctx4[:, b, :, :],
                                     pO[:, b * C:(b + 1) * C].unsqueeze(1).to_broadcast([P, CH, C]), ACT.Copy))
            steps.wait()
            act.wait_ge(ld_small, 16 * 8)
            nc.scalar.activation(tg[:, :], gcol[:, :], ACT.Tanh).then_inc(setup_act, 1)
            for l in range(2):
                act.wait_ge(setup_ps, 2 + l)
                nc.scalar.activation(wT[l][:, :, :].rearrange("p i n -> p (i n)"), pE[l][:, :], ACT.Copy).then_inc(setup_act, 1)
            act.wait_ge(setup_ps, 4)
            nc.scalar.activation(wdT[:, :], pW[0:L, 0:D], ACT.Copy).then_inc(setup_act, 1)
            for l in range(2):
                act.wait_ge(setup_ps, 5 + l)
                nc.scalar.activation(kT[l][:, :], (pTA, pTB)[l][:, 0:B * C], ACT.Identity,
                                     bias=bcol[:, 2 * l + 1:2 * l + 2]).then_inc(setup_act, 1)
            steps.mark(nc.scalar.activation(bug[:, :, :].rearrange("p i c -> p (i c)"), pTA[:, 128:128 + 2 * NC], ACT.Copy))
            steps.mark(nc.scalar.mul(bqs[:, 0:1], bcol[:, 0:1], SC))
            steps.mark(nc.scalar.mul(bqs[:, 1:2], bcol[:, 2:3], SC))
            act.wait_ge(setup_ps, 8)
            kv = pO[:, 0:2 * D].rearrange("p (g k d) -> p k g d", g=H, k=2)
            nc.scalar.activation(wqkv[:, D:2 * D].rearrange("p (g d) -> p g d", g=H), kv[:, 0], ACT.Copy,
                                 scale=gam[:, 0:1]).then_inc(setup_act, 1)
            nc.scalar.activation(wqkv[:, 2 * D:3 * D].rearrange("p (d g) -> p g d", g=H), kv[:, 1], ACT.Copy,
                                 scale=gam[:, 0:1]).then_inc(setup_act, 1)
            steps.wait()
            act.wait_ge(eps_set, 3)

            def rstd_of(n):
                act.wait_ge(stats, n + 1)
                k = steps.mark(nc.scalar.activation(lnv[:, n:n + 1], mv[:, n, 1:2], ACT.Ln, bias=eps[:, 0:1]))
                if NT <= n < 2 * NT:
                    t = n - NT
                    k2 = steps.mark(nc.scalar.activation(lnu[:, t:t + 1], mv[:, n, 1:2], ACT.Ln,
                                                         bias=eps[:, 1:2], scale=1.0 + 1e-6))
                    steps.wait(k)
                    steps.mark(nc.scalar.activation(rstd[:, n:n + 1], lnv[:, n:n + 1], ACT.Exp, scale=-0.5))
                    steps.wait(k2)
                    nc.scalar.activation(ustd[:, t:t + 1], lnu[:, t:t + 1], ACT.Exp, scale=-0.5).then_inc(rstd_done, 1)
                    steps.wait()
                else:
                    steps.wait(k)
                    nc.scalar.activation(rstd[:, n:n + 1], lnv[:, n:n + 1], ACT.Exp, scale=-0.5).then_inc(rstd_done, 1)

            def copy_yT(n):
                act.wait_ge(yT_ps, n + 1)
                if n < 3 * NT:
                    if n >= 2:
                        m = n - 2
                        st = m // NT
                        if st == 1:
                            act.wait_ge(proj_ps, m + 1)
                        else:
                            act.wait_ge(q_ps, m + 1 if st == 0 else m + 1 - NT)
                    dst = yT[:, n % 2, :]
                else:
                    dst = yTD[:, (n - 3 * NT) * P:(n - 3 * NT + 1) * P]
                nc.scalar.activation(dst, pTA[:, 0:P], ACT.Copy).then_inc(yT_done, 1)

            def copy_oT(n):
                act.wait_ge(oT_ps, n + 1)
                at_least(act, w_ps, n - 1)
                nc.scalar.activation(oT[:, n % 2, :], pTB[:, 0:P], ACT.Copy).then_inc(oT_done, 1)

            def attention(l, i):
                base = 2 * l * NT
                ka = l * NT
                if 0 <= i + 1 < NT:
                    n = base + i + 1
                    copy_yT(n)
                    k = ka + i + 1
                    act.wait_ge(q_ps, k + 1)
                    at_least(act, proj_ps, n - 1)
                    nc.scalar.activation(qT[:, k % 2, :], pTA[:, 256:256 + P], ACT.Identity,
                                         bias=bqs[:, l:l + 1], scale=SC).then_inc(q_done, 1)
                if 0 <= i < NT:
                    k = ka + i
                    act.wait_ge(e_shift, k + 1)
                    nc.scalar.activation(e[:, k % 2, :], e[:, k % 2, :], ACT.Exp).then_inc(e_done, 1)
                if 0 <= i - 1 < NT:
                    copy_oT(l * 2 * NT + i - 1)
                if 0 <= i < NT:
                    k = ka + i
                    act.wait_ge(eT_ps, k + 1)
                    at_least(act, o_ps, k - 1)
                    nc.scalar.activation(eT[:, k % 2, :], pE[k % 2][:, :], ACT.Copy).then_inc(eT_done, 1)
                if 0 <= i - 2 < NT:
                    rstd_of(base + NT + i - 2)

            def heads(i):
                if 0 <= i - 2 < NT:
                    t = i - 2
                    act.wait_ge(h2T_ps, t + 1)
                    at_least(act, moe_ps, t - 1)
                    nc.scalar.activation(h2T[:, t % 2, :], pO[:, 0:P], ACT.Copy).then_inc(h2T_done, 1)
                if 0 <= i < NT:
                    act.wait_ge(sB_done, i + 1)
                    at_least(act, mulav, i - 1)
                    at_least(act, sumB, i - 1)
                    nc.scalar.activation(eB[:, i % 2, :], sB[:, i % 2, :], ACT.Exp, scale=SC).then_inc(eB_done, 1)
                if 0 <= i - 3 < NT:
                    rstd_of(2 * NT + i - 3)
                if 0 <= i - 1 < NT:
                    copy_oT(NT + i - 1)
                if 0 <= i - 2 < NT:
                    t = i - 2
                    act.wait_ge(gmx_done, t + 1)
                    at_least(act, moe_read, t - 1)
                    nc.scalar.activation(gex[:, t % 2, :], pW[:, 256:256 + E0], ACT.Exp, bias=gmx[:, t:t + 1],
                                         accum_out=gsum[:, t:t + 1]).then_inc(gex_done, 1)
                if 0 <= i + 2 < NT:
                    t = i + 2
                    copy_yT(NT + t)
                    act.wait_ge(proj_ps, NT + t + 1)
                    at_least(act, mulav, t - 3)
                    nc.scalar.activation(qkv[:, t % 4, :], pS[t % 2][:, 0:3 * D], ACT.Copy).then_inc(qkv_done, 1)
                if 0 <= i - 1 < NT:
                    t = i - 1
                    act.wait_ge(w_read, NT + t + 1)
                    k = steps.mark(nc.scalar.activation(sq[:, :], xp[:, t % 3, :], ACT.Square, accum_out=ssq[:, t:t + 1]))
                    steps.wait(k)
                    k = steps.mark(nc.scalar.activation(lns[:, t:t + 1], ssq[:, t:t + 1], ACT.Ln, bias=eps[:, 2:3], scale=1.0 / D))
                    steps.wait(k)
                    nc.scalar.activation(rms[:, t:t + 1], lns[:, t:t + 1], ACT.Exp, scale=-0.5).then_inc(rms_done, 1)

            def router(i):
                if 0 <= i + 1 < NT:
                    copy_yT(3 * NT + i + 1)
                if 0 <= i < NT:
                    act.wait_ge(rmx_done, i + 1)
                    at_least(act, rsc_done, i - 1)
                    nc.scalar.activation(rex[:, i % 2, :], pS[i % 2][:, 0:E1], ACT.Exp, bias=rmx[:, i:i + 1],
                                         accum_out=rsum[:, i:i + 1]).then_inc(rex_done, 1)

            for stage, i in SCHEDULE:
                if stage == "A" and i in (-2, 0):
                    for n in range(TB):
                        rstd_of(n + (0, TB)[i == 0])
                {"A": lambda i: attention(0, i), "B": heads, "C": lambda i: attention(1, i), "D": router}[stage](i)

            act.wait_ge(rT_ps, 1)
            nc.scalar.activation(rT[:, :], pTB[:, :], ACT.Copy).then_inc(rT_done, 1)
            for u, (c, b) in enumerate(UNITS):
                act.wait_ge(up_ps, u + 1)
                at_least(act, hg_done, u - 3)
                nc.scalar.activation(silu[:, u % 4, :], pS[b][:, :], ACT.Silu, bias=bug[:, 0, c:c + 1]).then_inc(silu_done, 1)
            act.wait_ge(pick_ps, 1)
            for b in range(2):
                nc.scalar.activation(allgs[:, b * HALF:(b + 1) * HALF], (pTA, pTB)[b][:, :], ACT.Copy).then_inc(allgs_done, 1)
            for b in range(2):
                act.wait_ge(down_ps, b + 1)
                nc.scalar.activation(fT[:, b * HALF:(b + 1) * HALF], pE[b][:, :], ACT.Copy,
                                     scale=tg[:, 3:4]).then_inc(fT_done, 1)

        @block.tensor
        def _(pe):
            mm = nc.tensor.matmul

            def bias(dst, row, last):
                m = mm(dst, row0[:, :], row, start=False, stop=True)
                return m

            pe.wait_ge(consts, 1)
            pe.wait_ge(ld_ctx, 16)
            nc.tensor.transpose(pO[:, 0:B * C], ctx_in[:, :], ident[0:B * C, 0:B * C]).then_inc(setup_ps, 1)
            for l in range(2):
                pe.wait_ge(ld_w[l], 64)
                for i in range(4):
                    m = nc.tensor.transpose(pE[l][:, i * D:(i + 1) * D], w_in[l][:, i, :], ident[:, :])
                m.then_inc(setup_ps, 1)
            pe.wait_ge(ld_ffn0, 16 * 8)
            nc.tensor.transpose(pW[0:L, 0:D], fdown_in[:, :], ident[:, :]).then_inc(setup_ps, 1)
            pe.wait_ge(setup_act, 4)
            pe.wait_ge(act_steps, 2)
            pe.wait_ge(ld_bug, 32)
            nc.tensor.transpose(pTA[:, 128:128 + 2 * NC], bug_in[:, :], ident[0:2 * NC, 0:2 * NC])
            for l in range(2):
                mm((pTA, pTB)[l][:, 0:B * C], wT[l][:, 1, :], ctxT[:, :]).then_inc(setup_ps, 1)
            pe.wait_ge(ld_rows, 16 * 8)
            for l in range(2):
                for b in range(B):
                    dst = (pS, pE)[l][b][:, 0:D]
                    mm(dst, ctx4[:, b, :, :].rearrange("p j k -> p (j k)"), wT[l][:, 2, :], start=True, stop=False)
                    m = bias(dst, brow[:, (BV0, BV1)[l]:(BV0, BV1)[l] + D], True)
                if l == 1:
                    m.then_inc(setup_ps, 1)
            pe.wait_ge(setup_act, 5)
            mm(pO[:, 0:2 * D], wdT[:, :], fup_in[:, :]).then_inc(setup_ps, 1)
            mm(pW[0:1, 0:2 * D], bdown_col[:, :], fup_in[:, :]).then_inc(setup_ps, 1)
            pe.wait_ge(setup_act, 9)
            pe.wait_ge(setup_vec, 5)
            pe.wait_ge(act_steps, 5)

            def queries_before(n):
                return min(n, NT) + min(max(n - 2 * NT, 0), NT)

            def transpose_y(n):
                pe.wait_ge(y_done, n + 1)
                at_least(pe, yT_done, n)
                at_least(pe, q_done, queries_before(n))
                nc.tensor.transpose(pTA[:, 0:P], y[:, n % 2, :], ident[:, :]).then_inc(yT_ps, 1)

            def transpose_o(n):
                pe.wait_ge(o_done, n + 1)
                at_least(pe, oT_done, n)
                nc.tensor.transpose(pTB[:, 0:P], o[:, n % 2, :], ident[:, :]).then_inc(oT_ps, 1)

            def project_o(n, w, bo):
                pe.wait_ge(oT_done, n + 1)
                at_least(pe, w_read, n)
                if NT < n < 2 * NT:
                    pe.wait_ge(gex_done, n - NT)
                elif n >= 2 * NT:
                    pe.wait_ge(gex_done, NT)
                mm(pW[:, 0:D], oT[:, n % 2, :], w, start=True, stop=False)
                bias(pW[:, 0:D], bo, True).then_inc(w_ps, 1)

            def scores_bank_free(n):
                m = n - 2
                if m < 0:
                    return
                st, t = divmod(m, NT)
                if st == 0:
                    pe.wait_ge(e_shift, t + 1)
                elif st == 1:
                    pe.wait_ge(qkv_done, t + 1)
                elif st == 2:
                    pe.wait_ge(e_shift, NT + t + 1)
                else:
                    pe.wait_ge(rex_done, t + 1)

            def attention(l, i):
                base = 2 * l * NT
                ka = l * NT
                if 0 <= i + 1 < NT:
                    n, k, b = base + i + 1, ka + i + 1, (i + 1) // TB
                    transpose_y(n)
                    pe.wait_ge(yT_done, n + 1)
                    mm(pTA[:, 256:256 + P], wT[l][:, 0, :], yT[:, n % 2, :]).then_inc(q_ps, 1)
                    pe.wait_ge(q_done, k + 1)
                    scores_bank_free(n)
                    pe.wait_ge(kblk_done, 2 * l + b + 1)
                    mm(pS[n % 2][:, :], qT[:, k % 2, :],
                       kblk[l][:, b, :, :].rearrange("p h k -> p (h k)")).then_inc(proj_ps, 1)
                if 0 <= i - 1 < NT:
                    transpose_o(base + i - 1)
                if 0 <= i < NT:
                    n, k, b = base + i, ka + i, i // TB
                    pe.wait_ge(e_done, k + 1)
                    at_least(pe, eT_done, k - 1)
                    if l == 1 and i < 2:
                        pe.wait_ge(moe_read, NT)
                    for c in range(HC):
                        m = nc.tensor.transpose(pE[k % 2][:, c * P:(c + 1) * P], e[:, k % 2, c * P:(c + 1) * P], ident[:, :])
                    m.then_inc(eT_ps, 1)
                    pe.wait_ge(eT_done, k + 1)
                    at_least(pe, o_done, n)
                    for c in range(HC):
                        w9 = CH * HC9
                        m = mm(pO[:, c * w9:(c + 1) * w9], eT[:, k % 2, c * P:(c + 1) * P],
                               vblk[l][:, b, c, :, :].rearrange("p j d -> p (j d)"))
                    m.then_inc(o_ps, 1)
                if 0 <= i - 1 < NT:
                    project_o(base + i - 1, wT[l][:, 3, :], brow[:, (BO0, BO1)[l]:(BO0, BO1)[l] + D])

            def heads(i):
                if 0 <= i - 2 < NT:
                    t = i - 2
                    pe.wait_ge(h2_done, t + 1)
                    at_least(pe, h2T_done, t)
                    if t == 0:
                        pe.wait_ge(o_done, NT)
                    nc.tensor.transpose(pO[:, 0:P], h2[:, :], ident[:, :]).then_inc(h2T_ps, 1)
                    pe.wait_ge(h2T_done, t + 1)
                    mm(pW[:, 256:256 + E0], h2T[:, t % 2, :], wg[:, :], start=True, stop=False)
                    bias(pW[:, 256:256 + E0], brow[:, BG:BG + E0], True).then_inc(gl_ps, 1)
                    at_least(pe, moe_read, t)
                    for j in range(2):
                        m = mm(pE[j][:, :], h2T[:, t % 2, :],
                               we[:, j * E0 // 2:(j + 1) * E0 // 2, :].rearrange("p e f -> p (e f)"))
                    m.then_inc(moe_ps, 1)
                if 0 <= i - 1 < NT:
                    transpose_o(NT + i - 1)
                if 0 <= i + 2 < NT:
                    n = NT + i + 2
                    transpose_y(n)
                if 0 <= i - 1 < NT:
                    project_o(NT + i - 1, fo[:, :], brow[:, BOF:BOF + D])
                if 0 <= i + 2 < NT:
                    pe.wait_ge(yT_done, n + 1)
                    scores_bank_free(n)
                    mm(pS[n % 2][:, 0:3 * D], yT[:, n % 2, :], wqkv[:, :], start=True, stop=False)
                    bias(pS[n % 2][:, 0:3 * D], brow[:, BQKV:BQKV + 3 * D], True).then_inc(proj_ps, 1)

            def router(i):
                if 0 <= i + 1 < NT:
                    n = 3 * NT + i + 1
                    transpose_y(n)
                    pe.wait_ge(yT_done, n + 1)
                    scores_bank_free(n)
                    mm(pS[n % 2][:, 0:E1], yTD[:, (i + 1) * P:(i + 2) * P], wr[:, :], start=True, stop=False)
                    bias(pS[n % 2][:, 0:E1], brow[:, BR:BR + E1], True).then_inc(proj_ps, 1)

            pe.wait_ge(scaled0, 3)
            pe.wait_ge(ld_ffn1, 16)
            for stage, i in SCHEDULE:
                {"A": lambda i: attention(0, i), "B": heads, "C": lambda i: attention(1, i), "D": router}[stage](i)

            pe.wait_ge(rsc_done, NT)
            for j in range(TB):
                m = nc.tensor.transpose(pTB[:, j * P:(j + 1) * P], rsc[:, j, :, :].rearrange("p b e -> p (b e)"), ident[:, :])
            m.then_inc(rT_ps, 1)
            pe.wait_ge(ld_up, 16 * 5)
            pe.wait_ge(rex_done, NT)
            pe.wait_ge(w_read, 3 * NT)
            for u, (c, b) in enumerate(UNITS):
                cols = yTD[:, b * HALF:(b + 1) * HALF]
                at_least(pe, silu_done, u - 1)
                mm(pS[b][:, :], wup[:, c * EC:(c + 1) * EC, :].rearrange("p j h -> p (j h)"), cols).then_inc(up_ps, 1)
                at_least(pe, hg_done, u - 1)
                mm(pE[b][:, :], wgate[:, c * EC:(c + 1) * EC, :].rearrange("p j h -> p (j h)"), cols).then_inc(gate_ps, 1)
            pe.wait_ge(pick_vec, 1)
            pe.wait_ge(consts_sel, 1)
            pe.wait_ge(rT_done, 1)
            dg = diag[:, :, :].rearrange("p c q -> p (c q)")
            for b in range(2):
                m = mm((pTA, pTB)[b][:, :], ones[:, 0:P], dg[:, b * HALF:(b + 1) * HALF])
            m.then_inc(pick_ps, 1)
            pe.wait_ge(pick_vec, 2)
            nc.tensor.transpose(pO[0:1, 0:P], st2[:, 0:1], ident[:, :]).then_inc(pick_ps, 1)
            pe.wait_ge(pick_vec, 3)
            mm(pO[:, 256:257], ones[0:1, 0:P], lmax[0:1, 0:1]).then_inc(pick_ps, 1)
            pe.wait_ge(pick_vec, 4)
            mm(pW[:, 0:GH], upto[:, :], small[:, 2, :], start=True, stop=False)
            mm(pW[:, 0:GH], samehalf[:, :], small[:, 4, :], start=False, stop=False)
            mm(pW[:, 0:GH], low2high[:, :], small[:, 5, :], start=False, stop=True).then_inc(pick_ps, 1)
            pe.wait_ge(pick_vec, 5)
            mm(pO[:, 0:2], swap[:, :], st2[:, 2:4]).then_inc(pick_ps, 1)
            pe.wait_ge(pick_vec, 6)
            mm(pW[:, 0:2], swap[:, :], st2[:, 4:6]).then_inc(pick_ps, 1)
            pe.wait_ge(pick_vec, 7)
            mm(pO[:, :], samehalf[:, :], fs[:, :]).then_inc(pick_ps, 1)
            pe.wait_ge(fs_done, 1)
            pe.wait_ge(silu_done, len(UNITS))
            pe.wait_ge(hg_done, len(UNITS))
            pe.wait_ge(bdn_zero, 2)
            BC = (pS0, pS1, pTA, pTB)

            def spread(u):
                c, b = UNITS[u]
                if u < 4:
                    pe.wait_ge(allgs_done, 2)
                at_least(pe, h_done, u - 3)
                mm(BC[u % 4][:, :], sel[:, b, c, :], fs[:, :]).then_inc(bc_ps, 1)

            for u in range(2):
                spread(u)
            for u, (c, b) in enumerate(UNITS):
                if u + 2 < len(UNITS):
                    spread(u + 2)
                pe.wait_ge(h_done, u + 1)
                mm(pE[b][:, :], wdn[:, c, :], hg[:, c, b * HALF:(b + 1) * HALF], start=c == 0, stop=False)
                if c == NC - 1:
                    mm(pE[b][:, :], bdn[:, b, :], fs[:, :], start=False, stop=True).then_inc(down_ps, 1)
            pe.wait_ge(h_done, len(UNITS))
            for b in range(2):
                pe.wait_ge(fT_done, b + 1)
                for j in range(TB):
                    m = nc.tensor.transpose((pTA, pTB)[b][:, j * P:(j + 1) * P],
                                            fT[:, b * HALF + j * P:b * HALF + (j + 1) * P], ident[:, :])
                m.then_inc(res_ps, 1)

        @block.vector
        def _(dve):
            v = nc.vector
            steps = Steps(dve, vec_steps)
            v.memset(brow[:, :], 0.0).then_inc(rows_zero, 1)
            for k, val in enumerate((1e-5, 1e-11, 1e-6)):
                v.memset(eps[:, k:k + 1], val).then_inc(eps_set, 1)
            v.memset(bdn[E1:P, 0, :], 0.0).then_inc(bdn_zero, 1)
            v.memset(bdn[0:E1, 1, :], 0.0).then_inc(bdn_zero, 1)

            dve.wait_ge(consts, 1)
            dve.wait_ge(setup_ps, 7)
            for l in range(2):
                for b in range(B):
                    vv = (pS, pE)[l][b][:, 0:D].rearrange("p (c j d) -> p c j d", c=HC, j=CH)
                    for c in range(HC):
                        steps.mark(v.tensor_tensor(vblk[l][:, b, c, :, 0:HD], vv[:, c],
                                        jmask[:, :].unsqueeze(2).to_broadcast([P, CH, HD]), ALU.mult))
                    steps.wait()
                    v.tensor_copy(vblk[l][:, b, :, :, HD],
                                  jmask[:, :].unsqueeze(1).to_broadcast([P, HC, CH])).then_inc(setup_vec, 1)
            steps.wait()
            dve.wait_ge(setup_ps, 9)
            dve.wait_ge(ld_ffn0, 16 * 8)
            kvp = pW[0:1, 0:2 * D].rearrange("p (g k d) -> p k g d", g=H, k=2)
            kvb = bup_row[:, :].rearrange("p (g k d) -> p k g d", g=H, k=2)
            steps.mark(v.tensor_tensor(brow[0:1, BQKV + D:BQKV + 2 * D].rearrange("p (g d) -> p g d", g=H),
                                       kvp[:, 0], kvb[:, 0], ALU.add))
            v.tensor_tensor(brow[0:1, BQKV + 2 * D:BQKV + 3 * D].rearrange("p (d g) -> p g d", g=H),
                            kvp[:, 1], kvb[:, 1], ALU.add).then_inc(setup_vec, 1)

            def statistics(*tiles):
                for n in tiles:
                    at_least(dve, stats, n - TB + 1)
                    steps.mark(v.bn_stats(st6[:, n % TB, :], x[:, n % NT, :]))
                for k, n in enumerate(tiles):
                    steps.wait(steps.n - len(tiles) + 1 + k)
                    v.bn_aggr(mv[:, n, :], st6[:, n % TB, :]).then_inc(stats, 1)

            def normalise(n):
                t = n % NT
                dve.wait_ge(rstd_done, n + 1)
                at_least(dve, yT_ps, n - 1)
                if NT <= n < 2 * NT:
                    steps.mark(v.tensor_scalar(yB[:, t, :], x[:, t, :], mv[:, n, 0:1], rstd[:, n:n + 1],
                                               ALU.subtract, ALU.mult))
                    scale = ustd[:, t:t + 1]
                else:
                    scale = rstd[:, n:n + 1]
                v.tensor_scalar(y[:, n % 2, :], x[:, t, :], mv[:, n, 0:1], scale,
                                ALU.subtract, ALU.mult).then_inc(y_done, 1)

            def attention(l, i):
                base = 2 * l * NT
                ka = l * NT
                if 0 <= i < NT:
                    n, k = base + i, ka + i
                    s3 = pS[n % 2][:, :].rearrange("p (h k) -> p h k", h=H)
                    dve.wait_ge(proj_ps, n + 1)
                    if l == 1:
                        if i == 0:
                            dve.wait_ge(ld_mask, 16)
                        steps.mark(v.copy_predicated(s3, maskt[:, i, :].unsqueeze(1).to_broadcast([P, H, C]),
                                                     neg[:, :].unsqueeze(2).to_broadcast([P, H, C])))
                        steps.wait()
                    steps.mark(v.tensor_reduce(mx[:, k % 2, :], s3, AX.X, ALU.max))
                    steps.wait()
                    at_least(dve, eT_ps, k - 1)
                    v.tensor_tensor(e[:, k % 2, :].rearrange("p (h k) -> p h k", h=H), s3,
                                    mx[:, k % 2, :].unsqueeze(2).to_broadcast([P, H, C]),
                                    ALU.subtract).then_inc(e_shift, 1)
                if 0 <= i + 2 < NT:
                    normalise(base + i + 2)
                if 0 <= i - 1 < NT:
                    n, k = base + i - 1, ka + i - 1
                    o9 = pO[:, 0:H * HC9].rearrange("p (h d) -> p h d", h=H)
                    dve.wait_ge(o_ps, k + 1)
                    if l == 0:
                        steps.mark(v.tensor_scalar(den[:, k % 2, :], o9[:, :, HD], 1e-10, None, ALU.add))
                        steps.wait()
                        steps.mark(v.reciprocal(rec[:, k % 2, :], den[:, k % 2, :]))
                    else:
                        steps.mark(v.reciprocal(rec[:, k % 2, :], o9[:, :, HD]))
                    steps.wait()
                    at_least(dve, oT_ps, n - 1)
                    v.tensor_tensor(o[:, n % 2, :].rearrange("p (h d) -> p h d", h=H), o9[:, :, 0:HD],
                                    rec[:, k % 2, :].unsqueeze(2).to_broadcast([P, H, HD]),
                                    ALU.mult).then_inc(o_done, 1)
                if 0 <= i - 2 < NT:
                    t = i - 2
                    n = base + t
                    dve.wait_ge(w_ps, n + 1)
                    v.scalar_tensor_tensor(out=x[:, t, :], in0=pW[:, 0:D], scalar=tg[:, l:l + 1], in1=x[:, t, :],
                                           op0=ALU.mult, op1=ALU.add).then_inc(w_read, 1)
                    dve.wait_ge(w_read, n + 1)
                    statistics(n + NT)

            def heads(i):
                if 0 <= i < NT:
                    dve.wait_ge(mulqk, i + 1)
                    v.tensor_reduce(sB[:, i % 2, :], prod[:, i % 2, :].rearrange("p (s d) -> p s d", d=HD),
                                    AX.X, ALU.add).then_inc(redqk, 1)
                if 0 <= i - 2 < NT:
                    t = i - 2
                    dve.wait_ge(rms_done, t + 1)
                    at_least(dve, h2T_ps, t)
                    v.tensor_scalar(h2[:, :], xp[:, t % 3, :], rms[:, t:t + 1], None, ALU.mult).then_inc(h2_done, 1)
                if 0 <= i < NT:
                    s3 = sB[:, i % 2, :].rearrange("p (h g) -> p h g", h=H)
                    dve.wait_ge(redqk, i + 1)
                    steps.mark(v.tensor_reduce(mx[:, i % 2, :], s3, AX.X, ALU.max))
                    steps.wait()
                    v.tensor_tensor(s3, s3, mx[:, i % 2, :].unsqueeze(2).to_broadcast([P, H, H]),
                                    ALU.subtract).then_inc(sB_done, 1)
                if 0 <= i - 3 < NT:
                    t = i - 3
                    dve.wait_ge(gex_done, t + 1)
                    steps.mark(v.reciprocal(grec[:, t:t + 1], gsum[:, t:t + 1]))
                    steps.wait()
                    steps.mark(v.tensor_scalar(gate[:, t % 2, :], gex[:, t % 2, :], grec[:, t:t + 1], None, ALU.mult))
                    steps.wait()
                    dve.wait_ge(moe_ps, t + 1)
                    for k in range(E0 // 2):
                        for j in range(2):
                            ex = j * (E0 // 2) + k
                            src = pE[j][:, k * D:(k + 1) * D]
                            g = gate[:, t % 2, ex:ex + 1]
                            dst = acc[:, j, k % 2, :]
                            if k >= 1:
                                steps.wait(steps.n - 1)
                            if k == 0 and j == 1:
                                ins = v.tensor_scalar(dst, src, g, None, ALU.mult)
                            else:
                                add = xp[:, t % 3, :] if k == 0 else acc[:, j, (k - 1) % 2, :]
                                ins = v.scalar_tensor_tensor(out=dst, in0=src, scalar=g, in1=add, op0=ALU.mult, op1=ALU.add)
                            steps.mark(ins)
                    steps.wait()
                    last = (E0 // 2 - 1) % 2
                    v.tensor_tensor(acc[:, 0, 1 - last, :], acc[:, 0, last, :], acc[:, 1, last, :], ALU.add).then_inc(moe_read, 1)
                    dve.wait_ge(moe_read, t + 1)
                    steps.mark(v.scalar_tensor_tensor(out=x[:, t, :], in0=acc[:, 0, 1 - last, :], scalar=tg[:, 2:3],
                                                      in1=x[:, t, :], op0=ALU.mult, op1=ALU.add))
                    steps.wait()
                    statistics(2 * NT + t)
                if 0 <= i - 1 < NT:
                    t = i - 1
                    n = NT + t
                    dve.wait_ge(mulav, t + 1)
                    v.tensor_reduce(oraw[:, :], prov[:, t % 2, :].rearrange("p (s g) -> p s g", g=H),
                                    AX.X, ALU.add).then_inc(redav, 1)
                    dve.wait_ge(redav, t + 1)
                    dve.wait_ge(sumB, t + 1)
                    steps.mark(v.reciprocal(rec[:, t % 2, :], den[:, t % 2, :]))
                    steps.wait()
                    at_least(dve, oT_ps, n - 1)
                    v.tensor_tensor(o[:, n % 2, :].rearrange("p (h d) -> p h d", h=H),
                                    oraw[:, :].rearrange("p (h d) -> p h d", h=H),
                                    rec[:, t % 2, :].unsqueeze(2).to_broadcast([P, H, HD]),
                                    ALU.mult).then_inc(o_done, 1)
                if 0 <= i - 2 < NT:
                    t = i - 2
                    dve.wait_ge(gl_ps, t + 1)
                    v.tensor_reduce(gmx[:, t:t + 1], pW[:, 256:256 + E0], AX.X, ALU.max, negate=True).then_inc(gmx_done, 1)
                if 0 <= i + 2 < NT:
                    normalise(NT + i + 2)
                if 0 <= i < NT:
                    dve.wait_ge(eB_done, i + 1)
                    v.tensor_reduce(den[:, i % 2, :], eB[:, i % 2, :].rearrange("p (h g) -> p h g", h=H),
                                    AX.X, ALU.add).then_inc(sumB, 1)
                if 0 <= i - 1 < NT:
                    t = i - 1
                    n = NT + t
                    dve.wait_ge(w_ps, n + 1)
                    v.tensor_tensor(xp[:, t % 3, :], pW[:, 0:D], yB[:, t, :], ALU.add).then_inc(w_read, 1)

            def router(i):
                if 0 <= i < NT:
                    dve.wait_ge(proj_ps, 3 * NT + i + 1)
                    v.tensor_reduce(rmx[:, i:i + 1], pS[i % 2][:, 0:E1], AX.X, ALU.max, negate=True).then_inc(rmx_done, 1)
                if 0 <= i + 2 < NT:
                    normalise(3 * NT + i + 2)
                if 0 <= i - 1 < NT:
                    t = i - 1
                    dve.wait_ge(rex_done, t + 1)
                    steps.mark(v.reciprocal(rrec[:, t:t + 1], rsum[:, t:t + 1]))
                    steps.wait()
                    v.tensor_scalar(rsc[:, t % TB, t // TB, :], rex[:, t % 2, :], rrec[:, t:t + 1], None,
                                    ALU.mult).then_inc(rsc_done, 1)

            dve.wait_ge(ld_x, 16)
            dve.wait_ge(setup_act, 2)
            statistics(*range(TB))
            for stage, i in SCHEDULE:
                if stage == "A" and i == 0:
                    dve.wait_ge(ld_x, 32)
                    statistics(*range(TB, NT))
                {"A": lambda i: attention(0, i), "B": heads, "C": lambda i: attention(1, i), "D": router}[stage](i)

            hg_next = [0]

            def hidden(upto_unit):
                while hg_next[0] < min(upto_unit, len(UNITS)):
                    u = hg_next[0]
                    c, b = UNITS[u]
                    dve.wait_ge(gate_ps, u + 1)
                    dve.wait_ge(silu_done, u + 1)
                    v.scalar_tensor_tensor(out=hg[:, c, b * HALF:(b + 1) * HALF], in0=pE[b][:, :],
                                           scalar=bug[:, 1, c:c + 1], in1=silu[:, u % 4, :],
                                           op0=ALU.add, op1=ALU.mult).then_inc(hg_done, 1)
                    hg_next[0] += 1

            dve.wait_ge(rT_done, 1)
            dve.wait_ge(ld_up, 16 * 5)
            src = rT

            def exchange(src, dst, k, j):
                if j is None:
                    s = src[:, :].rearrange("p (b k) -> p b k", k=k)
                    d = dst[:, :].rearrange("p (b k) -> p b k", k=k)
                    lo, hi = s[:, :, 0:k // 2], s[:, :, k // 2:k]
                    lo_back = s[:, :, k // 2 - 1::-1]
                    hi_back = s[:, :, k - 1:k // 2 - 1:-1]
                    dlo, dhi = d[:, :, 0:k // 2], d[:, :, k // 2:k]
                else:
                    s = src[:, :].rearrange("p (b two j) -> p b two j", two=2, j=j)
                    d = dst[:, :].rearrange("p (b two j) -> p b two j", two=2, j=j)
                    lo, hi = s[:, :, 0, :], s[:, :, 1, :]
                    lo_back, hi_back = lo, hi
                    dlo, dhi = d[:, :, 0, :], d[:, :, 1, :]
                steps.mark(v.tensor_tensor(dlo, lo, hi_back, ALU.max))
                steps.mark(v.tensor_tensor(dhi, hi, lo_back, ALU.min))

            stage_no = 0
            total = len(SORT) + len(MERGE) + 1
            for k, j in SORT:
                exchange(src, sort[stage_no % 2], k, j)
                src = sort[stage_no % 2]
                stage_no += 1
                hidden(stage_no * len(UNITS) // total)
                steps.wait()
            lo, hi = slice(0, E1), slice(E1, P)
            dst = sort[stage_no % 2]
            steps.mark(v.tensor_copy(other[lo, :], src[hi, :]))
            steps.mark(v.tensor_copy(other[hi, :], src[lo, :]))
            steps.wait()
            steps.mark(v.tensor_tensor(dst[lo, :], src[lo, :], other[lo, ::-1], ALU.max))
            steps.mark(v.tensor_tensor(dst[hi, :], src[hi, :], other[hi, ::-1], ALU.min))
            src = dst
            stage_no += 1
            steps.wait()
            for k, j in MERGE:
                exchange(src, sort[stage_no % 2], k, j)
                src = sort[stage_no % 2]
                stage_no += 1
                hidden(stage_no * len(UNITS) // total)
                steps.wait()
            groups = src[:, :].rearrange("p (c g) -> p c g", g=G)
            steps.mark(v.tensor_reduce(gs[:, :], groups, AX.X, ALU.add))
            steps.mark(v.tensor_reduce(gmin[:, :], groups, AX.X, ALU.min))
            steps.wait(steps.n - 1)
            dve.wait_ge(consts_sel, 1)
            v.tensor_tensor(diag[:, :, :], gs[:, :].unsqueeze(2).to_broadcast([P, GH, P]),
                            ident[:, :].unsqueeze(1).to_broadcast([P, GH, P]), ALU.mult).then_inc(pick_vec, 1)
            hidden(len(UNITS))

            count, cand, tie, incl, excl, incl_all, key, pick, big, gsel = (small[:, k, :] for k in range(10))
            dve.wait_ge(allgs_done, 2)
            for c in range(GH):
                if c >= 2:
                    steps.wait(steps.n - 1)
                steps.mark(v.tensor_scalar(junk[:, c % 2, :], allgs[:, :], gs[:, c:c + 1], None, ALU.is_gt, ALU.add,
                                           accum_out=count[:, c:c + 1]))
            steps.wait()
            steps.mark(v.scalar_tensor_tensor(out=cand, in0=count, scalar=float(BUDGET), in1=count,
                                              op0=ALU.is_lt, op1=ALU.mult))
            steps.wait()
            v.tensor_reduce(st2[:, 0:1], cand, AX.X, ALU.max).then_inc(pick_vec, 1)
            dve.wait_ge(pick_ps, 2)
            v.tensor_reduce(lmax[0:1, 0:1], pO[0:1, 0:P], AX.X, ALU.max).then_inc(pick_vec, 1)
            dve.wait_ge(pick_ps, 3)
            steps.mark(v.tensor_scalar(tie, count, pO[:, 256:257], None, ALU.is_equal))
            steps.wait()
            steps.mark(v.tensor_tensor_scan(incl, ones[:, 0:GH], tie, 0.0, ALU.mult, ALU.add))
            steps.wait()
            steps.mark(v.tensor_tensor(excl, incl, tie, ALU.subtract))
            steps.wait()
            v.tensor_copy(incl_all, incl[:, GH - 1:GH].to_broadcast([P, GH])).then_inc(pick_vec, 1)
            dve.wait_ge(pick_ps, 4)
            steps.mark(v.scalar_tensor_tensor(out=key, in0=pW[:, 0:GH], scalar=-1.0, in1=tie, op0=ALU.add, op1=ALU.mult))
            steps.wait()
            steps.mark(v.tensor_tensor(key, key, count, ALU.add))
            steps.wait()
            steps.mark(v.tensor_scalar(pick, key, float(BUDGET), None, ALU.is_lt, ALU.add, accum_out=st2[:, 3:4]))
            steps.wait()
            steps.mark(v.tensor_scalar(big, pick, -2.0, 2.0, ALU.mult, ALU.add))
            steps.wait()
            steps.mark(v.tensor_tensor(gsel, big, gmin[:, :], ALU.max))
            steps.wait()
            v.tensor_reduce(st2[:, 2:3], gsel, AX.X, ALU.min).then_inc(pick_vec, 1)
            dve.wait_ge(pick_ps, 5)
            thr, room, need = st2[:, 6:7], st2[:, 7:8], st2[:, 1:2]
            steps.mark(v.tensor_tensor(thr, pO[:, 0:1], st2[:, 2:3], ALU.min))
            steps.mark(v.tensor_scalar(room, pO[:, 1:2], st2[:, 3:4], float(G), ALU.add, ALU.mult))
            steps.wait()

            steps.mark(v.tensor_scalar(eq[:, :], rT[:, :], thr, None, ALU.is_equal, ALU.add, accum_out=st2[:, 5:6]))
            v.tensor_scalar(gt[:, :], rT[:, :], thr, None, ALU.is_gt, ALU.add, accum_out=st2[:, 4:5]).then_inc(pick_vec, 1)
            dve.wait_ge(pick_vec, 6)
            steps.wait()
            steps.mark(v.tensor_tensor_scan(junk[:, 0, 0:HALF], ones[:, 0:HALF], eq[:, :], 0.0, ALU.mult, ALU.add))
            dve.wait_ge(pick_ps, 6)
            steps.mark(v.tensor_scalar(need, pW[:, 0:1], st2[:, 4:5], -1.0, ALU.add, ALU.mult))
            steps.wait()
            steps.mark(v.tensor_tensor(need, need, room, ALU.add))
            steps.wait()
            steps.mark(v.tensor_tensor(room, pW[:, 1:2], high[:, :], ALU.mult))
            steps.wait()
            steps.mark(v.tensor_tensor(need, need, room, ALU.subtract))
            steps.wait()
            steps.mark(v.scalar_tensor_tensor(out=eq[:, :], in0=junk[:, 0, 0:HALF], scalar=need, in1=eq[:, :],
                                              op0=ALU.is_le, op1=ALU.mult))
            steps.wait()
            steps.mark(v.tensor_tensor(gt[:, :], gt[:, :], eq[:, :], ALU.add))
            steps.wait()
            v.tensor_tensor(fs[:, :], gt[:, :], rT[:, :], ALU.mult).then_inc(pick_vec, 1)
            dve.wait_ge(pick_ps, 7)
            steps.mark(v.tensor_scalar(gt[:, :], pO[:, :], 1e-6, None, ALU.add))
            steps.wait()
            steps.mark(v.reciprocal(eq[:, :], gt[:, :]))
            steps.wait()
            v.tensor_tensor(fs[:, :], fs[:, :], eq[:, :], ALU.mult).then_inc(fs_done, 1)

            BC = (pS0, pS1, pTA, pTB)
            for u, (c, b) in enumerate(UNITS):
                dve.wait_ge(bc_ps, u + 1)
                part = hg[:, c, b * HALF:(b + 1) * HALF]
                v.tensor_tensor(part, BC[u % 4][:, :], part, ALU.mult).then_inc(h_done, 1)
            for b in range(2):
                dve.wait_ge(res_ps, b + 1)
                tiles = slice(b * TB, (b + 1) * TB)
                v.tensor_tensor(res[:, tiles, :], (pTA, pTB)[b][:, :].rearrange("p (t d) -> p t d", t=TB),
                                x[:, tiles, :], ALU.add).then_inc(res_done, 1)


def kernel(**inputs):
    import numpy as _np
    import concourse.bacc as _bacc
    from concourse import mybir as _mybir
    from concourse.bass_utils import run_bass_kernel_spmd as _run

    nc = _bacc.Bacc("TRN2", target_bir_lowering=False, num_devices=1)
    arrays, args = {}, {}
    for name, value in inputs.items():
        arr = _np.ascontiguousarray(value)
        arrays[f"in_{name}"] = arr
        args[name] = nc.dram_tensor(f"in_{name}", arr.shape, _mybir.dt.from_np(arr.dtype), kind="ExternalInput").ap()
    out = nc.dram_tensor("out_0", inputs["x"].shape, _mybir.dt.float32, kind="ExternalOutput").ap()
    gated_layers(nc, args, out)
    r = _run(nc, [arrays], core_ids=[0])
    return r.results[0]["out_0"]
```

```python
from contextlib import ExitStack

import concourse.bass as bass
from concourse import mybir

ALU = mybir.AluOpType
ACT = mybir.ActivationFunctionType
AX = mybir.AxisListType
F32 = mybir.dt.float32
F32R = mybir.dt.float32r
U8 = mybir.dt.uint8


def at_least(eng, sem, value):
    if value > 0:
        eng.wait_ge(sem, value)


class Steps:

    def __init__(self, eng, sem):
        self.eng, self.sem, self.n = eng, sem, 0

    def mark(self, ins):
        ins.then_inc(self.sem, 1)
        self.n += 1
        return self.n

    def wait(self, n=None):
        self.eng.wait_ge(self.sem, self.n if n is None else n)


def gated_layers(nc, a, out):
    B, S, D = a["x"].shape
    C = a["ctx_1024"].shape[1]
    HD = 8
    H = D // HD
    T = B * S
    P = 128
    NT = T // P
    TB = S // P
    L = a["L0_ffn_Wdown"].shape[1]
    E0 = a["L0_ffn_We"].shape[0]
    E1, _, EH = a["L1_ffn_Wup"].shape
    G = 64
    NG = T // G
    BUDGET = NG * 16
    NC = E1 * EH // P
    EC = P // EH
    CH = P // C
    HC = H // CH
    HC9 = HD + 1
    SC = float(HD) ** -0.5
    HALF = T // 2
    GH = HALF // G
    assert P == D and B == 2 and HALF == S == 512 and 2 * E1 == P and H * C == 512

    with ExitStack() as ctx:
        def sb(name, shape, dt=F32):
            return ctx.enter_context(nc.sbuf_tensor(name, shape, dt))

        def bank(name):
            return ctx.enter_context(nc.psum_tensor(name, [P, 512], F32))

        def sem(name):
            return ctx.enter_context(nc.semaphore(name))

        x = sb("x_tok", [P, NT, D])
        ctx_in = sb("ctx_in", [B * C, D])
        bcol = sb("bcol", [P, 4])
        gcol = sb("gcol", [P, 4])
        tg = sb("tg", [P, 4])
        brow = sb("brow", [P, 8 * D + E0 + E1])
        maskt = sb("maskt", [P, NT, C], U8)
        fq_in = sb("fq_in", [P, D])
        fdown_in = sb("fdown_in", [P, L])
        fup_in = sb("fup_in", [L, 2 * D])
        bup_row = sb("bup_row", [1, 2 * D])
        bdown_col = sb("bdown_col", [L, 1])
        gam = sb("gam", [P, 2])
        fo = sb("fo", [P, D])
        wg = sb("wg", [P, E0])
        we = sb("we", [P, E0, D])
        wr = sb("wr", [P, E1])
        wup = sb("wup", [P, E1, EH])
        wgate = sb("wgate", [P, E1, EH])
        wdn = sb("wdn", [P, NC, D])
        bdn = sb("bdn", [P, 2, D])
        bug_in = sb("bug_in", [2 * NC, P])
        bug = sb("bug", [P, 2, NC])

        ident = sb("ident", [P, P])
        row0 = sb("row0", [P, P])
        headmask = sb("headmask", [P, H])
        jmask = sb("jmask", [P, CH])
        eps = sb("eps", [P, 3])
        neg = sb("neg", [P, 1])
        ones = sb("ones", [P, 512])
        swap = sb("swap", [P, P])
        samehalf = sb("samehalf", [P, P])
        low2high = sb("low2high", [P, P])
        upto = sb("upto", [P, P])
        high = sb("high", [P, 1])
        sel = sb("sel", [P, 2, NC, P], F32R)
        halfcol = sb("halfcol", [P, 2])
        sel_mark = sb("sel_mark", [P, 2])

        def before(name, shape, dt=F32):
            with nc.sbuf_tensor(name, shape, dt) as tensor:
                return tensor

        products = before("products", [P, 2, 2, H * H * HD])
        ws = before("ws", [P, NC, 2, 2, P], F32R)
        hg_high = sb("hg_high", [P, NC // 2, T])
        assert 2 * 2 * H * H * HD == NC * 2 * 2 * P == NC // 2 * T
        hg_low = sb("hg_low", [P, NC // 2, T])
        early = hg_low[:, :, :].rearrange("p c t -> p (c t)")

        def hidden_values(c, b):
            return (hg_low, hg_high)[c // (NC // 2)][:, c % (NC // 2), b * HALF:(b + 1) * HALF]

        taken = [0]

        def shared(*dims):
            n = 1
            for d in dims:
                n *= d
            part = early[:, taken[0]:taken[0] + n]
            taken[0] += n
            assert taken[0] <= NC // 2 * T
            names = "abc"[:len(dims)]
            return part.rearrange(f"p ({' '.join(names)}) -> p {' '.join(names)}", **dict(zip(names, dims)))

        ctxT = sb("ctxT", [P, B * C])
        ctx4 = sb("ctx4", [P, B, CH, C])
        wT = [sb(f"wT{l}", [P, 4, D]) for l in (0, 1)]
        kT = [sb(f"kT{l}", [P, B * C]) for l in (0, 1)]
        w_in = [shared(4, D) for _ in (0, 1)]
        kblk = [shared(B, H, C) for _ in (0, 1)]
        vblk = [sb(f"vblk{l}", [P, B, HC, CH, HC9]) for l in (0, 1)]
        wdT = sb("wdT", [L, D])
        wqkv = sb("wqkv", [P, 3 * D])
        bqs = sb("bqs", [P, 2])

        st6 = sb("st6", [P, TB, 6])
        mv = sb("mv", [P, 4 * NT, 2])
        lnv = sb("lnv", [P, 4 * NT])
        rstd = sb("rstd", [P, 4 * NT])
        lnu = sb("lnu", [P, NT])
        ustd = sb("ustd", [P, NT])
        negm, nmr, nmu = [sb(n, [P, NT]) for n in ("negm", "nmr", "nmu")]
        y = sb("y", [P, 2, D])
        yB = shared(NT, D)
        yT = sb("yT", [P, 2, P])
        yTD = sb("yTD", [P, T])
        qT = sb("qT", [P, 2, P])
        mx = sb("mx", [P, 2, H])
        e = shared(2, 512)
        eT = shared(2, 512)
        den = sb("den", [P, 2, H])
        rec = sb("rec", [P, 2, H])
        o = sb("o", [P, 2, D])
        oT = sb("oT", [P, 2, D])
        qkv = shared(4, 3 * D)
        prod, prov = products[:, 0], products[:, 1]
        sB = sb("sB", [P, 2, H * H])
        eB = sb("eB", [P, 2, H * H])
        oraw = sb("oraw", [P, D])
        xp = sb("xp", [P, 2, D])
        sq = sb("sq", [P, D])
        ssq = sb("ssq", [P, NT])
        lns = sb("lns", [P, NT])
        rms = sb("rms", [P, NT])
        h2 = sb("h2", [P, 2, D])
        h2T = sb("h2T", [P, P])
        gmx = sb("gmx", [P, NT])
        gex = sb("gex", [P, 2, E0])
        gsum = sb("gsum", [P, NT])
        grec = sb("grec", [P, NT])
        rmx = sb("rmx", [P, NT])
        rex = sb("rex", [P, 2, E1])
        rsum = sb("rsum", [P, NT])
        rrec = sb("rrec", [P, NT])
        rsc = sb("rsc", [P, TB, 2, E1])
        rT = sb("rT", [P, HALF])
        sort = [sb(f"sort{i}", [P, HALF]) for i in (0, 1)]
        gs = sb("gs", [P, GH])
        gmin = sb("gmin", [P, GH])
        xh = before("xh", [P, T], F32R)
        allgs = sb("allgs", [P, 2 * HALF])
        xl = before("xl", [P, T], F32R)
        junk = sb("junk", [P, 2, 2 * HALF], mybir.dt.bfloat16)
        small = sb("small", [P, 16, GH])
        lmax = sb("lmax", [1, 4])
        st2 = sb("st2", [P, 8])
        gt = sb("gt", [P, HALF])
        other = gt
        cum = sb("cum", [P, HALF])
        eq = sb("eq", [P, HALF])
        fs = sb("fs", [P, HALF])
        silu = sb("silu", [P, 4, HALF])
        sel_f32 = silu[:, :, :].rearrange("p a t -> p (a t)")
        gsb = sb("gsb", [P, 3, HALF])
        fsr = sb("fsr", [P, 2, HALF], F32R)
        hgate = allgs[:, :].rearrange("p (e d) -> p e d", e=E0)
        hgateT = gsb[:, 0:2, :].rearrange("p a t -> p (a t)")
        rden = sb("rden", [P, 2, TB])
        scale3 = sb("scale3", [P, 2, TB])
        fT = sb("fT", [P, T])
        diag = fT[:, :].rearrange("p (c q) -> p c q", c=GH)
        res = allgs[:, :].rearrange("p (t d) -> p t d", t=NT)

        pTA, pTB, pS0, pS1, pE0, pE1, pO, pW = [bank(n) for n in ("pTA", "pTB", "pS0", "pS1", "pE0", "pE1", "pO", "pW")]
        pS, pE = (pS0, pS1), (pE0, pE1)
        BC = (pS0, pS1, pTA, pTB)

        ld_x = [sem("ld_x0"), sem("ld_x1")]
        ld_ctx = sem("ld_ctx")
        ld_w = [[sem(f"ld_w{l}k"), sem(f"ld_w{l}qvo")] for l in (0, 1)]
        ld_gate = sem("ld_gate")
        ld_b = [sem("ld_b0"), sem("ld_b1")]
        ld_rows = [sem(f"ld_rows{k}") for k in range(3)]
        ld_mask = sem("ld_mask")
        ld_ffn0 = sem("ld_ffn0")
        ld_ffn1 = sem("ld_ffn1")
        ld_up = sem("ld_up")
        ld_bug = sem("ld_bug")
        stored = sem("stored")
        rows_zero = sem("rows_zero")
        eps_set = sem("eps_set")
        bdn_zero = sem("bdn_zero")
        consts = sem("consts")
        sel_made = sem("sel_made")
        sel_done = sem("sel_done")
        pool_steps = sem("pool_steps")
        vec_steps = sem("vec_steps")
        act_steps = sem("act_steps")
        setup_ps = sem("setup_ps")
        tg_done = sem("tg_done")
        wT_done = sem("wT_done")
        kT_done = [sem(f"kT_done{l}") for l in (0, 1)]
        ctx_done = sem("ctx_done")
        wk_done = sem("wk_done")
        part_ps = sem("part_ps")
        part_read = sem("part_read")
        wkv_done = sem("wkv_done")
        vblk_done = sem("vblk_done")
        den_ps = sem("den_ps")
        kblk_done = sem("kblk_done")
        scaled0 = sem("scaled0")
        stats = sem("stats")
        rstd_done = sem("rstd_done")
        y_done = sem("y_done")
        yT_ps = sem("yT_ps")
        yT_done = sem("yT_done")
        q_ps = sem("q_ps")
        q_done = sem("q_done")
        proj_ps = sem("proj_ps")
        e_shift = sem("e_shift")
        e_done = sem("e_done")
        eT_ps = sem("eT_ps")
        eT_done = sem("eT_done")
        o_ps = sem("o_ps")
        o_done = sem("o_done")
        oT_ps = sem("oT_ps")
        oT_done = sem("oT_done")
        w_ps = sem("w_ps")
        w_read = sem("w_read")
        qkv_done = sem("qkv_done")
        mulqk = sem("mulqk")
        redqk = sem("redqk")
        sB_done = sem("sB_done")
        eB_done = sem("eB_done")
        sumB = sem("sumB")
        mulav = sem("mulav")
        mulav_vec = sem("mulav_vec")
        yC_done = sem("yC_done")
        yB_ready = sem("yB_ready")
        yB_done = sem("yB_done")
        xp_done = sem("xp_done")
        w_high = sem("w_high")
        w_low = sem("w_low")
        x_high = sem("x_high")
        x_low = sem("x_low")
        recB = sem("recB")
        hgate_done = sem("hgate_done")
        hgT_ps = sem("hgT_ps")
        hgT_done = sem("hgT_done")
        redav = sem("redav")
        h2_done = sem("h2_done")
        h2T_ps = sem("h2T_ps")
        h2T_done = sem("h2T_done")
        gl_ps = sem("gl_ps")
        gmx_done = sem("gmx_done")
        gex_done = sem("gex_done")
        moe_ps = sem("moe_ps")
        moe_read = sem("moe_read")
        rmx_done = sem("rmx_done")
        rex_done = sem("rex_done")
        rsc_done = sem("rsc_done")
        rT_ps = sem("rT_ps")
        rT_done = sem("rT_done")
        up_ps = sem("up_ps")
        gate_ps = sem("gate_ps")
        silu_done = sem("silu_done")
        gsb_done = sem("gsb_done")
        hg_pool = sem("hg_pool")
        hg_dve = sem("hg_dve")
        pick_vec = sem("pick_vec")
        pick_ps = sem("pick_ps")
        allgs_done = sem("allgs_done")
        fs_done = sem("fs_done")
        bc_ps = sem("bc_ps")
        h_done = sem("h_done")
        down_ps = sem("down_ps")
        fT_done = sem("fT_done")
        res_ps = sem("res_ps")
        res_done = sem("res_done")

        BO0, BOF, BO1, BV0, BV1, BQKV = (i * D for i in range(6))
        BG = BQKV + 3 * D
        BR = BG + E0

        SCHEDULE = []
        for stage, first, last, beside in (("A", -4, NT + 1, 0), ("B", -4, NT + 2, 6), ("C", -4, NT + 1, 6), ("D", -3, NT, 6)):
            new = [(stage, i) for i in range(first, last + 1)]
            pairs = 4 if stage == "C" else beside
            old, SCHEDULE = SCHEDULE[len(SCHEDULE) - beside:], SCHEDULE[:len(SCHEDULE) - beside]
            SCHEDULE += [step for pair in zip(old, new[:pairs]) for step in pair] + old[pairs:] + new[pairs:]
        PIECES = 8

        def piece(k):
            which, first, n = k // (PIECES // 2), k % (PIECES // 2) * (2 * NC // PIECES), 2 * NC // PIECES
            src = (wup, wgate)[which][:, first * EC:(first + n) * EC, :].rearrange("p (c j) h -> p c (j h)", c=n)
            return src, ws[:, first:first + n, which, 0, :], ws[:, first:first + n, which, 1, :]

        PARTS = 6

        def ahead(l, t):
            return l == 1 and 0 <= t < 2

        HP = 12

        UNITS = [(c, b) for c in range(NC) for b in range(2)]

        def on_dve(u):
            return u % 4 == 3

        def dve_units(u):
            return u // 4

        def pool_units(u):
            return u - u // 4

        SORT = []
        k = 2
        while k <= HALF:
            SORT.append((k, None))
            j = k // 4
            while j >= 1:
                SORT.append((k, j))
                j //= 2
            k *= 2
        MERGE = [(HALF, HALF // 2), (HALF, HALF // 4), (HALF, HALF // 8)]
        assert MERGE[-1][1] == G

        block = ctx.enter_context(nc.Block())

        @block.sync
        def _(sp):
            def col(name):
                return a[name].rearrange("(n a) -> n a", a=1)

            def row(name):
                return a[name].rearrange("(a n) -> a n", a=1)

            def attention_weight(l, i):
                sp.dma_start(w_in[l][:, i, :], a[f"L{l}_xattn_" + ("Wq", "Wk", "Wv", "Wo")[i]]).then_inc(
                    ld_w[l][int(i != 1)], 16)

            xr = a["x"].rearrange("b (t p) d -> p (b t) d", p=P)
            sp.dma_start(ctx_in[:, :], a["ctx_1024"].rearrange("b s d -> (b s) d")).then_inc(ld_ctx, 16)
            for i in (1, 0):
                attention_weight(0, i)
            sp.dma_start(x[:, 0:TB, :], xr[:, 0:TB, :]).then_inc(ld_x[0], 16)
            attention_weight(0, 2)
            attention_weight(0, 3)
            sp.dma_start(x[:, TB:NT, :], xr[:, TB:NT, :]).then_inc(ld_x[1], 16)
            for i in (1, 2, 0, 3):
                attention_weight(1, i)
            sp.dma_start(bcol[:, 2:3], col("L1_xattn_bq")).then_inc(ld_b[1], 16)
            sp.dma_start(bcol[:, 3:4], col("L1_xattn_bk")).then_inc(ld_b[1], 16)
            sp.wait_ge(rows_zero, 1)
            sp.dma_start(brow[0:1, BV1:BV1 + D], row("L1_xattn_bv")).then_inc(ld_rows[1], 16)
            sp.dma_start(fdown_in[:, :], a["L0_ffn_Wdown"]).then_inc(ld_ffn0, 16)
            sp.dma_start(fup_in[:, :], a["L0_ffn_Wup"]).then_inc(ld_ffn0, 16)
            sp.dma_start(bup_row[:, :], row("L0_ffn_bup")).then_inc(ld_ffn0, 16)
            sp.dma_start(bdown_col[:, :], col("L0_ffn_bdown")).then_inc(ld_ffn0, 16)
            for i in range(2):
                sp.dma_start(gam[:, i:i + 1], col(f"L0_ffn_gamma{i + 1}")).then_inc(ld_ffn0, 16)
            sp.dma_start(fq_in[:, :], a["L0_ffn_Wq"]).then_inc(ld_ffn0, 16)
            sp.dma_start(fo[:, :], a["L0_ffn_Wo"]).then_inc(ld_ffn0, 16)
            sp.dma_start(wg[:, :], a["L0_ffn_Wg"]).then_inc(ld_ffn0, 16)
            sp.dma_start(we[:, :, :], a["L0_ffn_We"].rearrange("e d f -> d e f")).then_inc(ld_ffn0, 16)
            for i, w in enumerate(("bup", "bgate")):
                sp.dma_start(bug_in[i * NC:(i + 1) * NC, :],
                             a["L1_ffn_" + w].rearrange("(c j) h -> c (j h)", j=EC)).then_inc(ld_bug, 16)
            for name, at, n in (("L0_ffn_bq", BQKV, D), ("L0_ffn_bo", BOF, D), ("L0_ffn_bg", BG, E0),
                                ("L1_xattn_bo", BO1, D), ("L1_ffn_br", BR, E1)):
                sp.dma_start(brow[0:1, at:at + n], row(name)).then_inc(ld_rows[2], 16)
            mr = a["mask_Bx1xSxS2_bk1"].rearrange("b o (t p) c -> p (b o t) c", p=P)
            sp.dma_start(maskt[:, :, :], mr).then_inc(ld_mask, 16)
            sp.dma_start(wr[:, :], a["L1_ffn_Wr"]).then_inc(ld_ffn1, 16)
            sp.dma_start(wup[:, :, :], a["L1_ffn_Wup"].rearrange("e d h -> d e h")).then_inc(ld_up, 16)
            sp.dma_start(wgate[:, :, :], a["L1_ffn_Wgate"].rearrange("e d h -> d e h")).then_inc(ld_up, 16)
            sp.dma_start(wdn[:, :, :], a["L1_ffn_Wdown"].rearrange("(c j) h d -> (j h) c d", j=EC)).then_inc(ld_up, 16)
            sp.wait_ge(bdn_zero, 2)
            for b in range(2):
                sp.dma_start(bdn[b * E1:(b + 1) * E1, b, :], a["L1_ffn_bdown"]).then_inc(ld_up, 16)
            orr = out.rearrange("b (t p) d -> p (b t) d", p=P)
            for b in range(2):
                sp.wait_ge(res_done, TB * (b + 1))
                sp.dma_start(orr[:, b * TB:(b + 1) * TB, :], res[:, b * TB:(b + 1) * TB, :]).then_inc(stored, 16)
            sp.wait_ge(stored, 32)

        @block.gpsimd
        def _(pool):
            steps = Steps(pool, pool_steps)

            def mask_from(tile, value, *selects):
                steps.mark(nc.gpsimd.memset(tile, value))
                for op, fill, base, pattern, mult in selects:
                    steps.wait()
                    steps.mark(nc.gpsimd.affine_select(out=tile, in_=tile, compare_op=op, fill=fill, base=base,
                                                       pattern=pattern, channel_multiplier=mult))

            mask_from(ident[:, :], 0.0, (ALU.not_equal, 1.0, 0, [[-1, P]], 1))
            steps.wait()
            nc.gpsimd.memset(neg[:, :], -1e9).then_inc(consts, 1)
            mask_from(row0[:, :], 0.0, (ALU.not_equal, 1.0, 0, [[0, P]], 1))
            mask_from(jmask[:, :], 1.0, (ALU.is_ge, 0.0, 0, [[-C, CH]], 1),
                      (ALU.is_ge, 0.0, C - 1, [[C, CH]], -1))
            mask_from(headmask[:, :], 1.0, (ALU.is_ge, 0.0, 0, [[-HD, H]], 1),
                      (ALU.is_ge, 0.0, HD - 1, [[HD, H]], -1))
            steps.wait()
            nc.gpsimd.memset(ones[:, :], 1.0).then_inc(consts, 1)

            def block_keys(l):
                pool.wait_ge(kT_done[l], 1)
                for b in range(B):
                    nc.gpsimd.tensor_tensor(
                        kblk[l][:, b, :, :],
                        kT[l][:, b * C:(b + 1) * C].unsqueeze(1).to_broadcast([P, H, C]),
                        headmask[:, :].unsqueeze(2).to_broadcast([P, H, C]), ALU.mult).then_inc(kblk_done, 1)

            block_keys(0)
            pool.wait_ge(ld_ffn0, 16 * 10)
            nc.gpsimd.tensor_scalar(wqkv[:, 0:D], fq_in[:, :], gam[:, 0:1], None, ALU.mult).then_inc(scaled0, 1)
            nc.gpsimd.tensor_scalar(wg[:, :], wg[:, :], gam[:, 1:2], None, ALU.mult).then_inc(scaled0, 1)
            we2 = we[:, :, :].rearrange("p e f -> p (e f)")
            pool.wait_ge(tg_done, 1)
            nc.gpsimd.tensor_scalar(we2, we2, gam[:, 1:2], tg[:, 2:3], ALU.mult, ALU.mult).then_inc(scaled0, 1)

            mask_from(swap[:, :], 0.0, (ALU.not_equal, 1.0, E1, [[-1, P]], 1), (ALU.not_equal, 1.0, -E1, [[-1, P]], 1))
            mask_from(samehalf[:, :].rearrange("p (b e) -> p b e", b=2), 1.0,
                      (ALU.is_ge, 0.0, 0, [[-E1, 2], [0, E1]], 1), (ALU.is_ge, 0.0, E1 - 1, [[E1, 2], [0, E1]], -1))
            mask_from(low2high[:, :].rearrange("p (b e) -> p b e", b=2), 1.0,
                      (ALU.is_ge, 0.0, E1 - 1, [[0, 2], [0, E1]], -1), (ALU.is_ge, 0.0, -1, [[1, 2], [0, E1]], 0))
            mask_from(upto[:, :], 1.0, (ALU.is_ge, 0.0, 0, [[1, P]], -1))
            steps.wait()
            steps.mark(nc.gpsimd.tensor_tensor(upto[:, :], upto[:, :], samehalf[:, :], ALU.mult))
            mask_from(high[:, :], 1.0, (ALU.is_ge, 0.0, -E1, [[0, 1]], 1))
            mask_from(halfcol[:, :], 1.0, (ALU.is_ge, 0.0, 0, [[-E1, 2]], 1), (ALU.is_ge, 0.0, E1 - 1, [[E1, 2]], -1))
            block_keys(1)

            def mul_qk(t):
                pool.wait_ge(qkv_done, t + 1)
                at_least(pool, redqk, t - 1)
                q = qkv[:, t % 4, 0:D].rearrange("p (h d) -> p h d", h=H)
                k = qkv[:, t % 4, D:2 * D].rearrange("p (h d) -> p h d", h=H)
                nc.gpsimd.tensor_tensor(prod[:, t % 2, :].rearrange("p (h g d) -> p h g d", h=H, g=H),
                                        q.unsqueeze(2).to_broadcast([P, H, H, HD]),
                                        k.unsqueeze(1).to_broadcast([P, H, H, HD]), ALU.mult).then_inc(mulqk, 1)

            def mul_av(t):
                pool.wait_ge(eB_done, t + 1)
                at_least(pool, redav, t - 1)
                w = eB[:, t % 2, :].rearrange("p (h g) -> p h g", h=H)
                v = qkv[:, t % 4, 2 * D:3 * D].rearrange("p (d g) -> p d g", d=HD)
                nc.gpsimd.tensor_tensor(prov[:, t % 2, :].rearrange("p (h d g) -> p h d g", h=H, d=HD)[:, 0:HP],
                                        w[:, 0:HP].unsqueeze(2).to_broadcast([P, HP, HD, H]),
                                        v.unsqueeze(1).to_broadcast([P, HP, HD, H]), ALU.mult).then_inc(mulav, 1)

            def weight_low(k):
                pool.wait_ge(w_high, k + 1)
                src, high, low = piece(k)
                nc.gpsimd.tensor_tensor(low, src, high.bitcast(F32), ALU.subtract).then_inc(w_low, 1)

            def normalise_c(t):
                n = 2 * NT + t
                pool.wait_ge(rstd_done, n + 1)
                pool.wait_ge(yT_ps, n - 1)
                nc.gpsimd.tensor_scalar(y[:, n % 2, :], x[:, t, :], mv[:, n, 0:1], rstd[:, n:n + 1],
                                        ALU.subtract, ALU.mult).then_inc(yC_done, 1)

            for t in range(NT + 1):
                if t < NT:
                    mul_qk(t)
                if t >= 1:
                    mul_av(t - 1)
                if t >= NT - 2:
                    normalise_c(t - NT + 2)
            for t in range(3, NT):
                normalise_c(t)
                k = t - 3
                weight_low(k)
            for k in range(NT - 3, PIECES):
                weight_low(k)

            for t in range(NT):
                pool.wait_ge(x_high, t + 1)
                pool.wait_ge(yT_done, 3 * NT + t + 1)
                cols = slice(t * P, (t + 1) * P)
                nc.gpsimd.tensor_tensor(xl[:, cols], yTD[:, cols], xh[:, cols].bitcast(F32), ALU.subtract).then_inc(x_low, 1)

            for u, (c, b) in enumerate(UNITS):
                if not on_dve(u):
                    m = pool_units(u)
                    pool.wait_ge(gsb_done, m + 1)
                    if u < 4:
                        pool.wait_ge(rT_ps, 1)
                    nc.gpsimd.tensor_tensor(hidden_values(c, b), gsb[:, m % 3, :], silu[:, u % 4, :],
                                            ALU.mult).then_inc(hg_pool, 1)

            pool.wait_ge(hg_pool, pool_units(len(UNITS)))
            pool.wait_ge(hg_dve, dve_units(len(UNITS)))
            for b in range(2):
                at_least(pool, sel_done, b)
                mask_from(sel_f32.rearrange("p (c j h) -> p c j h", c=NC, j=EC), 0.0,
                          (ALU.not_equal, 1.0, -b * E1, [[-EC, NC], [-1, EC], [0, EH]], 1))
                steps.wait()
                nc.gpsimd.memset(sel_mark[:, b:b + 1], 0.0).then_inc(sel_made, 1)

        @block.scalar
        def _(act):
            steps = Steps(act, act_steps)

            def col(name):
                return a[name].rearrange("(n a) -> n a", a=1)

            for i, g in enumerate(("g_xattn", "g_ffn")):
                act.dma_start(gcol[:, 2 * i:2 * i + 2], a[g].partition_broadcast(P)).then_inc(ld_gate, 16)
            act.dma_start(bcol[:, 1:2], col("L0_xattn_bk")).then_inc(ld_b[0], 16)
            act.dma_start(bcol[:, 0:1], col("L0_xattn_bq")).then_inc(ld_b[0], 16)
            act.wait_ge(rows_zero, 1)
            for name, at in (("L0_xattn_bv", BV0), ("L0_xattn_bo", BO0)):
                act.dma_start(brow[0:1, at:at + D], a[name].rearrange("(a n) -> a n", a=1)).then_inc(ld_rows[0], 16)
            nc.scalar.preload_act_table_set("exp_and_others")
            act.wait_ge(ld_gate, 32)
            nc.scalar.activation(tg[:, :], gcol[:, :], ACT.Tanh).then_inc(tg_done, 1)
            nc.scalar.preload_act_table_set("natural_log_exp_and_others")

            def setup0():
                act.wait_ge(setup_ps, 3)
                nc.scalar.activation(wT[0][:, 0, :], pE[0][:, 0:D], ACT.Copy).then_inc(wT_done, 1)
                nc.scalar.activation(wT[0][:, 2:4, :].rearrange("p i n -> p (i n)"), pE[0][:, D:3 * D],
                                     ACT.Copy).then_inc(wT_done, 1)
                act.wait_ge(ld_b[0], 32)
                steps.mark(nc.scalar.mul(bqs[:, 0:1], bcol[:, 0:1], SC))
                steps.wait()

            def weights_ready(k):
                if k in (0, 1, 2, 4):
                    act.wait_ge(part_ps, k + 1)
                if k == 0:
                    nc.scalar.activation(wT[1][:, 0:3, :].rearrange("p i n -> p (i n)"), pTB[:, P:P + 3 * D],
                                         ACT.Copy).then_inc(part_read, 1)
                elif k == 1:
                    steps.mark(nc.scalar.activation(wT[1][:, 3, :], pTB[:, P:2 * P], ACT.Copy))
                    nc.scalar.activation(bug[:, :, :].rearrange("p i c -> p (i c)"), pTB[:, 2 * P:2 * P + 2 * NC],
                                         ACT.Copy).then_inc(part_read, 1)
                    act.wait_ge(ld_b[1], 32)
                    steps.mark(nc.scalar.mul(bqs[:, 1:2], bcol[:, 2:3], SC))
                elif k == 2:
                    nc.scalar.activation(kT[1][:, :], pTB[:, P:P + B * C], ACT.Identity, bias=bcol[:, 3:4]).then_inc(kT_done[1], 1)
                    nc.scalar.activation(wdT[:, :], pTB[0:L, 2 * P:2 * P + D], ACT.Copy).then_inc(part_read, 1)
                elif k == 4:
                    kv = pTB[:, P:P + 2 * D].rearrange("p (g k d) -> p k g d", g=H, k=2)
                    nc.scalar.activation(wqkv[:, D:2 * D].rearrange("p (g d) -> p g d", g=H), kv[:, 0], ACT.Copy,
                                         scale=gam[:, 0:1]).then_inc(wkv_done, 1)
                    nc.scalar.activation(wqkv[:, 2 * D:3 * D].rearrange("p (d g) -> p g d", g=H), kv[:, 1], ACT.Copy,
                                         scale=gam[:, 0:1]).then_inc(part_read, 1)

            std_step = {}

            def rstd_of(n):
                act.wait_ge(stats, n + 1)
                k = steps.mark(nc.scalar.activation(lnv[:, n:n + 1], mv[:, n, 1:2], ACT.Ln, bias=eps[:, 0:1]))
                if NT <= n < 2 * NT:
                    t = n - NT
                    k2 = steps.mark(nc.scalar.activation(lnu[:, t:t + 1], mv[:, n, 1:2], ACT.Ln,
                                                         bias=eps[:, 1:2], scale=1.0 + 1e-6))
                    steps.wait(k)
                    steps.mark(nc.scalar.activation(rstd[:, n:n + 1], lnv[:, n:n + 1], ACT.Exp, scale=-0.5))
                    steps.wait(k2)
                    std_step[t] = steps.n
                    nc.scalar.activation(ustd[:, t:t + 1], lnu[:, t:t + 1], ACT.Exp, scale=-0.5).then_inc(rstd_done, 1)
                else:
                    steps.wait(k)
                    nc.scalar.activation(rstd[:, n:n + 1], lnv[:, n:n + 1], ACT.Exp, scale=-0.5).then_inc(rstd_done, 1)

            def copy_yT(n):
                act.wait_ge(yT_ps, n + 1)
                if n < 3 * NT:
                    m = n - 2
                    if m >= 0:
                        if NT <= m < 2 * NT:
                            act.wait_ge(proj_ps, m + 1)
                        else:
                            act.wait_ge(q_ps, (m if m < NT else m - NT) + 1)
                    dst = yT[:, n % 2, :]
                else:
                    dst = yTD[:, (n - 3 * NT) * P:(n - 3 * NT + 1) * P]
                if n >= 3 * NT:
                    t = n - 3 * NT
                    nc.scalar.activation(xh[:, t * P:(t + 1) * P], pTA[:, 0:P], ACT.Copy).then_inc(x_high, 1)
                nc.scalar.activation(dst, pTA[:, 0:P], ACT.Copy).then_inc(yT_done, 1)

            def copy_oT(n):
                act.wait_ge(oT_ps, n + 1)
                at_least(act, w_ps, n - 1)
                nc.scalar.activation(oT[:, n % 2, :], pTB[:, 0:P], ACT.Copy).then_inc(oT_done, 1)

            def exponentials(k):
                act.wait_ge(e_shift, k + 1)
                nc.scalar.activation(e[:, k % 2, :], e[:, k % 2, :], ACT.Exp).then_inc(e_done, 1)

            def attention(l, i):
                base, k0 = 2 * l * NT, l * NT
                if 0 <= i < NT and not ahead(l, i):
                    exponentials(k0 + i)
                if l == 0 and 1 <= i <= PARTS:
                    weights_ready(i - 1)
                t = i + 2
                if 0 <= t < NT:
                    n, k = base + t, k0 + t
                    act.wait_ge(q_ps, k + 1)
                    at_least(act, proj_ps, n - 1)
                    nc.scalar.activation(qT[:, k % 2, :], pTA[:, 256:256 + P], ACT.Identity,
                                         bias=bqs[:, l:l + 1], scale=SC).then_inc(q_done, 1)
                t = i
                if 0 <= t < NT:
                    k = k0 + t
                    act.wait_ge(eT_ps, k + 1)
                    at_least(act, o_ps, k - 1)
                    nc.scalar.activation(eT[:, k % 2, :], pE[k % 2][:, :], ACT.Copy).then_inc(eT_done, 1)
                if 0 <= i + 3 < NT:
                    copy_yT(base + i + 3)
                if 0 <= i - 1 < NT:
                    copy_oT(base + i - 1)
                if 0 <= i - 2 < NT:
                    rstd_of(base + NT + i - 2)
                if l == 1 and 0 <= i < PIECES:
                    if i == 0:
                        act.wait_ge(ld_up, 16 * 5)
                        act.wait_ge(redav, NT)
                    src, high, _ = piece(i)
                    nc.scalar.activation(high, src, ACT.Copy).then_inc(w_high, 1)

            def normalise(t):
                act.wait_ge(rstd_done, NT + t + 1)
                k = steps.mark(nc.scalar.activation(nmu[:, t:t + 1], ustd[:, t:t + 1], ACT.Copy, scale=negm[:, t:t + 1]))
                steps.wait(std_step[t])
                steps.mark(nc.scalar.activation(nmr[:, t:t + 1], rstd[:, NT + t:NT + t + 1], ACT.Copy, scale=negm[:, t:t + 1]))
                steps.wait(k)
                at_least(act, yT_ps, NT + t - 1)
                nc.scalar.activation(y[:, t % 2, :], x[:, t, :], ACT.Identity, bias=nmu[:, t:t + 1],
                                     scale=ustd[:, t:t + 1]).then_inc(yB_ready, 1)
                steps.wait(k + 1)
                nc.scalar.activation(yB[:, t, :], x[:, t, :], ACT.Identity, bias=nmr[:, t:t + 1],
                                     scale=rstd[:, NT + t:NT + t + 1]).then_inc(yB_done, 1)

            def heads(i):
                if 0 <= i + 2 < NT:
                    copy_yT(NT + i + 2)
                t = i - 3
                if 0 <= t < NT:
                    for j in range(2):
                        act.wait_ge(hgT_ps, 2 * t + j + 1)
                        at_least(act, moe_ps, t)
                        nc.scalar.activation(hgateT[:, j * 512:(j + 1) * 512], pE[j][:, :], ACT.Copy).then_inc(hgT_done, 1)
                if 0 <= i < NT:
                    act.wait_ge(sB_done, i + 1)
                    at_least(act, mulav, i - 1)
                    at_least(act, mulav_vec, i - 1)
                    at_least(act, sumB, i - 1)
                    nc.scalar.activation(eB[:, i % 2, :], sB[:, i % 2, :], ACT.Exp, scale=SC).then_inc(eB_done, 1)
                t = i - 2
                if 0 <= t < NT:
                    act.wait_ge(w_read, NT + t + 1)
                    steps.mark(nc.scalar.activation(sq[:, :], xp[:, t % 2, :], ACT.Square, accum_out=ssq[:, t:t + 1]))
                    steps.wait()
                    steps.mark(nc.scalar.activation(lns[:, t:t + 1], ssq[:, t:t + 1], ACT.Ln, bias=eps[:, 2:3], scale=1.0 / D))
                    steps.wait()
                    steps.mark(nc.scalar.activation(rms[:, t:t + 1], lns[:, t:t + 1], ACT.Exp, scale=-0.5))
                    steps.wait()
                    at_least(act, h2T_ps, t - 1)
                    nc.scalar.activation(h2[:, t % 2, :], xp[:, t % 2, :], ACT.Copy, scale=rms[:, t:t + 1]).then_inc(h2_done, 1)
                if 0 <= t < NT:
                    act.wait_ge(h2T_ps, t + 1)
                    at_least(act, gl_ps, t)
                    nc.scalar.activation(h2T[:, :], pTB[:, P:2 * P], ACT.Copy).then_inc(h2T_done, 1)
                if 0 <= i + 2 < NT:
                    act.wait_ge(proj_ps, NT + i + 2 + 1)
                    at_least(act, mulav, i - 1)
                    at_least(act, mulav_vec, i - 1)
                    nc.scalar.activation(qkv[:, (i + 2) % 4, :], pS[i % 2][:, 0:3 * D], ACT.Copy).then_inc(qkv_done, 1)
                if 0 <= i + 4 < NT:
                    normalise(i + 4)
                if 0 <= i - 1 < NT:
                    copy_oT(NT + i - 1)
                if 0 <= t < NT:
                    act.wait_ge(gmx_done, t + 1)
                    nc.scalar.activation(gex[:, t % 2, :], pW[:, 256:256 + E0], ACT.Exp, bias=gmx[:, t:t + 1],
                                         accum_out=gsum[:, t:t + 1]).then_inc(gex_done, 1)
                    act.wait_ge(gex_done, t + 1)
                    at_least(act, hgT_ps, 2 * t)
                    for k in range(E0):
                        ins = nc.scalar.activation(hgate[:, k, :], h2[:, t % 2, :], ACT.Copy, scale=gex[:, t % 2, k:k + 1])
                        if k % (E0 // 2) == E0 // 2 - 1:
                            ins.then_inc(hgate_done, 1)
                if 0 <= i - 3 < NT:
                    rstd_of(2 * NT + i - 3)

            def router(i):
                if 0 <= i + 2 < NT:
                    copy_yT(3 * NT + i + 2)
                if 0 <= i < NT:
                    act.wait_ge(rmx_done, i + 1)
                    at_least(act, rsc_done, i - 1)
                    nc.scalar.activation(rex[:, i % 2, :], pS[i % 2][:, 0:E1], ACT.Exp, bias=rmx[:, i:i + 1],
                                         accum_out=rsum[:, i:i + 1]).then_inc(rex_done, 1)

            for stage, i in SCHEDULE:
                if (stage, i) == ("A", -4):
                    act.wait_ge(eps_set, 3)
                    for n in range(TB):
                        rstd_of(n)
                    setup0()
                if (stage, i) == ("A", -1):
                    for n in range(TB, NT):
                        rstd_of(n)
                if stage == "B" and ahead(1, i - NT - 1):
                    exponentials(i - 1)
                {"A": lambda i: attention(0, i), "B": heads, "C": lambda i: attention(1, i), "D": router}[stage](i)

            act.wait_ge(rT_ps, 1)
            nc.scalar.activation(rT[:, :], pTB[:, :], ACT.Copy).then_inc(rT_done, 1)
            for u, (c, b) in enumerate(UNITS):
                act.wait_ge(up_ps, u + 1)
                if u >= 4:
                    act.wait_ge(*((hg_dve, dve_units(u - 4) + 1) if on_dve(u) else (hg_pool, pool_units(u - 4) + 1)))
                nc.scalar.activation(silu[:, u % 4, :], pS[b][:, :], ACT.Silu, bias=bug[:, 0, c:c + 1]).then_inc(silu_done, 1)
                if not on_dve(u):
                    m = pool_units(u)
                    act.wait_ge(gate_ps, u + 1)
                    at_least(act, hg_pool, m - 2)
                    nc.scalar.activation(gsb[:, m % 3, :], pE[b][:, :], ACT.Identity, bias=bug[:, 1, c:c + 1]).then_inc(gsb_done, 1)
            act.wait_ge(pick_ps, 1)
            for b in range(2):
                nc.scalar.activation(allgs[:, b * HALF:(b + 1) * HALF], (pTA, pTB)[b][:, :], ACT.Copy).then_inc(allgs_done, 1)
            for b in range(2):
                act.wait_ge(sel_made, b + 1)
                nc.scalar.activation(sel[:, b, :, :].rearrange("p c q -> p (c q)"), sel_f32, ACT.Copy).then_inc(sel_done, 1)
            for b in range(2):
                act.wait_ge(down_ps, b + 1)
                nc.scalar.activation(fT[:, b * HALF:(b + 1) * HALF], pE[b][:, :], ACT.Copy).then_inc(fT_done, 1)

        @block.tensor
        def _(pe):
            mm = nc.tensor.matmul
            transpose = nc.tensor.transpose

            def bias(dst, row):
                return mm(dst, row0[:, :], row, start=False, stop=True)

            def values(l, b, dst):
                mm(dst, ctx4[:, b, :, :].rearrange("p j k -> p (j k)"), wT[l][:, 2, :], start=True, stop=False)
                at = (BV0, BV1)[l]
                return bias(dst, brow[:, at:at + D])

            pe.wait_ge(consts, 1)
            pe.wait_ge(ld_ctx, 16)
            transpose(pO[:, 0:B * C], ctx_in[:, :], ident[0:B * C, 0:B * C]).then_inc(setup_ps, 1)
            pe.wait_ge(ld_w[0][0], 16)
            transpose(pE1[:, 0:D], w_in[0][:, 1, :], ident[:, :]).then_inc(setup_ps, 1)
            pe.wait_ge(ctx_done, 2)
            pe.wait_ge(wk_done, 1)
            pe.wait_ge(ld_w[0][1], 48)
            for k, i in enumerate((0, 2, 3)):
                m = transpose(pE0[:, k * D:(k + 1) * D], w_in[0][:, i, :], ident[:, :])
            m.then_inc(setup_ps, 1)
            mm(pTA[:, 0:B * C], wT[0][:, 1, :], ctxT[:, :]).then_inc(setup_ps, 1)
            pe.wait_ge(wT_done, 2)
            pe.wait_ge(ld_rows[0], 32)
            pe.wait_ge(consts, 2)
            values(0, 0, pS0[:, 0:D])
            values(0, 1, pS1[:, 0:D]).then_inc(setup_ps, 1)

            def weights_ready(k):
                if k == 0:
                    pe.wait_ge(ld_w[1][0], 16)
                    pe.wait_ge(ld_w[1][1], 48)
                    for i in range(3):
                        m = transpose(pTB[:, P + i * D:P + (i + 1) * D], w_in[1][:, i, :], ident[:, :])
                elif k == 1:
                    pe.wait_ge(ld_bug, 32)
                    transpose(pTB[:, P:2 * P], w_in[1][:, 3, :], ident[:, :])
                    m = transpose(pTB[:, 2 * P:2 * P + 2 * NC], bug_in[:, :], ident[0:2 * NC, 0:2 * NC])
                elif k == 2:
                    pe.wait_ge(ld_ffn0, 16 * 10)
                    mm(pTB[:, P:P + B * C], wT[1][:, 1, :], ctxT[:, :])
                    m = transpose(pTB[0:L, 2 * P:2 * P + D], fdown_in[:, :], ident[:, :])
                elif k == 3:
                    pe.wait_ge(ld_rows[1], 16)
                    values(1, 0, pTB[:, P:P + D])
                    m = values(1, 1, pTB[:, P + D:P + 2 * D])
                elif k == 4:
                    m = mm(pTB[:, P:P + 2 * D], wdT[:, :], fup_in[:, :])
                elif k == 5:
                    m = mm(pTB[0:1, P:P + 2 * D], bdown_col[:, :], fup_in[:, :])
                m.then_inc(part_ps, 1)

            def queries_before(n):
                return min(n, NT) + min(max(n - 2 * NT, 0), NT)

            def transpose_y(n):
                if NT <= n < 2 * NT:
                    pe.wait_ge(yB_ready, n - NT + 1)
                elif 2 * NT <= n < 3 * NT:
                    pe.wait_ge(yC_done, n - 2 * NT + 1)
                else:
                    pe.wait_ge(y_done, (n if n < NT else n - 2 * NT) + 1)
                if n == 0:
                    pe.wait_ge(kT_done[0], 1)
                at_least(pe, yT_done, n)
                at_least(pe, q_done, queries_before(n))
                transpose(pTA[:, 0:P], y[:, n % 2, :], ident[:, :]).then_inc(yT_ps, 1)

            def transpose_o(n):
                pe.wait_ge(o_done, n + 1)
                at_least(pe, oT_done, n)
                at_least(pe, part_read, min(n + 1, PARTS))
                transpose(pTB[:, 0:P], o[:, n % 2, :], ident[:, :]).then_inc(oT_ps, 1)

            def project_o(n, w, bo):
                pe.wait_ge(oT_done, n + 1)
                at_least(pe, w_read, n)
                if NT < n < 2 * NT:
                    pe.wait_ge(gex_done, n - NT)
                elif n >= 2 * NT:
                    pe.wait_ge(gex_done, NT)
                mm(pW[:, 0:D], oT[:, n % 2, :], w, start=True, stop=False)
                bias(pW[:, 0:D], bo).then_inc(w_ps, 1)

            def scores_bank_free(n):
                if n < 2:
                    pe.wait_ge(vblk_done, 2)
                    return
                st, t = divmod(n - 2, NT)
                pe.wait_ge(*((e_shift, t + 1), (qkv_done, t + 1), (e_shift, NT + t + 1), (rex_done, t + 1))[st])

            def attention(l, i):
                base, k0 = 2 * l * NT, l * NT
                t = i
                if 0 <= t < NT:
                    k = k0 + t
                    pe.wait_ge(e_done, k + 1)
                    at_least(pe, eT_done, k - 1)
                    if l == 1 and t < 2:
                        pe.wait_ge(hgT_done, 2 * NT)
                    for c in range(HC):
                        m = transpose(pE[k % 2][:, c * P:(c + 1) * P], e[:, k % 2, c * P:(c + 1) * P], ident[:, :])
                    m.then_inc(eT_ps, 1)
                if 0 <= i + 3 < NT:
                    transpose_y(base + i + 3)
                if 0 <= i - 1 < NT:
                    transpose_o(base + i - 1)
                t = i + 2
                if 0 <= t < NT:
                    n, k, b = base + t, k0 + t, t // TB
                    pe.wait_ge(q_done, k + 1)
                    scores_bank_free(n)
                    pe.wait_ge(kblk_done, 2 * l + b + 1)
                    mm(pS[n % 2][:, :], qT[:, k % 2, :],
                       kblk[l][:, b, :, :].rearrange("p h k -> p (h k)")).then_inc(proj_ps, 1)
                t = i
                if 0 <= t < NT:
                    n, k, b = base + t, k0 + t, t // TB
                    pe.wait_ge(eT_done, k + 1)
                    if l == 0:
                        at_least(pe, o_done, n)
                    elif t > 0:
                        pe.wait_ge(o_done, n)
                    else:
                        pe.wait_ge(moe_read, NT)
                        pe.wait_ge(vblk_done, 4)
                    w9 = CH * HC9
                    for c in range(HC):
                        m = mm(pO[:, c * w9:(c + 1) * w9], eT[:, k % 2, c * P:(c + 1) * P],
                               vblk[l][:, b, c, :, :].rearrange("p j d -> p (j d)"))
                    m.then_inc(o_ps, 1)
                t = i + 3
                if 0 <= t < NT:
                    pe.wait_ge(yT_done, base + t + 1)
                    mm(pTA[:, 256:256 + P], wT[l][:, 0, :], yT[:, (base + t) % 2, :]).then_inc(q_ps, 1)
                if 0 <= i - 1 < NT:
                    at = (BO0, BO1)[l]
                    project_o(base + i - 1, wT[l][:, 3, :], brow[:, at:at + D])
                if l == 0 and 0 <= i < PARTS:
                    weights_ready(i)

            def heads(i):
                if 0 <= i + 2 < NT:
                    transpose_y(NT + i + 2)
                t = i - 3
                if 0 <= t < NT:
                    for j in range(2):
                        pe.wait_ge(hgate_done, 2 * t + j + 1)
                        at_least(pe, hgT_done, 2 * t)
                        if t == 0:
                            pe.wait_ge(eT_done, NT)
                        for k in range(E0 // 2):
                            m = transpose(pE[j][:, k * P:(k + 1) * P], hgate[:, j * E0 // 2 + k, :], ident[:, :])
                        m.then_inc(hgT_ps, 1)
                if 0 <= i + 2 < NT:
                    n = NT + i + 2
                    pe.wait_ge(yT_done, n + 1)
                    scores_bank_free(n)
                    mm(pS[n % 2][:, 0:3 * D], yT[:, n % 2, :], wqkv[:, :], start=True, stop=False)
                    bias(pS[n % 2][:, 0:3 * D], brow[:, BQKV:BQKV + 3 * D]).then_inc(proj_ps, 1)

                def experts(half):
                    t = i - 3
                    if 0 <= t < NT:
                        at_least(pe, moe_read, t)
                        if t == 0:
                            pe.wait_ge(o_done, NT)
                        pe.wait_ge(hgT_done, 2 * t + 1 + half)
                        for k in range(half * E0 // 2, (half + 1) * E0 // 2):
                            m = mm(pO[:, P:2 * P], hgateT[:, k * P:(k + 1) * P], we[:, k, :], start=k == 0, stop=k == E0 - 1)
                        if half == 1:
                            m.then_inc(moe_ps, 1)

                experts(0)
                t = i - 2
                if 0 <= t < NT:
                    pe.wait_ge(h2_done, t + 1)
                    pe.wait_ge(oT_done, NT + t + 1)
                    at_least(pe, h2T_done, t)
                    transpose(pTB[:, P:2 * P], h2[:, t % 2, :], ident[:, :]).then_inc(h2T_ps, 1)
                    pe.wait_ge(h2T_done, t + 1)
                    pe.wait_ge(w_read, NT + t + 1)
                    mm(pW[:, 256:256 + E0], h2T[:, :], wg[:, :], start=True, stop=False)
                    bias(pW[:, 256:256 + E0], brow[:, BG:BG + E0]).then_inc(gl_ps, 1)
                experts(1)
                if 0 <= i - 1 < NT:
                    transpose_o(NT + i - 1)
                    project_o(NT + i - 1, fo[:, :], brow[:, BOF:BOF + D])

            def router(i):
                t = i + 2
                if 0 <= t < NT:
                    n = 3 * NT + t
                    transpose_y(n)
                    pe.wait_ge(yT_done, n + 1)
                    scores_bank_free(n)
                    mm(pS[n % 2][:, 0:E1], yTD[:, t * P:(t + 1) * P], wr[:, :], start=True, stop=False)
                    bias(pS[n % 2][:, 0:E1], brow[:, BR:BR + E1]).then_inc(proj_ps, 1)

            for stage, i in SCHEDULE:
                if (stage, i) == ("B", -2):
                    pe.wait_ge(wkv_done, 1)
                    pe.wait_ge(part_read, PARTS)
                    pe.wait_ge(scaled0, 3)
                    pe.wait_ge(ld_rows[2], 16 * 5)
                    pe.wait_ge(ld_ffn1, 16)
                {"A": lambda i: attention(0, i), "B": heads, "C": lambda i: attention(1, i), "D": router}[stage](i)

            def transpose_scores():
                pe.wait_ge(rsc_done, NT)
                for j in range(TB):
                    m = transpose(pTB[:, j * P:(j + 1) * P], rsc[:, j, :, :].rearrange("p b e -> p (b e)"), ident[:, :])
                m.then_inc(rT_ps, 1)

            def split_product(dst, c, which, b):
                cols = slice(b * HALF, (b + 1) * HALF)
                high, low = ws[:, c, which, 0, :], ws[:, c, which, 1, :]
                mm(dst, high, xh[:, cols], start=True, stop=False)
                mm(dst, high, xl[:, cols], start=False, stop=False)
                return mm(dst, low, xh[:, cols], start=False, stop=True)

            pe.wait_ge(ld_up, 16 * 5)
            pe.wait_ge(w_low, PIECES)
            pe.wait_ge(x_low, NT)
            pe.wait_ge(rex_done, NT)
            pe.wait_ge(w_read, 3 * NT)
            for u, (c, b) in enumerate(UNITS):
                at_least(pe, silu_done, u - 1)
                split_product(pS[b][:, :], c, 0, b).then_inc(up_ps, 1)
                if u == 0:
                    transpose_scores()
                if u >= 2:
                    pe.wait_ge(*((hg_dve, dve_units(u - 2) + 1) if on_dve(u - 2) else (gsb_done, pool_units(u - 2) + 1)))
                split_product(pE[b][:, :], c, 1, b).then_inc(gate_ps, 1)
            pe.wait_ge(pick_vec, 1)
            pe.wait_ge(rT_done, 1)
            dg = diag.rearrange("p c q -> p (c q)")
            for b in range(2):
                m = mm((pTA, pTB)[b][:, :], ones[:, 0:P], dg[:, b * HALF:(b + 1) * HALF])
            m.then_inc(pick_ps, 1)
            pe.wait_ge(pick_vec, 2)
            transpose(pO[0:1, 0:P], st2[:, 0:1], ident[:, :]).then_inc(pick_ps, 1)
            pe.wait_ge(pick_vec, 3)
            mm(pO[:, 256:257], ones[0:1, 0:P], lmax[0:1, 0:1]).then_inc(pick_ps, 1)
            pe.wait_ge(pick_vec, 4)
            mm(pW[:, 0:GH], upto[:, :], small[:, 2, :], start=True, stop=False)
            mm(pW[:, 0:GH], samehalf[:, :], small[:, 4, :], start=False, stop=False)
            mm(pW[:, 0:GH], low2high[:, :], small[:, 5, :], start=False, stop=True).then_inc(pick_ps, 1)
            pe.wait_ge(pick_vec, 5)
            mm(pO[:, 0:2], swap[:, :], st2[:, 2:4]).then_inc(pick_ps, 1)
            pe.wait_ge(pick_vec, 6)
            mm(pW[:, 0:2], swap[:, :], st2[:, 4:6]).then_inc(pick_ps, 1)
            pe.wait_ge(silu_done, len(UNITS))
            pe.wait_ge(hg_dve, dve_units(len(UNITS)))
            pe.wait_ge(hg_pool, pool_units(len(UNITS)))
            pe.wait_ge(sel_done, 2)
            pe.wait_ge(allgs_done, 2)
            pe.wait_ge(fs_done, 2)

            def spread(u):
                c, b = UNITS[u]
                at_least(pe, h_done, u - 3)
                for part in range(2):
                    m = mm(BC[u % 4][:, :], sel[:, b, c, :], fsr[:, part, :], start=part == 0, stop=part == 1)
                m.then_inc(bc_ps, 1)

            for u in range(2):
                spread(u)
            for j in range(TB):
                m = mm(pO[:, 2 * j:2 * j + 2], fs[:, j * P:(j + 1) * P], halfcol[:, :])
            m.then_inc(den_ps, 1)
            for u, (c, b) in enumerate(UNITS):
                if u + 2 < len(UNITS):
                    spread(u + 2)
                pe.wait_ge(h_done, u + 1)
                mm(pE[b][:, :], wdn[:, c, :], hidden_values(c, b), start=c == 0, stop=False)
                if c == NC - 1:
                    mm(pE[b][:, :], bdn[:, b, :], fs[:, :], start=False, stop=True).then_inc(down_ps, 1)
            pe.wait_ge(h_done, len(UNITS))
            for b in range(2):
                pe.wait_ge(fT_done, b + 1)
                for j in range(TB):
                    m = transpose((pTA, pTB)[b][:, j * P:(j + 1) * P],
                                  fT[:, b * HALF + j * P:b * HALF + (j + 1) * P], ident[:, :])
                m.then_inc(res_ps, 1)

        @block.vector
        def _(dve):
            v = nc.vector
            steps = Steps(dve, vec_steps)
            v.memset(brow[:, :], 0.0).then_inc(rows_zero, 1)
            for k, val in enumerate((1e-5, 1e-11, 1e-6)):
                v.memset(eps[:, k:k + 1], val).then_inc(eps_set, 1)
            v.memset(bdn[E1:P, 0, :], 0.0).then_inc(bdn_zero, 1)
            v.memset(bdn[0:E1, 1, :], 0.0).then_inc(bdn_zero, 1)

            def masked_values(l, b, src):
                vv = src.rearrange("p (c j d) -> p c j d", c=HC, j=CH)
                v.tensor_copy(vblk[l][:, b, :, :, HD], jmask[:, :].unsqueeze(1).to_broadcast([P, HC, CH]))
                v.tensor_tensor(vblk[l][:, b, :, :, 0:HD], vv,
                                jmask[:, :].unsqueeze(1).unsqueeze(3).to_broadcast([P, HC, CH, HD]),
                                ALU.mult).then_inc(vblk_done, 1)

            def setup0():
                dve.wait_ge(setup_ps, 1)
                v.tensor_copy(ctxT[:, :], pO[:, 0:B * C]).then_inc(ctx_done, 1)
                v.tensor_copy(ctx4[:, :, :, :], pO[:, 0:B * C].rearrange("p (b k) -> p b k", b=B).unsqueeze(2)
                              .to_broadcast([P, B, CH, C])).then_inc(ctx_done, 1)
                dve.wait_ge(setup_ps, 2)
                v.tensor_copy(wT[0][:, 1, :], pE[1][:, 0:D]).then_inc(wk_done, 1)

            def weights_ready(k):
                if k in (3, 5):
                    dve.wait_ge(part_ps, k + 1)
                if k == 3:
                    for b in range(B):
                        masked_values(1, b, pTB[:, P + b * D:P + (b + 1) * D])
                    dve.wait_ge(vblk_done, 4)
                    v.memset(scale3[:, 0, 0:1], 0.0).then_inc(part_read, 1)
                elif k == 5:
                    dve.wait_ge(ld_ffn0, 16 * 10)
                    kvp = pTB[0:1, P:P + 2 * D].rearrange("p (g k d) -> p k g d", g=H, k=2)
                    kvb = bup_row[:, :].rearrange("p (g k d) -> p k g d", g=H, k=2)
                    steps.mark(v.tensor_tensor(brow[0:1, BQKV + D:BQKV + 2 * D].rearrange("p (g d) -> p g d", g=H),
                                               kvp[:, 0], kvb[:, 0], ALU.add))
                    steps.wait()
                    v.tensor_tensor(brow[0:1, BQKV + 2 * D:BQKV + 3 * D].rearrange("p (d g) -> p g d", g=H),
                                    kvp[:, 1], kvb[:, 1], ALU.add).then_inc(part_read, 1)

            def statistics(*tiles):
                for n in tiles:
                    at_least(dve, stats, n - TB + 1)
                    steps.mark(v.bn_stats(st6[:, n % TB, :], x[:, n % NT, :]))
                first = steps.n - len(tiles) + 1
                for k, n in enumerate(tiles):
                    steps.wait(first + k)
                    if NT <= n < 2 * NT:
                        steps.mark(v.bn_aggr(mv[:, n, :], st6[:, n % TB, :]))
                        steps.wait()
                        v.tensor_scalar(negm[:, n - NT:n - NT + 1], mv[:, n, 0:1], -1.0, None, ALU.mult).then_inc(stats, 1)
                    else:
                        v.bn_aggr(mv[:, n, :], st6[:, n % TB, :]).then_inc(stats, 1)

            def normalise(n):
                t = n % NT
                dve.wait_ge(rstd_done, n + 1)
                at_least(dve, yT_ps, n - 1)
                v.tensor_scalar(y[:, n % 2, :], x[:, t, :], mv[:, n, 0:1], rstd[:, n:n + 1],
                                ALU.subtract, ALU.mult).then_inc(y_done, 1)

            def shifted_scores(l, t):
                n, k = 2 * l * NT + t, l * NT + t
                s3 = pS[n % 2][:, :].rearrange("p (h k) -> p h k", h=H)
                dve.wait_ge(proj_ps, n + 1)
                if l == 1:
                    if t == 0:
                        dve.wait_ge(ld_mask, 16)
                    steps.mark(v.copy_predicated(s3, maskt[:, t, :].unsqueeze(1).to_broadcast([P, H, C]),
                                                 neg[:, :].unsqueeze(2).to_broadcast([P, H, C])))
                    steps.wait()
                steps.mark(v.tensor_reduce(mx[:, k % 2, :], s3, AX.X, ALU.max))
                steps.wait()
                at_least(dve, eT_ps, k - 1)
                v.tensor_tensor(e[:, k % 2, :].rearrange("p (h k) -> p h k", h=H), s3,
                                mx[:, k % 2, :].unsqueeze(2).to_broadcast([P, H, C]),
                                ALU.subtract).then_inc(e_shift, 1)

            def attention(l, i):
                base, k0 = 2 * l * NT, l * NT
                if 0 <= i < NT and not ahead(l, i):
                    shifted_scores(l, i)
                if l == 0 and 1 <= i <= PARTS:
                    weights_ready(i - 1)
                t = i - 1
                if 0 <= t < NT:
                    n, k = base + t, k0 + t
                    o9 = pO[:, 0:H * HC9].rearrange("p (h d) -> p h d", h=H)
                    dve.wait_ge(o_ps, k + 1)
                    if l == 0:
                        steps.mark(v.tensor_scalar(den[:, k % 2, :], o9[:, :, HD], 1e-10, None, ALU.add))
                        steps.wait()
                        steps.mark(v.reciprocal(rec[:, k % 2, :], den[:, k % 2, :]))
                    else:
                        steps.mark(v.reciprocal(rec[:, k % 2, :], o9[:, :, HD]))
                    steps.wait()
                    at_least(dve, oT_ps, n - 1)
                    v.tensor_tensor(o[:, n % 2, :].rearrange("p (h d) -> p h d", h=H), o9[:, :, 0:HD],
                                    rec[:, k % 2, :].unsqueeze(2).to_broadcast([P, H, HD]),
                                    ALU.mult).then_inc(o_done, 1)
                t = i - 2
                if 0 <= t < NT:
                    n = base + t
                    dve.wait_ge(w_ps, n + 1)
                    v.scalar_tensor_tensor(out=x[:, t, :], in0=pW[:, 0:D], scalar=tg[:, l:l + 1], in1=x[:, t, :],
                                           op0=ALU.mult, op1=ALU.add).then_inc(w_read, 1)
                    dve.wait_ge(w_read, n + 1)
                    statistics(n + NT)
                if l == 0 and 0 <= i + 4 < NT:
                    normalise(base + i + 4)

            def heads(i):
                if 0 <= i < NT:
                    dve.wait_ge(mulqk, i + 1)
                    v.tensor_reduce(sB[:, i % 2, :], prod[:, i % 2, :].rearrange("p (s d) -> p s d", d=HD),
                                    AX.X, ALU.add).then_inc(redqk, 1)
                if 0 <= i - 1 < NT:
                    dve.wait_ge(sumB, i)
                    v.reciprocal(rec[:, (i - 1) % 2, :], den[:, (i - 1) % 2, :]).then_inc(recB, 1)
                t = i - 2
                if 0 <= t < NT:
                    dve.wait_ge(w_ps, NT + t + 1)
                    dve.wait_ge(yB_done, t + 1)
                    if t > 0:
                        dve.wait_ge(gex_done, t)
                    at_least(dve, h2_done, t - 1)
                    v.tensor_tensor(xp[:, t % 2, :], pW[:, 0:D], yB[:, t, :], ALU.add).then_inc(w_read, 1)
                if 0 <= i < NT:
                    s3 = sB[:, i % 2, :].rearrange("p (h g) -> p h g", h=H)
                    dve.wait_ge(redqk, i + 1)
                    top = steps.mark(v.tensor_reduce(mx[:, i % 2, :], s3, AX.X, ALU.max))
                if 0 <= t < NT:
                    dve.wait_ge(w_read, NT + t + 1)
                    v.scalar_tensor_tensor(out=x[:, t, :], in0=xp[:, t % 2, :], scalar=tg[:, 2:3], in1=x[:, t, :],
                                           op0=ALU.mult, op1=ALU.add).then_inc(xp_done, 1)
                if 0 <= i < NT:
                    steps.wait(top)
                    v.tensor_tensor(s3, s3, mx[:, i % 2, :].unsqueeze(2).to_broadcast([P, H, H]),
                                    ALU.subtract).then_inc(sB_done, 1)
                t = i - 1
                if 0 <= t < NT:
                    n = NT + t
                    dve.wait_ge(mulav, t + 1)
                    dve.wait_ge(mulav_vec, t + 1)
                    v.tensor_reduce(oraw[:, :], prov[:, t % 2, :].rearrange("p (s g) -> p s g", g=H),
                                    AX.X, ALU.add).then_inc(redav, 1)
                    dve.wait_ge(recB, t + 1)
                    if i < NT:
                        dve.wait_ge(eB_done, i + 1)
                        v.tensor_reduce(den[:, i % 2, :], eB[:, i % 2, :].rearrange("p (h g) -> p h g", h=H),
                                        AX.X, ALU.add).then_inc(sumB, 1)
                    dve.wait_ge(redav, t + 1)
                    at_least(dve, oT_ps, n - 1)
                    v.tensor_tensor(o[:, n % 2, :].rearrange("p (h d) -> p h d", h=H),
                                    oraw[:, :].rearrange("p (h d) -> p h d", h=H),
                                    rec[:, t % 2, :].unsqueeze(2).to_broadcast([P, H, HD]),
                                    ALU.mult).then_inc(o_done, 1)
                t = i - 2
                if 0 <= t < NT:
                    dve.wait_ge(gl_ps, t + 1)
                    v.tensor_reduce(gmx[:, t:t + 1], pW[:, 256:256 + E0], AX.X, ALU.max, negate=True).then_inc(gmx_done, 1)
                if 0 <= i < NT:
                    dve.wait_ge(eB_done, i + 1)
                    w = eB[:, i % 2, :].rearrange("p (h g) -> p h g", h=H)
                    val = qkv[:, i % 4, 2 * D:3 * D].rearrange("p (d g) -> p d g", d=HD)
                    if i == 0:
                        v.tensor_reduce(den[:, i % 2, :], w, AX.X, ALU.add).then_inc(sumB, 1)
                    v.tensor_tensor(prov[:, i % 2, :].rearrange("p (h d g) -> p h d g", h=H, d=HD)[:, HP:H],
                                    w[:, HP:H].unsqueeze(2).to_broadcast([P, H - HP, HD, H]),
                                    val.unsqueeze(1).to_broadcast([P, H - HP, HD, H]), ALU.mult).then_inc(mulav_vec, 1)
                t = i - 3
                if 0 <= t < NT:
                    dve.wait_ge(gex_done, t + 1)
                    steps.mark(v.reciprocal(grec[:, t:t + 1], gsum[:, t:t + 1]))
                    dve.wait_ge(moe_ps, t + 1)
                    dve.wait_ge(xp_done, t + 1)
                    steps.wait()
                    v.scalar_tensor_tensor(out=x[:, t, :], in0=pO[:, P:2 * P], scalar=grec[:, t:t + 1], in1=x[:, t, :],
                                           op0=ALU.mult, op1=ALU.add).then_inc(moe_read, 1)
                    dve.wait_ge(moe_read, t + 1)
                    statistics(2 * NT + t)

            def router(i):
                if 0 <= i < NT:
                    dve.wait_ge(proj_ps, 3 * NT + i + 1)
                    v.tensor_reduce(rmx[:, i:i + 1], pS[i % 2][:, 0:E1], AX.X, ALU.max, negate=True).then_inc(rmx_done, 1)
                if 0 <= i + 3 < NT:
                    normalise(3 * NT + i + 3)
                t = i - 1
                if 0 <= t < NT:
                    dve.wait_ge(rex_done, t + 1)
                    steps.mark(v.reciprocal(rrec[:, t:t + 1], rsum[:, t:t + 1]))
                    steps.wait()
                    v.tensor_scalar(rsc[:, t % TB, t // TB, :], rex[:, t % 2, :], rrec[:, t:t + 1], None,
                                    ALU.mult).then_inc(rsc_done, 1)

            setup0()
            dve.wait_ge(ld_x[0], 16)
            statistics(*range(TB))
            dve.wait_ge(ld_b[0], 32)
            dve.wait_ge(setup_ps, 4)
            v.tensor_scalar(kT[0][:, :], pTA[:, 0:B * C], bcol[:, 1:2], None, ALU.add).then_inc(kT_done[0], 1)
            for stage, i in SCHEDULE:
                if (stage, i) == ("A", -2):
                    dve.wait_ge(ld_x[1], 16)
                    statistics(*range(TB, NT))
                    dve.wait_ge(consts, 2)
                    dve.wait_ge(setup_ps, 5)
                    for b in range(B):
                        masked_values(0, b, pS[b][:, 0:D])
                    dve.wait_ge(tg_done, 1)
                if stage == "B" and ahead(1, i - NT - 1):
                    shifted_scores(1, i - NT - 1)
                {"A": lambda i: attention(0, i), "B": heads, "C": lambda i: attention(1, i), "D": router}[stage](i)

            done = [0]

            def hidden(share):
                while done[0] < int(share * dve_units(len(UNITS))):
                    u = 4 * done[0] + 3
                    c, b = UNITS[u]
                    dve.wait_ge(gate_ps, u + 1)
                    dve.wait_ge(silu_done, u + 1)
                    v.scalar_tensor_tensor(out=hidden_values(c, b), in0=pE[b][:, :],
                                           scalar=bug[:, 1, c:c + 1], in1=silu[:, u % 4, :],
                                           op0=ALU.add, op1=ALU.mult).then_inc(hg_dve, 1)
                    done[0] += 1

            dve.wait_ge(rT_done, 1)

            def exchange(src, dst, k, j):
                if j is None:
                    s = src[:, :].rearrange("p (b k) -> p b k", k=k)
                    d = dst[:, :].rearrange("p (b k) -> p b k", k=k)
                    lo, hi = s[:, :, 0:k // 2], s[:, :, k // 2:k]
                    lo_back = s[:, :, k // 2 - 1::-1]
                    hi_back = s[:, :, k - 1:k // 2 - 1:-1]
                    dlo, dhi = d[:, :, 0:k // 2], d[:, :, k // 2:k]
                else:
                    s = src[:, :].rearrange("p (b two j) -> p b two j", two=2, j=j)
                    d = dst[:, :].rearrange("p (b two j) -> p b two j", two=2, j=j)
                    lo, hi = s[:, :, 0, :], s[:, :, 1, :]
                    lo_back, hi_back = lo, hi
                    dlo, dhi = d[:, :, 0, :], d[:, :, 1, :]
                steps.mark(v.tensor_tensor(dlo, lo, hi_back, ALU.max))
                steps.mark(v.tensor_tensor(dhi, hi, lo_back, ALU.min))

            src = rT
            stage_no = 0
            total = len(SORT) + len(MERGE) + 1
            for k, j in SORT:
                exchange(src, sort[stage_no % 2], k, j)
                src = sort[stage_no % 2]
                stage_no += 1
                hidden(stage_no / total)
                steps.wait()
            lo, hi = slice(0, E1), slice(E1, P)
            dst = sort[stage_no % 2]
            steps.mark(v.tensor_copy(other[lo, :], src[hi, :]))
            steps.mark(v.tensor_copy(other[hi, :], src[lo, :]))
            steps.wait()
            steps.mark(v.tensor_tensor(dst[lo, :], src[lo, :], other[lo, ::-1], ALU.max))
            steps.mark(v.tensor_tensor(dst[hi, :], src[hi, :], other[hi, ::-1], ALU.min))
            src = dst
            stage_no += 1
            steps.wait()
            for k, j in MERGE:
                exchange(src, sort[stage_no % 2], k, j)
                src = sort[stage_no % 2]
                stage_no += 1
                hidden(stage_no / total)
                steps.wait()
            groups = src[:, :].rearrange("p (c g) -> p c g", g=G)
            steps.mark(v.tensor_reduce(gs[:, :], groups, AX.X, ALU.add))
            steps.wait()
            v.tensor_tensor(diag, gs[:, :].unsqueeze(2).to_broadcast([P, GH, P]),
                            ident[:, :].unsqueeze(1).to_broadcast([P, GH, P]), ALU.mult).then_inc(pick_vec, 1)
            steps.mark(v.tensor_reduce(gmin[:, :], groups, AX.X, ALU.min))

            count, cand, tie, incl, excl, incl_all, key, pick, big, gsel = (small[:, k, :] for k in range(10))
            dve.wait_ge(allgs_done, 2)
            for c in range(GH):
                if c >= 2:
                    steps.wait(steps.n - 1)
                steps.mark(v.tensor_scalar(junk[:, c % 2, :], allgs[:, :], gs[:, c:c + 1], None, ALU.is_gt, ALU.add,
                                           accum_out=count[:, c:c + 1]))
            steps.wait()
            steps.mark(v.scalar_tensor_tensor(out=cand, in0=count, scalar=float(BUDGET), in1=count,
                                              op0=ALU.is_lt, op1=ALU.mult))
            steps.wait()
            v.tensor_reduce(st2[:, 0:1], cand, AX.X, ALU.max).then_inc(pick_vec, 1)
            dve.wait_ge(pick_ps, 2)
            v.tensor_reduce(lmax[0:1, 0:1], pO[0:1, 0:P], AX.X, ALU.max).then_inc(pick_vec, 1)
            dve.wait_ge(pick_ps, 3)
            steps.mark(v.tensor_scalar(tie, count, pO[:, 256:257], None, ALU.is_equal))
            steps.wait()
            steps.mark(v.tensor_tensor_scan(incl, ones[:, 0:GH], tie, 0.0, ALU.mult, ALU.add))
            steps.wait()
            steps.mark(v.tensor_tensor(excl, incl, tie, ALU.subtract))
            steps.wait()
            v.tensor_copy(incl_all, incl[:, GH - 1:GH].to_broadcast([P, GH])).then_inc(pick_vec, 1)
            dve.wait_ge(pick_ps, 4)
            steps.mark(v.scalar_tensor_tensor(out=key, in0=pW[:, 0:GH], scalar=-1.0, in1=tie, op0=ALU.add, op1=ALU.mult))
            steps.wait()
            steps.mark(v.tensor_tensor(key, key, count, ALU.add))
            steps.wait()
            steps.mark(v.tensor_scalar(pick, key, float(BUDGET), None, ALU.is_lt, ALU.add, accum_out=st2[:, 3:4]))
            steps.wait()
            steps.mark(v.tensor_scalar(big, pick, -2.0, 2.0, ALU.mult, ALU.add))
            steps.wait()
            steps.mark(v.tensor_tensor(gsel, big, gmin[:, :], ALU.max))
            steps.wait()
            v.tensor_reduce(st2[:, 2:3], gsel, AX.X, ALU.min).then_inc(pick_vec, 1)
            dve.wait_ge(pick_ps, 5)
            thr, room, need = st2[:, 6:7], st2[:, 7:8], st2[:, 1:2]
            steps.mark(v.tensor_tensor(thr, pO[:, 0:1], st2[:, 2:3], ALU.min))
            steps.mark(v.tensor_scalar(room, pO[:, 1:2], st2[:, 3:4], float(G), ALU.add, ALU.mult))
            steps.wait()

            steps.mark(v.tensor_scalar(eq[:, :], rT[:, :], thr, None, ALU.is_equal, ALU.add, accum_out=st2[:, 5:6]))
            v.tensor_scalar(gt[:, :], rT[:, :], thr, None, ALU.is_gt, ALU.add, accum_out=st2[:, 4:5]).then_inc(pick_vec, 1)
            steps.wait()
            steps.mark(v.tensor_tensor_scan(cum[:, :], ones[:, :], eq[:, :], 0.0, ALU.mult, ALU.add))
            dve.wait_ge(pick_vec, 6)
            dve.wait_ge(pick_ps, 6)
            steps.mark(v.tensor_scalar(need, pW[:, 0:1], st2[:, 4:5], -1.0, ALU.add, ALU.mult))
            steps.wait()
            steps.mark(v.tensor_tensor(need, need, room, ALU.add))
            steps.wait()
            steps.mark(v.tensor_tensor(room, pW[:, 1:2], high[:, :], ALU.mult))
            steps.wait()
            steps.mark(v.tensor_tensor(need, need, room, ALU.subtract))
            steps.wait()
            steps.mark(v.scalar_tensor_tensor(out=eq[:, :], in0=cum[:, :], scalar=need, in1=eq[:, :],
                                              op0=ALU.is_le, op1=ALU.mult))
            steps.wait()
            steps.mark(v.tensor_tensor(gt[:, :], gt[:, :], eq[:, :], ALU.add))
            steps.wait()
            steps.mark(v.tensor_tensor(fs[:, :], gt[:, :], rT[:, :], ALU.mult))
            steps.wait()
            v.tensor_copy(fsr[:, 0, :], fs[:, :]).then_inc(fs_done, 1)
            dve.wait_ge(fs_done, 1)
            v.tensor_tensor(fsr[:, 1, :], fs[:, :], fsr[:, 0, :].bitcast(F32), ALU.subtract).then_inc(fs_done, 1)

            dve.wait_ge(hg_pool, pool_units(len(UNITS)))
            for u, (c, b) in enumerate(UNITS):
                dve.wait_ge(bc_ps, u + 1)
                part = hidden_values(c, b)
                v.tensor_tensor(part, BC[u % 4][:, :], part, ALU.mult).then_inc(h_done, 1)
                if u == 1:
                    dve.wait_ge(den_ps, 1)
                    steps.mark(v.tensor_scalar(rden[:, :, :], pO[:, 0:2 * TB].rearrange("p (j b) -> p b j", b=2),
                                               1e-6, None, ALU.add))
                    steps.wait()
                    steps.mark(v.reciprocal(scale3[:, :, :], rden[:, :, :]))
                    steps.wait()
                    steps.mark(v.tensor_scalar(rden[:, :, :], scale3[:, :, :], tg[:, 3:4], None, ALU.mult))
            steps.wait()
            for b in range(2):
                dve.wait_ge(res_ps, b + 1)
                for j in range(TB):
                    t = b * TB + j
                    v.scalar_tensor_tensor(out=res[:, t, :], in0=(pTA, pTB)[b][:, j * P:(j + 1) * P],
                                           scalar=rden[:, b, j:j + 1], in1=x[:, t, :],
                                           op0=ALU.mult, op1=ALU.add).then_inc(res_done, 1)


def kernel(**inputs):
    import numpy as _np
    import concourse.bacc as _bacc
    from concourse import mybir as _mybir
    from concourse.bass_utils import run_bass_kernel_spmd as _run

    nc = _bacc.Bacc("TRN2", target_bir_lowering=False, num_devices=1)
    arrays, args = {}, {}
    for name, value in inputs.items():
        arr = _np.ascontiguousarray(value)
        arrays[f"in_{name}"] = arr
        args[name] = nc.dram_tensor(f"in_{name}", arr.shape, _mybir.dt.from_np(arr.dtype), kind="ExternalInput").ap()
    out = nc.dram_tensor("out_0", inputs["x"].shape, _mybir.dt.float32, kind="ExternalOutput").ap()
    gated_layers(nc, args, out)
    r = _run(nc, [arrays], core_ids=[0])
    return r.results[0]["out_0"]
```

```python
from contextlib import ExitStack

import concourse.bass as bass
from concourse import mybir

ALU = mybir.AluOpType
ACT = mybir.ActivationFunctionType
AX = mybir.AxisListType
F32 = mybir.dt.float32
F32R = mybir.dt.float32r
U8 = mybir.dt.uint8


def at_least(eng, sem, value):
    if value > 0:
        eng.wait_ge(sem, value)


class Steps:

    def __init__(self, eng, sem):
        self.eng, self.sem, self.n = eng, sem, 0

    def mark(self, ins):
        ins.then_inc(self.sem, 1)
        self.n += 1
        return self.n

    def wait(self, n=None):
        self.eng.wait_ge(self.sem, self.n if n is None else n)


def gated_layers(nc, a, out):
    B, S, D = a["x"].shape
    C = a["ctx_1024"].shape[1]
    HD = 8
    H = D // HD
    T = B * S
    P = 128
    NT = T // P
    TB = S // P
    L = a["L0_ffn_Wdown"].shape[1]
    E0 = a["L0_ffn_We"].shape[0]
    E1, _, EH = a["L1_ffn_Wup"].shape
    G = 64
    NG = T // G
    BUDGET = NG * 16
    NC = E1 * EH // P
    EC = P // EH
    CH = P // C
    HC = H // CH
    HC9 = HD + 1
    SC = float(HD) ** -0.5
    HALF = T // 2
    GH = HALF // G
    assert P == D and B == 2 and HALF == S == 512 and 2 * E1 == P and H * C == 512

    with ExitStack() as ctx:
        def sb(name, shape, dt=F32):
            return ctx.enter_context(nc.sbuf_tensor(name, shape, dt))

        def bank(name):
            return ctx.enter_context(nc.psum_tensor(name, [P, 512], F32))

        def sem(name):
            return ctx.enter_context(nc.semaphore(name))

        def before(name, shape, dt=F32):
            with nc.sbuf_tensor(name, shape, dt) as tensor:
                return tensor

        x = sb("x_tok", [P, NT, D])
        ctx_in = sb("ctx_in", [B * C, D])
        bcol = sb("bcol", [P, 4])
        gcol = sb("gcol", [P, 4])
        tg = sb("tg", [P, 4])
        brow = before("brow", [P, 8 * D + E0 + E1])
        wd_high0 = sb("wd_high0", [P, 8 * D + E0 + E1], F32R)[:, 0:NC // 2 * D].rearrange("p (c d) -> p c d", d=D)
        maskt = sb("maskt", [P, NT, C], U8)
        fq_in = sb("fq_in", [P, D])
        fdown_in = sb("fdown_in", [P, L])
        fup_in = sb("fup_in", [L, 2 * D])
        bup_row = sb("bup_row", [1, 2 * D])
        bdown_col = sb("bdown_col", [L, 1])
        gam = sb("gam", [P, 2])
        fo = sb("fo", [P, D])
        wg = sb("wg", [P, E0])
        we = before("we", [P, E0, D])
        wd_high1 = sb("wd_high1", [P, NC // 2, D], F32R)
        wr = sb("wr", [P, E1])
        w_up_gate = before("w_up_gate", [P, 2, E1, EH])
        wup, wgate = w_up_gate[:, 0], w_up_gate[:, 1]
        hr = sb("hr", [P, 2, 4, HALF], F32R)
        wdn = sb("wdn", [P, NC, D])
        bdn = sb("bdn", [P, 2, D])
        bug_in = sb("bug_in", [2 * NC, P])
        bug = sb("bug", [P, 2, NC])

        ident = sb("ident", [P, P])
        row0 = sb("row0", [P, P])
        headmask = sb("headmask", [P, H])
        jmask = sb("jmask", [P, CH])
        eps = sb("eps", [P, 3])
        neg = sb("neg", [P, 1])
        ones = sb("ones", [P, 512])
        swap = sb("swap", [P, P])
        samehalf = sb("samehalf", [P, P])
        low2high = sb("low2high", [P, P])
        upto = sb("upto", [P, P])
        high = sb("high", [P, 1])
        sel = sb("sel", [P, 2, NC, P], F32R)
        halfcol = sb("halfcol", [P, 2])
        sel_mark = sb("sel_mark", [P, 2])

        products = before("products", [P, 2, 2, H * H * HD])
        ws = before("ws", [P, NC, 2, 2, P], F32R)
        hg_high = sb("hg_high", [P, NC // 2, T])
        assert 2 * 2 * H * H * HD == NC * 2 * 2 * P == NC // 2 * T
        hg_low = sb("hg_low", [P, NC // 2, T])
        early = hg_low[:, :, :].rearrange("p c t -> p (c t)")

        def hidden_values(c, b):
            return (hg_low, hg_high)[c // (NC // 2)][:, c % (NC // 2), b * HALF:(b + 1) * HALF]

        taken = [0]

        def shared(*dims):
            n = 1
            for d in dims:
                n *= d
            part = early[:, taken[0]:taken[0] + n]
            taken[0] += n
            assert taken[0] <= NC // 2 * T
            names = "abc"[:len(dims)]
            return part.rearrange(f"p ({' '.join(names)}) -> p {' '.join(names)}", **dict(zip(names, dims)))

        ctxT = sb("ctxT", [P, B * C])
        ctx4 = sb("ctx4", [P, B, CH, C])
        wT = [sb(f"wT{l}", [P, 4, D]) for l in (0, 1)]
        kT = [sb(f"kT{l}", [P, B * C]) for l in (0, 1)]
        w_in = [shared(4, D) for _ in (0, 1)]
        kblk = [shared(B, H, C) for _ in (0, 1)]
        vblk = [sb(f"vblk{l}", [P, B, HC, CH, HC9]) for l in (0, 1)]
        wdT = sb("wdT", [L, D])
        wqkv = sb("wqkv", [P, 3 * D])
        bqs = sb("bqs", [P, 2])

        st6 = sb("st6", [P, TB, 6])
        mv = sb("mv", [P, 4 * NT, 2])
        lnv = sb("lnv", [P, 4 * NT])
        rstd = sb("rstd", [P, 4 * NT])
        lnu = sb("lnu", [P, NT])
        ustd = sb("ustd", [P, NT])
        negm, nmr, nmu = [sb(n, [P, NT]) for n in ("negm", "nmr", "nmu")]
        y = sb("y", [P, 2, D])
        yB = shared(NT, D)
        yT = sb("yT", [P, 2, P])
        yTD = before("yTD", [P, T])
        wd_low0 = sb("wd_low0", [P, NC // 2, D], F32R)
        qT = sb("qT", [P, 2, P])
        mx = sb("mx", [P, 2, H])
        e = shared(2, 512)
        eT = shared(2, 512)
        den = sb("den", [P, 2, H])
        rec = sb("rec", [P, 2, H])
        o = sb("o", [P, 2, D])
        oT = sb("oT", [P, 2, D])
        qkv = shared(4, 3 * D)
        prod, prov = products[:, 0], products[:, 1]
        sB = sb("sB", [P, 2, H * H])
        eB = sb("eB", [P, 2, H * H])
        oraw = sb("oraw", [P, D])
        xp = sb("xp", [P, 2, D])
        sq = sb("sq", [P, D])
        ssq = sb("ssq", [P, NT])
        lns = sb("lns", [P, NT])
        rms = sb("rms", [P, NT])
        h2 = sb("h2", [P, 2, D])
        h2T = sb("h2T", [P, P])
        gmx = sb("gmx", [P, NT])
        gex = sb("gex", [P, 2, E0])
        gsum = sb("gsum", [P, NT])
        grec = sb("grec", [P, NT])
        rmx = sb("rmx", [P, NT])
        rex = sb("rex", [P, 2, E1])
        rsum = sb("rsum", [P, NT])
        rrec = sb("rrec", [P, NT])
        rsc = sb("rsc", [P, TB, 2, E1])
        rT = sb("rT", [P, HALF])
        sorts = before("sorts", [P, 2, HALF])
        sort = [sorts[:, i, :] for i in (0, 1)]
        wd_low1 = sb("wd_low1", [P, NC // 2, D], F32R)
        wd = ((wd_high0, wd_high1), (wd_low0, wd_low1))
        gs = sb("gs", [P, GH])
        gmin = sb("gmin", [P, GH])
        xh = before("xh", [P, T], F32R)
        allgs = sb("allgs", [P, 2 * HALF])
        xl = before("xl", [P, T], F32R)
        junk = sb("junk", [P, 2, 2 * HALF], mybir.dt.bfloat16)
        small = sb("small", [P, 16, GH])
        lmax = sb("lmax", [1, 4])
        st2 = sb("st2", [P, 8])
        gt = sb("gt", [P, HALF])
        other = gt
        cum = sb("cum", [P, HALF])
        eq = sb("eq", [P, HALF])
        fs = sb("fs", [P, HALF])
        silu = sb("silu", [P, 4, HALF])
        sel_f32 = silu[:, :, :].rearrange("p a t -> p (a t)")
        gsb = sb("gsb", [P, 3, HALF])
        larger = gsb[:, :, :].rearrange("p a t -> p (a t)").bitcast(mybir.dt.bfloat16).rearrange("p (k t) -> p k t", k=3)
        fsr = sb("fsr", [P, 2, HALF], F32R)
        hgate = allgs[:, :].rearrange("p (e d) -> p e d", e=E0)
        hgateT = gsb[:, 0:2, :].rearrange("p a t -> p (a t)")
        rden = sb("rden", [P, 2, TB])
        scale3 = sb("scale3", [P, 2, TB])
        fT = sb("fT", [P, T])
        diag = fT[:, :].rearrange("p (c q) -> p c q", c=GH)
        res = allgs[:, :].rearrange("p (t d) -> p t d", t=NT)

        pTA, pTB, pS0, pS1, pE0, pE1, pO, pW = [bank(n) for n in ("pTA", "pTB", "pS0", "pS1", "pE0", "pE1", "pO", "pW")]
        pS, pE = (pS0, pS1), (pE0, pE1)
        BC = (pS0, pS1, pTA, pTB)
        RESULT = (pO, pW)

        ld_x = [sem("ld_x0"), sem("ld_x1")]
        ld_ctx = sem("ld_ctx")
        ld_w = [[sem(f"ld_w{l}k"), sem(f"ld_w{l}qvo")] for l in (0, 1)]
        ld_gate = sem("ld_gate")
        ld_b = [sem("ld_b0"), sem("ld_b1")]
        ld_rows = [sem(f"ld_rows{k}") for k in range(3)]
        ld_mask = sem("ld_mask")
        ld_ffn0 = sem("ld_ffn0")
        ld_ffn1 = sem("ld_ffn1")
        ld_up = sem("ld_up")
        ld_bug = sem("ld_bug")
        stored = sem("stored")
        rows_zero = sem("rows_zero")
        eps_set = sem("eps_set")
        bdn_zero = sem("bdn_zero")
        consts = sem("consts")
        sel_made = sem("sel_made")
        sel_done = sem("sel_done")
        pool_steps = sem("pool_steps")
        vec_steps = sem("vec_steps")
        act_steps = sem("act_steps")
        setup_ps = sem("setup_ps")
        tg_done = sem("tg_done")
        wT_done = sem("wT_done")
        kT_done = [sem(f"kT_done{l}") for l in (0, 1)]
        ctx_done = sem("ctx_done")
        wk_done = sem("wk_done")
        part_ps = sem("part_ps")
        part_read = sem("part_read")
        wkv_done = sem("wkv_done")
        vblk_done = sem("vblk_done")
        den_ps = sem("den_ps")
        kblk_done = sem("kblk_done")
        scaled0 = sem("scaled0")
        stats = sem("stats")
        rstd_done = sem("rstd_done")
        y_done = sem("y_done")
        yT_ps = sem("yT_ps")
        yT_done = sem("yT_done")
        q_ps = sem("q_ps")
        q_done = sem("q_done")
        proj_ps = sem("proj_ps")
        e_shift = sem("e_shift")
        e_done = sem("e_done")
        eT_ps = sem("eT_ps")
        eT_done = sem("eT_done")
        o_ps = sem("o_ps")
        o_done = sem("o_done")
        oT_ps = sem("oT_ps")
        oT_done = sem("oT_done")
        w_ps = sem("w_ps")
        w_read = sem("w_read")
        qkv_done = sem("qkv_done")
        mulqk = sem("mulqk")
        redqk = sem("redqk")
        sB_done = sem("sB_done")
        eB_done = sem("eB_done")
        sumB = sem("sumB")
        mulav = sem("mulav")
        mulav_vec = sem("mulav_vec")
        yC_done = sem("yC_done")
        yB_ready = sem("yB_ready")
        yB_done = sem("yB_done")
        xp_done = sem("xp_done")
        w_high = sem("w_high")
        w_low = sem("w_low")
        x_high = sem("x_high")
        x_low = sem("x_low")
        recB = sem("recB")
        hgate_done = [sem(f"hgate_done{j}") for j in range(2)]
        hgT_ps = sem("hgT_ps")
        hgT_done = sem("hgT_done")
        redav = sem("redav")
        h2_done = sem("h2_done")
        h2T_ps = sem("h2T_ps")
        h2T_done = sem("h2T_done")
        gl_ps = sem("gl_ps")
        gmx_done = sem("gmx_done")
        gex_done = sem("gex_done")
        moe_ps = sem("moe_ps")
        moe_read = sem("moe_read")
        rmx_done = sem("rmx_done")
        rex_done = sem("rex_done")
        rsc_done = sem("rsc_done")
        rT_ps = sem("rT_ps")
        rT_done = sem("rT_done")
        up_ps = sem("up_ps")
        gate_ps = sem("gate_ps")
        silu_done = sem("silu_done")
        gsb_done = sem("gsb_done")
        hg_pool = sem("hg_pool")
        rT_low = sem("rT_low")
        compared = sem("compared")
        counted = sem("counted")
        mask_done = sem("mask_done")
        fs_whole = sem("fs_whole")
        pick_vec = sem("pick_vec")
        pick_ps = sem("pick_ps")
        allgs_done = sem("allgs_done")
        fs_done = sem("fs_done")
        bc_ps = sem("bc_ps")
        h_done = sem("h_done")
        wdn_high = sem("wdn_high")
        wdn_low = sem("wdn_low")
        h_high = sem("h_high")
        h_low_pool = sem("h_low_pool")
        h_low_vec = sem("h_low_vec")
        down_used = sem("down_used")
        fT_done = sem("fT_done")
        res_ps = sem("res_ps")
        res_done = sem("res_done")

        BO0, BOF, BO1, BV0, BV1, BQKV = (i * D for i in range(6))
        BG = BQKV + 3 * D
        BR = BG + E0

        SCHEDULE = []
        for stage, first, last, beside in (("A", -4, NT + 1, 0), ("B", -4, NT + 2, 6), ("C", -4, NT + 1, 6), ("D", -3, NT, 6)):
            new = [(stage, i) for i in range(first, last + 1)]
            pairs = 4 if stage == "C" else beside
            old, SCHEDULE = SCHEDULE[len(SCHEDULE) - beside:], SCHEDULE[:len(SCHEDULE) - beside]
            SCHEDULE += [step for pair in zip(old, new[:pairs]) for step in pair] + old[pairs:] + new[pairs:]
        PIECES = 8

        def piece(k):
            which, first, n = k // (PIECES // 2), k % (PIECES // 2) * (2 * NC // PIECES), 2 * NC // PIECES
            src = (wup, wgate)[which][:, first * EC:(first + n) * EC, :].rearrange("p (c j) h -> p c (j h)", c=n)
            return src, ws[:, first:first + n, which, 0, :], ws[:, first:first + n, which, 1, :]

        PARTS = 6

        def ahead(l, t):
            return l == 1 and 0 <= t < 2

        POOL_Y = 3
        GATES_VEC = NT - 2
        HP = 12

        TAIL = [(c, b) for b in range(2) for c in range(NC)]
        UNITS = [(c, b) for c in range(NC) for b in range(2)]

        COUNTED = (0, 1, 2, 3, 4)
        COUNTS = [(c, c in COUNTED) for c in (0, 1, 5, 2, 6, 3, 4, 7)]

        SORT = []
        k = 2
        while k <= HALF:
            SORT.append((k, None))
            j = k // 4
            while j >= 1:
                SORT.append((k, j))
                j //= 2
            k *= 2
        MERGE = [(HALF, HALF // 2), (HALF, HALF // 4), (HALF, HALF // 8)]
        assert MERGE[-1][1] == G

        block = ctx.enter_context(nc.Block())

        @block.sync
        def _(sp):
            def col(name):
                return a[name].rearrange("(n a) -> n a", a=1)

            def row(name):
                return a[name].rearrange("(a n) -> a n", a=1)

            def attention_weight(l, i):
                sp.dma_start(w_in[l][:, i, :], a[f"L{l}_xattn_" + ("Wq", "Wk", "Wv", "Wo")[i]]).then_inc(
                    ld_w[l][int(i != 1)], 16)

            xr = a["x"].rearrange("b (t p) d -> p (b t) d", p=P)
            sp.dma_start(ctx_in[:, :], a["ctx_1024"].rearrange("b s d -> (b s) d")).then_inc(ld_ctx, 16)
            for i in (1, 0):
                attention_weight(0, i)
            sp.dma_start(x[:, 0:TB, :], xr[:, 0:TB, :]).then_inc(ld_x[0], 16)
            attention_weight(0, 2)
            attention_weight(0, 3)
            sp.dma_start(x[:, TB:NT, :], xr[:, TB:NT, :]).then_inc(ld_x[1], 16)
            for i in (1, 2, 0, 3):
                attention_weight(1, i)
            sp.dma_start(bcol[:, 2:3], col("L1_xattn_bq")).then_inc(ld_b[1], 16)
            sp.dma_start(bcol[:, 3:4], col("L1_xattn_bk")).then_inc(ld_b[1], 16)
            sp.wait_ge(rows_zero, 1)
            sp.dma_start(brow[0:1, BV1:BV1 + D], row("L1_xattn_bv")).then_inc(ld_rows[1], 16)
            sp.dma_start(fdown_in[:, :], a["L0_ffn_Wdown"]).then_inc(ld_ffn0, 16)
            sp.dma_start(fup_in[:, :], a["L0_ffn_Wup"]).then_inc(ld_ffn0, 16)
            sp.dma_start(bup_row[:, :], row("L0_ffn_bup")).then_inc(ld_ffn0, 16)
            sp.dma_start(bdown_col[:, :], col("L0_ffn_bdown")).then_inc(ld_ffn0, 16)
            for i in range(2):
                sp.dma_start(gam[:, i:i + 1], col(f"L0_ffn_gamma{i + 1}")).then_inc(ld_ffn0, 16)
            sp.dma_start(fq_in[:, :], a["L0_ffn_Wq"]).then_inc(ld_ffn0, 16)
            sp.dma_start(fo[:, :], a["L0_ffn_Wo"]).then_inc(ld_ffn0, 16)
            sp.dma_start(wg[:, :], a["L0_ffn_Wg"]).then_inc(ld_ffn0, 16)
            sp.dma_start(we[:, :, :], a["L0_ffn_We"].rearrange("e d f -> d e f")).then_inc(ld_ffn0, 16)
            for i, w in enumerate(("bup", "bgate")):
                sp.dma_start(bug_in[i * NC:(i + 1) * NC, :],
                             a["L1_ffn_" + w].rearrange("(c j) h -> c (j h)", j=EC)).then_inc(ld_bug, 16)
            for name, at, n in (("L0_ffn_bq", BQKV, D), ("L0_ffn_bo", BOF, D), ("L0_ffn_bg", BG, E0),
                                ("L1_xattn_bo", BO1, D), ("L1_ffn_br", BR, E1)):
                sp.dma_start(brow[0:1, at:at + n], row(name)).then_inc(ld_rows[2], 16)
            mr = a["mask_Bx1xSxS2_bk1"].rearrange("b o (t p) c -> p (b o t) c", p=P)
            sp.dma_start(maskt[:, :, :], mr).then_inc(ld_mask, 16)
            sp.dma_start(wr[:, :], a["L1_ffn_Wr"]).then_inc(ld_ffn1, 16)
            sp.dma_start(wup[:, :, :], a["L1_ffn_Wup"].rearrange("e d h -> d e h")).then_inc(ld_up, 16)
            sp.dma_start(wgate[:, :, :], a["L1_ffn_Wgate"].rearrange("e d h -> d e h")).then_inc(ld_up, 16)
            sp.dma_start(wdn[:, :, :], a["L1_ffn_Wdown"].rearrange("(c j) h d -> (j h) c d", j=EC)).then_inc(ld_up, 16)
            sp.wait_ge(bdn_zero, 2)
            for b in range(2):
                sp.dma_start(bdn[b * E1:(b + 1) * E1, b, :], a["L1_ffn_bdown"]).then_inc(ld_up, 16)
            orr = out.rearrange("b (t p) d -> p (b t) d", p=P)
            for b in range(2):
                sp.wait_ge(res_done, TB * (b + 1))
                sp.dma_start(orr[:, b * TB:(b + 1) * TB, :], res[:, b * TB:(b + 1) * TB, :]).then_inc(stored, 16)
            sp.wait_ge(stored, 32)

        @block.gpsimd
        def _(pool):
            steps = Steps(pool, pool_steps)

            def mask_from(tile, value, *selects):
                steps.mark(nc.gpsimd.memset(tile, value))
                for op, fill, base, pattern, mult in selects:
                    steps.wait()
                    steps.mark(nc.gpsimd.affine_select(out=tile, in_=tile, compare_op=op, fill=fill, base=base,
                                                       pattern=pattern, channel_multiplier=mult))

            mask_from(ident[:, :], 0.0, (ALU.not_equal, 1.0, 0, [[-1, P]], 1))
            steps.wait()
            nc.gpsimd.memset(neg[:, :], -1e9).then_inc(consts, 1)
            mask_from(row0[:, :], 0.0, (ALU.not_equal, 1.0, 0, [[0, P]], 1))
            mask_from(jmask[:, :], 1.0, (ALU.is_ge, 0.0, 0, [[-C, CH]], 1),
                      (ALU.is_ge, 0.0, C - 1, [[C, CH]], -1))
            mask_from(headmask[:, :], 1.0, (ALU.is_ge, 0.0, 0, [[-HD, H]], 1),
                      (ALU.is_ge, 0.0, HD - 1, [[HD, H]], -1))
            steps.wait()
            nc.gpsimd.memset(ones[:, :], 1.0).then_inc(consts, 1)

            def block_keys(l):
                pool.wait_ge(kT_done[l], 1)
                for b in range(B):
                    nc.gpsimd.tensor_tensor(
                        kblk[l][:, b, :, :],
                        kT[l][:, b * C:(b + 1) * C].unsqueeze(1).to_broadcast([P, H, C]),
                        headmask[:, :].unsqueeze(2).to_broadcast([P, H, C]), ALU.mult).then_inc(kblk_done, 1)

            block_keys(0)
            pool.wait_ge(ld_ffn0, 16 * 10)
            nc.gpsimd.tensor_scalar(wqkv[:, 0:D], fq_in[:, :], gam[:, 0:1], None, ALU.mult).then_inc(scaled0, 1)
            nc.gpsimd.tensor_scalar(wg[:, :], wg[:, :], gam[:, 1:2], None, ALU.mult).then_inc(scaled0, 1)
            we2 = we[:, :, :].rearrange("p e f -> p (e f)")
            pool.wait_ge(tg_done, 1)
            nc.gpsimd.tensor_scalar(we2, we2, gam[:, 1:2], tg[:, 2:3], ALU.mult, ALU.mult).then_inc(scaled0, 1)

            mask_from(swap[:, :], 0.0, (ALU.not_equal, 1.0, E1, [[-1, P]], 1), (ALU.not_equal, 1.0, -E1, [[-1, P]], 1))
            mask_from(samehalf[:, :].rearrange("p (b e) -> p b e", b=2), 1.0,
                      (ALU.is_ge, 0.0, 0, [[-E1, 2], [0, E1]], 1), (ALU.is_ge, 0.0, E1 - 1, [[E1, 2], [0, E1]], -1))
            mask_from(low2high[:, :].rearrange("p (b e) -> p b e", b=2), 1.0,
                      (ALU.is_ge, 0.0, E1 - 1, [[0, 2], [0, E1]], -1), (ALU.is_ge, 0.0, -1, [[1, 2], [0, E1]], 0))
            mask_from(upto[:, :], 1.0, (ALU.is_ge, 0.0, 0, [[1, P]], -1))
            steps.wait()
            steps.mark(nc.gpsimd.tensor_tensor(upto[:, :], upto[:, :], samehalf[:, :], ALU.mult))
            steps.wait()
            steps.mark(nc.gpsimd.tensor_tensor(upto[:, :], upto[:, :], samehalf[:, :], ALU.subtract))
            mask_from(high[:, :], 1.0, (ALU.is_ge, 0.0, -E1, [[0, 1]], 1))
            mask_from(halfcol[:, :], 1.0, (ALU.is_ge, 0.0, 0, [[-E1, 2]], 1), (ALU.is_ge, 0.0, E1 - 1, [[E1, 2]], -1))
            block_keys(1)

            def mul_qk(t):
                pool.wait_ge(qkv_done, t + 1)
                at_least(pool, redqk, t - 1)
                q = qkv[:, t % 4, 0:D].rearrange("p (h d) -> p h d", h=H)
                k = qkv[:, t % 4, D:2 * D].rearrange("p (h d) -> p h d", h=H)
                nc.gpsimd.tensor_tensor(prod[:, t % 2, :].rearrange("p (h g d) -> p h g d", h=H, g=H),
                                        q.unsqueeze(2).to_broadcast([P, H, H, HD]),
                                        k.unsqueeze(1).to_broadcast([P, H, H, HD]), ALU.mult).then_inc(mulqk, 1)

            def mul_av(t):
                pool.wait_ge(eB_done, t + 1)
                at_least(pool, redav, t - 1)
                w = eB[:, t % 2, :].rearrange("p (h g) -> p h g", h=H)
                v = qkv[:, t % 4, 2 * D:3 * D].rearrange("p (d g) -> p d g", d=HD)
                nc.gpsimd.tensor_tensor(prov[:, t % 2, :].rearrange("p (h d g) -> p h d g", h=H, d=HD)[:, 0:HP],
                                        w[:, 0:HP].unsqueeze(2).to_broadcast([P, HP, HD, H]),
                                        v.unsqueeze(1).to_broadcast([P, HP, HD, H]), ALU.mult).then_inc(mulav, 1)

            def normalise_b(t):
                n = NT + t
                pool.wait_ge(rstd_done, n + 1)
                pool.wait_ge(yT_ps, n - 1)
                for dst, std, done in ((y[:, n % 2, :], ustd[:, t:t + 1], yB_ready), (yB[:, t, :], rstd[:, n:n + 1], yB_done)):
                    nc.gpsimd.tensor_scalar(dst, x[:, t, :], mv[:, n, 0:1], std, ALU.subtract, ALU.mult).then_inc(done, 1)

            def weight_low(k):
                pool.wait_ge(w_high, k + 1)
                src, high, low = piece(k)
                nc.gpsimd.tensor_tensor(low, src, high.bitcast(F32), ALU.subtract).then_inc(w_low, 1)

            def normalise_c(t):
                n = 2 * NT + t
                pool.wait_ge(rstd_done, n + 1)
                pool.wait_ge(yT_ps, n - 1)
                nc.gpsimd.tensor_scalar(y[:, n % 2, :], x[:, t, :], mv[:, n, 0:1], rstd[:, n:n + 1],
                                        ALU.subtract, ALU.mult).then_inc(yC_done, 1)

            for t in range(POOL_Y):
                normalise_b(t)
            for t in range(NT + 1):
                if t < NT:
                    mul_qk(t)
                if t >= 1:
                    mul_av(t - 1)
                if t >= NT - 2:
                    normalise_c(t - NT + 2)
            for t in range(3, NT):
                normalise_c(t)
                k = t - 3
                weight_low(k)
            for k in range(NT - 3, PIECES):
                weight_low(k)

            for t in range(NT):
                pool.wait_ge(x_high, t + 1)
                pool.wait_ge(yT_done, 3 * NT + t + 1)
                cols = slice(t * P, (t + 1) * P)
                nc.gpsimd.tensor_tensor(xl[:, cols], yTD[:, cols], xh[:, cols].bitcast(F32), ALU.subtract).then_inc(x_low, 1)

            pool.wait_ge(rT_done, 2)
            nc.gpsimd.tensor_tensor(fsr[:, 1, :], rT[:, :], fsr[:, 0, :].bitcast(F32), ALU.subtract).then_inc(rT_low, 1)

            for u, (c, b) in enumerate(UNITS):
                pool.wait_ge(gsb_done, u + 1)
                if u == 0:
                    pool.wait_ge(rT_ps, 1)
                nc.gpsimd.tensor_tensor(hidden_values(c, b), gsb[:, u % 3, :], silu[:, u % 4, :],
                                        ALU.mult).then_inc(hg_pool, 1)

            pool.wait_ge(hg_pool, len(UNITS))
            for b in range(2):
                at_least(pool, sel_done, b)
                mask_from(sel_f32.rearrange("p (c j h) -> p c j h", c=NC, j=EC), 0.0,
                          (ALU.not_equal, 1.0, -b * E1, [[-EC, NC], [-1, EC], [0, EH]], 1))
                steps.wait()
                nc.gpsimd.memset(sel_mark[:, b:b + 1], 0.0).then_inc(sel_made, 1)

            for k in range(2):
                pool.wait_ge(wdn_high, k + 1)
                nc.gpsimd.tensor_tensor(wd[1][k][:, :, :], wdn[:, k * NC // 2:(k + 1) * NC // 2, :],
                                        wd[0][k][:, :, :].bitcast(F32), ALU.subtract).then_inc(wdn_low, 1)
            pool.wait_ge(mask_done, 1)
            nc.gpsimd.tensor_tensor(fs[:, :], gt[:, :], rT[:, :], ALU.mult).then_inc(fs_whole, 1)
            for u in range(0, len(TAIL), 2):
                c, b = TAIL[u]
                pool.wait_ge(h_high, u + 1)
                nc.gpsimd.tensor_tensor(hr[:, 1, u % 4, :], hidden_values(c, b), hr[:, 0, u % 4, :].bitcast(F32),
                                        ALU.subtract).then_inc(h_low_pool, 1)

        @block.scalar
        def _(act):
            steps = Steps(act, act_steps)

            def col(name):
                return a[name].rearrange("(n a) -> n a", a=1)

            for i, g in enumerate(("g_xattn", "g_ffn")):
                act.dma_start(gcol[:, 2 * i:2 * i + 2], a[g].partition_broadcast(P)).then_inc(ld_gate, 16)
            nc.scalar.preload_act_table_set("exp_and_others")
            act.dma_start(bcol[:, 1:2], col("L0_xattn_bk")).then_inc(ld_b[0], 16)
            act.dma_start(bcol[:, 0:1], col("L0_xattn_bq")).then_inc(ld_b[0], 16)
            act.wait_ge(rows_zero, 1)
            for name, at in (("L0_xattn_bv", BV0), ("L0_xattn_bo", BO0)):
                act.dma_start(brow[0:1, at:at + D], a[name].rearrange("(a n) -> a n", a=1)).then_inc(ld_rows[0], 16)
            act.wait_ge(ld_gate, 32)
            nc.scalar.activation(tg[:, :], gcol[:, :], ACT.Tanh).then_inc(tg_done, 1)
            nc.scalar.preload_act_table_set("natural_log_exp_and_others")

            def setup0():
                act.wait_ge(setup_ps, 3)
                nc.scalar.activation(wT[0][:, 0, :], pE[0][:, 0:D], ACT.Copy).then_inc(wT_done, 1)
                nc.scalar.activation(wT[0][:, 2:4, :].rearrange("p i n -> p (i n)"), pE[0][:, D:3 * D],
                                     ACT.Copy).then_inc(wT_done, 1)
                act.wait_ge(ld_b[0], 32)
                steps.mark(nc.scalar.mul(bqs[:, 0:1], bcol[:, 0:1], SC))
                steps.wait()

            def weights_ready(k):
                if k in (0, 1, 2, 4):
                    act.wait_ge(part_ps, k + 1)
                if k == 0:
                    nc.scalar.activation(wT[1][:, 0:3, :].rearrange("p i n -> p (i n)"), pTB[:, P:P + 3 * D],
                                         ACT.Copy).then_inc(part_read, 1)
                elif k == 1:
                    steps.mark(nc.scalar.activation(wT[1][:, 3, :], pTB[:, P:2 * P], ACT.Copy))
                    nc.scalar.activation(bug[:, :, :].rearrange("p i c -> p (i c)"), pTB[:, 2 * P:2 * P + 2 * NC],
                                         ACT.Copy).then_inc(part_read, 1)
                    act.wait_ge(ld_b[1], 32)
                    steps.mark(nc.scalar.mul(bqs[:, 1:2], bcol[:, 2:3], SC))
                elif k == 2:
                    nc.scalar.activation(kT[1][:, :], pTB[:, P:P + B * C], ACT.Identity, bias=bcol[:, 3:4]).then_inc(kT_done[1], 1)
                    nc.scalar.activation(wdT[:, :], pTB[0:L, 2 * P:2 * P + D], ACT.Copy).then_inc(part_read, 1)
                elif k == 4:
                    kv = pTB[:, P:P + 2 * D].rearrange("p (g k d) -> p k g d", g=H, k=2)
                    nc.scalar.activation(wqkv[:, D:2 * D].rearrange("p (g d) -> p g d", g=H), kv[:, 0], ACT.Copy,
                                         scale=gam[:, 0:1]).then_inc(wkv_done, 1)
                    nc.scalar.activation(wqkv[:, 2 * D:3 * D].rearrange("p (d g) -> p g d", g=H), kv[:, 1], ACT.Copy,
                                         scale=gam[:, 0:1]).then_inc(part_read, 1)

            std_step = {}

            def rstd_of(n):
                act.wait_ge(stats, n + 1)
                k = steps.mark(nc.scalar.activation(lnv[:, n:n + 1], mv[:, n, 1:2], ACT.Ln, bias=eps[:, 0:1]))
                if NT <= n < 2 * NT:
                    t = n - NT
                    k2 = steps.mark(nc.scalar.activation(lnu[:, t:t + 1], mv[:, n, 1:2], ACT.Ln,
                                                         bias=eps[:, 1:2], scale=1.0 + 1e-6))
                    steps.wait(k)
                    std_step[t] = steps.mark(nc.scalar.activation(rstd[:, n:n + 1], lnv[:, n:n + 1], ACT.Exp, scale=-0.5))
                    steps.wait(std_step[t] if t < POOL_Y else k2)
                    nc.scalar.activation(ustd[:, t:t + 1], lnu[:, t:t + 1], ACT.Exp, scale=-0.5).then_inc(rstd_done, 1)
                else:
                    steps.wait(k)
                    nc.scalar.activation(rstd[:, n:n + 1], lnv[:, n:n + 1], ACT.Exp, scale=-0.5).then_inc(rstd_done, 1)

            def copy_yT(n):
                act.wait_ge(yT_ps, n + 1)
                if n < 3 * NT:
                    m = n - 2
                    if m >= 0:
                        if NT <= m < 2 * NT:
                            act.wait_ge(proj_ps, m + 1)
                        else:
                            act.wait_ge(q_ps, (m if m < NT else m - NT) + 1)
                    dst = yT[:, n % 2, :]
                else:
                    dst = yTD[:, (n - 3 * NT) * P:(n - 3 * NT + 1) * P]
                nc.scalar.activation(dst, pTA[:, 0:P], ACT.Copy).then_inc(yT_done, 1)
                if n >= 3 * NT:
                    t = n - 3 * NT
                    nc.scalar.activation(xh[:, t * P:(t + 1) * P], pTA[:, 0:P], ACT.Copy).then_inc(x_high, 1)

            def copy_oT(n):
                act.wait_ge(oT_ps, n + 1)
                at_least(act, w_ps, n - 1)
                nc.scalar.activation(oT[:, n % 2, :], pTB[:, 0:P], ACT.Copy).then_inc(oT_done, 1)

            def exponentials(k):
                act.wait_ge(e_shift, k + 1)
                nc.scalar.activation(e[:, k % 2, :], e[:, k % 2, :], ACT.Exp).then_inc(e_done, 1)

            def attention(l, i):
                base, k0 = 2 * l * NT, l * NT
                if 0 <= i < NT and not ahead(l, i):
                    exponentials(k0 + i)
                if l == 0 and 1 <= i <= PARTS:
                    weights_ready(i - 1)
                t = i + 2
                if 0 <= t < NT:
                    n, k = base + t, k0 + t
                    act.wait_ge(q_ps, k + 1)
                    at_least(act, proj_ps, n - 1)
                    nc.scalar.activation(qT[:, k % 2, :], pTA[:, 256:256 + P], ACT.Identity,
                                         bias=bqs[:, l:l + 1], scale=SC).then_inc(q_done, 1)
                t = i
                if 0 <= t < NT:
                    k = k0 + t
                    act.wait_ge(eT_ps, k + 1)
                    at_least(act, o_ps, k - 1)
                    nc.scalar.activation(eT[:, k % 2, :], pE[k % 2][:, :], ACT.Copy).then_inc(eT_done, 1)
                if 0 <= i + 3 < NT:
                    copy_yT(base + i + 3)
                if 0 <= i - 1 < NT:
                    copy_oT(base + i - 1)
                if 0 <= i - 2 < NT:
                    rstd_of(base + NT + i - 2)
                if l == 1 and 0 <= i < PIECES:
                    if i == 0:
                        act.wait_ge(ld_up, 16 * 5)
                        act.wait_ge(redav, NT)
                    src, high, _ = piece(i)
                    nc.scalar.activation(high, src, ACT.Copy).then_inc(w_high, 1)

            def normalise(t):
                act.wait_ge(rstd_done, NT + t + 1)
                k = steps.mark(nc.scalar.activation(nmu[:, t:t + 1], ustd[:, t:t + 1], ACT.Copy, scale=negm[:, t:t + 1]))
                steps.wait(std_step[t])
                steps.mark(nc.scalar.activation(nmr[:, t:t + 1], rstd[:, NT + t:NT + t + 1], ACT.Copy, scale=negm[:, t:t + 1]))
                steps.wait(k)
                at_least(act, yT_ps, NT + t - 1)
                if t == POOL_Y:
                    act.wait_ge(yB_ready, t)
                    act.wait_ge(yB_done, t)
                nc.scalar.activation(y[:, t % 2, :], x[:, t, :], ACT.Identity, bias=nmu[:, t:t + 1],
                                     scale=ustd[:, t:t + 1]).then_inc(yB_ready, 1)
                steps.wait(k + 1)
                nc.scalar.activation(yB[:, t, :], x[:, t, :], ACT.Identity, bias=nmr[:, t:t + 1],
                                     scale=rstd[:, NT + t:NT + t + 1]).then_inc(yB_done, 1)

            def heads(i):
                if 0 <= i + 2 < NT:
                    copy_yT(NT + i + 2)
                t = i - 3
                if 0 <= t < NT:
                    for j in range(2):
                        act.wait_ge(hgT_ps, 2 * t + j + 1)
                        at_least(act, moe_ps, t)
                        nc.scalar.activation(hgateT[:, j * 512:(j + 1) * 512], pE[j][:, :], ACT.Copy).then_inc(hgT_done, 1)
                if 0 <= i < NT:
                    act.wait_ge(sB_done, i + 1)
                    at_least(act, mulav, i - 1)
                    at_least(act, mulav_vec, i - 1)
                    at_least(act, sumB, i - 1)
                    nc.scalar.activation(eB[:, i % 2, :], sB[:, i % 2, :], ACT.Exp, scale=SC).then_inc(eB_done, 1)
                t = i - 2
                if 0 <= t < NT:
                    act.wait_ge(w_read, NT + t + 1)
                    steps.mark(nc.scalar.activation(sq[:, :], xp[:, t % 2, :], ACT.Square, accum_out=ssq[:, t:t + 1]))
                    steps.wait()
                    steps.mark(nc.scalar.activation(lns[:, t:t + 1], ssq[:, t:t + 1], ACT.Ln, bias=eps[:, 2:3], scale=1.0 / D))
                    steps.wait()
                    steps.mark(nc.scalar.activation(rms[:, t:t + 1], lns[:, t:t + 1], ACT.Exp, scale=-0.5))
                    steps.wait()
                    at_least(act, h2T_ps, t - 1)
                    nc.scalar.activation(h2[:, t % 2, :], xp[:, t % 2, :], ACT.Copy, scale=rms[:, t:t + 1]).then_inc(h2_done, 1)
                if 0 <= t < NT:
                    act.wait_ge(h2T_ps, t + 1)
                    at_least(act, gl_ps, t)
                    nc.scalar.activation(h2T[:, :], pTB[:, P:2 * P], ACT.Copy).then_inc(h2T_done, 1)
                if 0 <= i + 2 < NT:
                    act.wait_ge(proj_ps, NT + i + 2 + 1)
                    at_least(act, mulav, i - 1)
                    at_least(act, mulav_vec, i - 1)
                    nc.scalar.activation(qkv[:, (i + 2) % 4, :], pS[i % 2][:, 0:3 * D], ACT.Copy).then_inc(qkv_done, 1)
                if POOL_Y <= i + 4 < NT:
                    normalise(i + 4)
                if 0 <= i - 1 < NT:
                    copy_oT(NT + i - 1)
                if 0 <= t < NT:
                    act.wait_ge(gmx_done, t + 1)
                    nc.scalar.activation(gex[:, t % 2, :], pW[:, 256:256 + E0], ACT.Exp, bias=gmx[:, t:t + 1],
                                         accum_out=gsum[:, t:t + 1]).then_inc(gex_done, 1)
                    act.wait_ge(gex_done, t + 1)
                    at_least(act, hgT_ps, 2 * t)
                    for k in range(E0 if t < GATES_VEC else E0 // 2):
                        ins = nc.scalar.activation(hgate[:, k, :], h2[:, t % 2, :], ACT.Copy, scale=gex[:, t % 2, k:k + 1])
                        if k % (E0 // 2) == E0 // 2 - 1:
                            ins.then_inc(hgate_done[k // (E0 // 2)], 1)
                if 0 <= i - 3 < NT:
                    rstd_of(2 * NT + i - 3)

            def router(i):
                if 0 <= i + 2 < NT:
                    copy_yT(3 * NT + i + 2)
                if 0 <= i < NT:
                    act.wait_ge(rmx_done, i + 1)
                    at_least(act, rsc_done, i - 1)
                    nc.scalar.activation(rex[:, i % 2, :], pS[i % 2][:, 0:E1], ACT.Exp, bias=rmx[:, i:i + 1],
                                         accum_out=rsum[:, i:i + 1]).then_inc(rex_done, 1)

            for stage, i in SCHEDULE:
                if (stage, i) == ("A", -4):
                    act.wait_ge(eps_set, 3)
                    rstd_of(0)
                    setup0()
                    for n in range(1, TB):
                        rstd_of(n)
                if (stage, i) == ("A", -1):
                    for n in range(TB, NT):
                        rstd_of(n)
                if stage == "B" and ahead(1, i - NT - 1):
                    exponentials(i - 1)
                {"A": lambda i: attention(0, i), "B": heads, "C": lambda i: attention(1, i), "D": router}[stage](i)

            act.wait_ge(rT_ps, 1)
            nc.scalar.activation(rT[:, :], pTB[:, :], ACT.Copy).then_inc(rT_done, 1)
            nc.scalar.activation(fsr[:, 0, :], pTB[:, :], ACT.Copy).then_inc(rT_done, 1)
            for u, (c, b) in enumerate(UNITS):
                act.wait_ge(up_ps, u + 1)
                if u >= 4:
                    act.wait_ge(hg_pool, u - 3)
                nc.scalar.activation(silu[:, u % 4, :], pS[b][:, :], ACT.Silu, bias=bug[:, 0, c:c + 1]).then_inc(silu_done, 1)
                act.wait_ge(gate_ps, u + 1)
                at_least(act, hg_pool, u - 2)
                nc.scalar.activation(gsb[:, u % 3, :], pE[b][:, :], ACT.Identity, bias=bug[:, 1, c:c + 1]).then_inc(gsb_done, 1)
            act.wait_ge(pick_ps, 1)
            for b in range(2):
                nc.scalar.activation(allgs[:, b * HALF:(b + 1) * HALF], (pTA, pTB)[b][:, :], ACT.Copy).then_inc(allgs_done, 1)
            for k, c in enumerate(COUNTED):
                act.wait_ge(compared, k + 1)
                at_least(act, counted, k)
                nc.scalar.activation(junk[:, 1, :], larger[:, k % 3, :], ACT.Copy,
                                     accum_out=small[:, 0, c:c + 1]).then_inc(counted, 1)
            act.wait_ge(pick_vec, 1)
            for k in range(2):
                nc.scalar.activation(wd[0][k][:, :, :], wdn[:, k * NC // 2:(k + 1) * NC // 2, :], ACT.Copy).then_inc(wdn_high, 1)
            for b in range(2):
                act.wait_ge(sel_made, b + 1)
                nc.scalar.activation(sel[:, b, :, :].rearrange("p c q -> p (c q)"), sel_f32, ACT.Copy).then_inc(sel_done, 1)
            def transposed_result(b):
                act.wait_ge(down_used, NC * (b + 1))
                nc.scalar.activation(fT[:, b * HALF:(b + 1) * HALF], pE[b][:, :], ACT.Copy).then_inc(fT_done, 1)

            for u, (c, b) in enumerate(TAIL):
                act.wait_ge(h_done, u + 1)
                at_least(act, down_used, u - 3)
                nc.scalar.activation(hr[:, 0, u % 4, :], hidden_values(c, b), ACT.Copy).then_inc(h_high, 1)
                if u == NC + 5:
                    transposed_result(0)
            transposed_result(1)

        @block.tensor
        def _(pe):
            mm = nc.tensor.matmul
            transpose = nc.tensor.transpose

            def bias(dst, row):
                mm(dst, row0[:, :], row, start=True, stop=False)

            def values(l, b, dst):
                at = (BV0, BV1)[l]
                bias(dst, brow[:, at:at + D])
                return mm(dst, ctx4[:, b, :, :].rearrange("p j k -> p (j k)"), wT[l][:, 2, :], start=False, stop=True)

            pe.wait_ge(consts, 1)
            pe.wait_ge(ld_ctx, 16)
            transpose(pO[:, 0:B * C], ctx_in[:, :], ident[0:B * C, 0:B * C]).then_inc(setup_ps, 1)
            pe.wait_ge(ld_w[0][0], 16)
            transpose(pE1[:, 0:D], w_in[0][:, 1, :], ident[:, :]).then_inc(setup_ps, 1)
            pe.wait_ge(ctx_done, 2)
            pe.wait_ge(wk_done, 1)
            pe.wait_ge(ld_w[0][1], 48)
            for k, i in enumerate((0, 2, 3)):
                m = transpose(pE0[:, k * D:(k + 1) * D], w_in[0][:, i, :], ident[:, :])
            m.then_inc(setup_ps, 1)
            mm(pTA[:, 0:B * C], wT[0][:, 1, :], ctxT[:, :]).then_inc(setup_ps, 1)

            def values0():
                pe.wait_ge(ld_rows[0], 32)
                pe.wait_ge(consts, 2)
                pe.wait_ge(wT_done, 2)
                values(0, 0, pW[:, 0:D])
                values(0, 1, pW[:, D:2 * D]).then_inc(setup_ps, 1)

            def weights_ready(k):
                if k == 0:
                    pe.wait_ge(ld_w[1][0], 16)
                    pe.wait_ge(ld_w[1][1], 48)
                    for i in range(3):
                        m = transpose(pTB[:, P + i * D:P + (i + 1) * D], w_in[1][:, i, :], ident[:, :])
                elif k == 1:
                    pe.wait_ge(ld_bug, 32)
                    transpose(pTB[:, P:2 * P], w_in[1][:, 3, :], ident[:, :])
                    m = transpose(pTB[:, 2 * P:2 * P + 2 * NC], bug_in[:, :], ident[0:2 * NC, 0:2 * NC])
                elif k == 2:
                    pe.wait_ge(ld_ffn0, 16 * 10)
                    mm(pTB[:, P:P + B * C], wT[1][:, 1, :], ctxT[:, :])
                    m = transpose(pTB[0:L, 2 * P:2 * P + D], fdown_in[:, :], ident[:, :])
                elif k == 3:
                    pe.wait_ge(ld_rows[1], 16)
                    values(1, 0, pTB[:, P:P + D])
                    m = values(1, 1, pTB[:, P + D:P + 2 * D])
                elif k == 4:
                    m = mm(pTB[:, P:P + 2 * D], wdT[:, :], fup_in[:, :])
                elif k == 5:
                    m = mm(pTB[0:1, P:P + 2 * D], bdown_col[:, :], fup_in[:, :])
                m.then_inc(part_ps, 1)

            def queries_before(n):
                return min(n, NT) + min(max(n - 2 * NT, 0), NT)

            def transpose_y(n):
                if NT <= n < 2 * NT:
                    pe.wait_ge(yB_ready, n - NT + 1)
                elif 2 * NT <= n < 3 * NT:
                    pe.wait_ge(yC_done, n - 2 * NT + 1)
                else:
                    pe.wait_ge(y_done, (n if n < NT else n - 2 * NT) + 1)
                if n == 0:
                    pe.wait_ge(kT_done[0], 1)
                at_least(pe, yT_done, n)
                at_least(pe, x_high, n - 3 * NT)
                at_least(pe, q_done, queries_before(n))
                transpose(pTA[:, 0:P], y[:, n % 2, :], ident[:, :]).then_inc(yT_ps, 1)

            def transpose_o(n):
                pe.wait_ge(o_done, n + 1)
                at_least(pe, oT_done, n)
                at_least(pe, part_read, min(n + 1, PARTS))
                transpose(pTB[:, 0:P], o[:, n % 2, :], ident[:, :]).then_inc(oT_ps, 1)

            def project_o(n, w, bo):
                at_least(pe, w_read, n)
                if NT < n < 2 * NT:
                    pe.wait_ge(gex_done, n - NT)
                elif n >= 2 * NT:
                    pe.wait_ge(gex_done, NT)
                bias(pW[:, 0:D], bo)
                pe.wait_ge(oT_done, n + 1)
                mm(pW[:, 0:D], oT[:, n % 2, :], w, start=False, stop=True).then_inc(w_ps, 1)

            def scores_bank_free(n):
                if n < 2:
                    return
                st, t = divmod(n - 2, NT)
                pe.wait_ge(*((e_shift, t + 1), (qkv_done, t + 1), (e_shift, NT + t + 1), (rex_done, t + 1))[st])

            def attention(l, i):
                base, k0 = 2 * l * NT, l * NT
                t = i
                if 0 <= t < NT:
                    k = k0 + t
                    pe.wait_ge(e_done, k + 1)
                    at_least(pe, eT_done, k - 1)
                    if l == 1 and t < 2:
                        pe.wait_ge(hgT_done, 2 * NT)
                    for c in range(HC):
                        m = transpose(pE[k % 2][:, c * P:(c + 1) * P], e[:, k % 2, c * P:(c + 1) * P], ident[:, :])
                    m.then_inc(eT_ps, 1)
                if 0 <= i + 3 < NT:
                    transpose_y(base + i + 3)
                if 0 <= i - 1 < NT:
                    transpose_o(base + i - 1)
                t = i + 2
                if 0 <= t < NT:
                    n, k, b = base + t, k0 + t, t // TB
                    pe.wait_ge(q_done, k + 1)
                    scores_bank_free(n)
                    pe.wait_ge(kblk_done, 2 * l + b + 1)
                    mm(pS[n % 2][:, :], qT[:, k % 2, :],
                       kblk[l][:, b, :, :].rearrange("p h k -> p (h k)")).then_inc(proj_ps, 1)
                t = i
                if 0 <= t < NT:
                    n, k, b = base + t, k0 + t, t // TB
                    pe.wait_ge(eT_done, k + 1)
                    if l == 0:
                        pe.wait_ge(vblk_done, 2)
                        at_least(pe, o_done, n)
                    elif t > 0:
                        pe.wait_ge(o_done, n)
                    else:
                        pe.wait_ge(moe_read, NT)
                        pe.wait_ge(vblk_done, 4)
                    w9 = CH * HC9
                    for c in range(HC):
                        m = mm(pO[:, c * w9:(c + 1) * w9], eT[:, k % 2, c * P:(c + 1) * P],
                               vblk[l][:, b, c, :, :].rearrange("p j d -> p (j d)"))
                    m.then_inc(o_ps, 1)
                t = i + 3
                if 0 <= t < NT:
                    pe.wait_ge(yT_done, base + t + 1)
                    if l == 0 and t == 0:
                        pe.wait_ge(wT_done, 1)
                    mm(pTA[:, 256:256 + P], wT[l][:, 0, :], yT[:, (base + t) % 2, :]).then_inc(q_ps, 1)
                if 0 <= i - 1 < NT:
                    at = (BO0, BO1)[l]
                    project_o(base + i - 1, wT[l][:, 3, :], brow[:, at:at + D])
                if l == 0 and 0 <= i < PARTS:
                    weights_ready(i)

            def heads(i):
                if 0 <= i + 2 < NT:
                    transpose_y(NT + i + 2)
                t = i - 3
                if 0 <= t < NT:
                    for j in range(2):
                        pe.wait_ge(hgate_done[j], t + 1)
                        at_least(pe, hgT_done, 2 * t)
                        if t == 0:
                            pe.wait_ge(eT_done, NT)
                        for k in range(E0 // 2):
                            m = transpose(pE[j][:, k * P:(k + 1) * P], hgate[:, j * E0 // 2 + k, :], ident[:, :])
                        m.then_inc(hgT_ps, 1)
                if 0 <= i + 2 < NT:
                    n = NT + i + 2
                    scores_bank_free(n)
                    bias(pS[n % 2][:, 0:3 * D], brow[:, BQKV:BQKV + 3 * D])
                    pe.wait_ge(yT_done, n + 1)
                    mm(pS[n % 2][:, 0:3 * D], yT[:, n % 2, :], wqkv[:, :], start=False, stop=True).then_inc(proj_ps, 1)

                def experts(half):
                    t = i - 3
                    if 0 <= t < NT:
                        at_least(pe, moe_read, t)
                        if t == 0:
                            pe.wait_ge(o_done, NT)
                        pe.wait_ge(hgT_done, 2 * t + 1 + half)
                        for k in range(half * E0 // 2, (half + 1) * E0 // 2):
                            m = mm(pO[:, P:2 * P], hgateT[:, k * P:(k + 1) * P], we[:, k, :], start=k == 0, stop=k == E0 - 1)
                        if half == 1:
                            m.then_inc(moe_ps, 1)

                experts(0)
                t = i - 2
                if 0 <= t < NT:
                    pe.wait_ge(h2_done, t + 1)
                    pe.wait_ge(oT_done, NT + t + 1)
                    at_least(pe, h2T_done, t)
                    transpose(pTB[:, P:2 * P], h2[:, t % 2, :], ident[:, :]).then_inc(h2T_ps, 1)
                    pe.wait_ge(w_read, NT + t + 1)
                    bias(pW[:, 256:256 + E0], brow[:, BG:BG + E0])
                    pe.wait_ge(h2T_done, t + 1)
                    mm(pW[:, 256:256 + E0], h2T[:, :], wg[:, :], start=False, stop=True).then_inc(gl_ps, 1)
                experts(1)
                if 0 <= i - 1 < NT:
                    transpose_o(NT + i - 1)
                    project_o(NT + i - 1, fo[:, :], brow[:, BOF:BOF + D])

            def router(i):
                if 0 <= i + 2 < NT:
                    transpose_y(3 * NT + i + 2)
                t = i + 1
                if 0 <= t < NT:
                    n = 3 * NT + t
                    scores_bank_free(n)
                    bias(pS[n % 2][:, 0:E1], brow[:, BR:BR + E1])
                    pe.wait_ge(yT_done, n + 1)
                    mm(pS[n % 2][:, 0:E1], yTD[:, t * P:(t + 1) * P], wr[:, :], start=False, stop=True).then_inc(proj_ps, 1)

            for stage, i in SCHEDULE:
                if (stage, i) == ("A", -1):
                    values0()
                if (stage, i) == ("B", -2):
                    pe.wait_ge(wkv_done, 1)
                    pe.wait_ge(part_read, PARTS)
                    pe.wait_ge(scaled0, 3)
                    pe.wait_ge(ld_rows[2], 16 * 5)
                    pe.wait_ge(ld_ffn1, 16)
                {"A": lambda i: attention(0, i), "B": heads, "C": lambda i: attention(1, i), "D": router}[stage](i)

            def transpose_scores():
                pe.wait_ge(rsc_done, NT)
                for j in range(TB):
                    m = transpose(pTB[:, j * P:(j + 1) * P], rsc[:, j, :, :].rearrange("p b e -> p (b e)"), ident[:, :])
                m.then_inc(rT_ps, 1)

            def split_product(dst, c, which, b):
                cols = slice(b * HALF, (b + 1) * HALF)
                high, low = ws[:, c, which, 0, :], ws[:, c, which, 1, :]
                mm(dst, high, xh[:, cols], start=True, stop=False)
                mm(dst, high, xl[:, cols], start=False, stop=False)
                return mm(dst, low, xh[:, cols], start=False, stop=True)

            pe.wait_ge(ld_up, 16 * 5)
            pe.wait_ge(w_low, PIECES)
            pe.wait_ge(x_low, NT)
            pe.wait_ge(rex_done, NT)
            pe.wait_ge(w_read, 3 * NT)
            for u, (c, b) in enumerate(UNITS):
                at_least(pe, silu_done, u - 1)
                split_product(pS[b][:, :], c, 0, b).then_inc(up_ps, 1)
                if u == 0:
                    transpose_scores()
                at_least(pe, gsb_done, u - 1)
                split_product(pE[b][:, :], c, 1, b).then_inc(gate_ps, 1)
            pe.wait_ge(pick_vec, 1)
            pe.wait_ge(rT_done, 2)
            dg = diag.rearrange("p c q -> p (c q)")
            for b in range(2):
                m = mm((pTA, pTB)[b][:, :], ones[:, 0:P], dg[:, b * HALF:(b + 1) * HALF])
            m.then_inc(pick_ps, 1)
            pe.wait_ge(pick_vec, 2)
            transpose(pO[0:1, 0:P], st2[:, 0:1], ident[:, :]).then_inc(pick_ps, 1)
            pe.wait_ge(pick_vec, 3)
            mm(pO[:, 256:257], ones[0:1, 0:P], lmax[0:1, 0:1]).then_inc(pick_ps, 1)
            pe.wait_ge(pick_vec, 4)
            tie, incl = small[:, 2, :], small[:, 3, :]
            mm(pW[:, 0:GH], upto[:, :], tie, start=True, stop=False)
            mm(pW[:, 0:GH], samehalf[:, :], incl, start=False, stop=False)
            mm(pW[:, 0:GH], low2high[:, :], incl[:, GH - 1:GH].to_broadcast([P, GH]), start=False, stop=True).then_inc(pick_ps, 1)
            pe.wait_ge(pick_vec, 5)
            mm(pO[:, 0:2], swap[:, :], st2[:, 2:4]).then_inc(pick_ps, 1)
            pe.wait_ge(pick_vec, 6)
            mm(pW[:, 0:2], swap[:, :], st2[:, 4:6]).then_inc(pick_ps, 1)
            pe.wait_ge(silu_done, len(UNITS))
            pe.wait_ge(hg_pool, len(UNITS))
            pe.wait_ge(sel_done, 2)
            pe.wait_ge(allgs_done, 2)

            def spread(u):
                c, b = TAIL[u]
                at_least(pe, h_done, u - 3)
                for part in range(2):
                    if u == 0:
                        pe.wait_ge(fs_done, part + 1)
                    m = mm(BC[u % 4][:, :], sel[:, b, c, :], fsr[:, part, :], start=part == 0, stop=part == 1)
                m.then_inc(bc_ps, 1)

            def result(b):
                pe.wait_ge(fT_done, b + 1)
                for j in range(TB):
                    m = transpose(RESULT[b][:, j * P:(j + 1) * P],
                                  fT[:, b * HALF + j * P:b * HALF + (j + 1) * P], ident[:, :])
                m.then_inc(res_ps, 1)

            for u in range(4):
                spread(u)
            pe.wait_ge(wdn_low, 2)
            for u, (c, b) in enumerate(TAIL):
                if u + 4 < len(TAIL):
                    spread(u + 4)
                if u == 3:
                    pe.wait_ge(fs_whole, 1)
                    for j in range(TB):
                        m = mm(pO[:, 2 * j:2 * j + 2], fs[:, j * P:(j + 1) * P], halfcol[:, :])
                    m.then_inc(den_ps, 1)
                k, cc = divmod(c, NC // 2)
                pe.wait_ge(h_high, u + 1)
                mm(pE[b][:, :], wd[0][k][:, cc, :], hr[:, 0, u % 4, :], start=c == 0, stop=False)
                mm(pE[b][:, :], wd[1][k][:, cc, :], hr[:, 0, u % 4, :], start=False, stop=False)
                if u % 2 == 0:
                    pe.wait_ge(h_low_pool, u // 2 + 1)
                else:
                    pe.wait_ge(h_low_vec, u // 2 + 1)
                if c == NC - 1:
                    mm(pE[b][:, :], bdn[:, b, :], fs[:, :], start=False, stop=False)
                last = mm(pE[b][:, :], wd[0][k][:, cc, :], hr[:, 1, u % 4, :], start=False, stop=c == NC - 1)
                last.then_inc(down_used, 1)
                if u == NC + 6:
                    result(0)
            result(1)

        @block.vector
        def _(dve):
            v = nc.vector
            steps = Steps(dve, vec_steps)
            v.memset(brow[:, :], 0.0).then_inc(rows_zero, 1)
            for k, val in enumerate((1e-5, 1e-11, 1e-6)):
                v.memset(eps[:, k:k + 1], val).then_inc(eps_set, 1)
            v.memset(bdn[E1:P, 0, :], 0.0).then_inc(bdn_zero, 1)
            v.memset(bdn[0:E1, 1, :], 0.0).then_inc(bdn_zero, 1)

            def masked_values(l, b, src):
                vv = src.rearrange("p (c j d) -> p c j d", c=HC, j=CH)
                v.tensor_copy(vblk[l][:, b, :, :, HD], jmask[:, :].unsqueeze(1).to_broadcast([P, HC, CH]))
                v.tensor_tensor(vblk[l][:, b, :, :, 0:HD], vv,
                                jmask[:, :].unsqueeze(1).unsqueeze(3).to_broadcast([P, HC, CH, HD]),
                                ALU.mult).then_inc(vblk_done, 1)

            def setup0():
                dve.wait_ge(setup_ps, 1)
                v.tensor_copy(ctxT[:, :], pO[:, 0:B * C]).then_inc(ctx_done, 1)
                v.tensor_copy(ctx4[:, :, :, :], pO[:, 0:B * C].rearrange("p (b k) -> p b k", b=B).unsqueeze(2)
                              .to_broadcast([P, B, CH, C])).then_inc(ctx_done, 1)
                dve.wait_ge(setup_ps, 2)
                v.tensor_copy(wT[0][:, 1, :], pE[1][:, 0:D]).then_inc(wk_done, 1)

            def weights_ready(k):
                if k in (3, 5):
                    dve.wait_ge(part_ps, k + 1)
                if k == 3:
                    for b in range(B):
                        masked_values(1, b, pTB[:, P + b * D:P + (b + 1) * D])
                    dve.wait_ge(vblk_done, 4)
                    v.memset(scale3[:, 0, 0:1], 0.0).then_inc(part_read, 1)
                elif k == 5:
                    dve.wait_ge(ld_ffn0, 16 * 10)
                    kvp = pTB[0:1, P:P + 2 * D].rearrange("p (g k d) -> p k g d", g=H, k=2)
                    kvb = bup_row[:, :].rearrange("p (g k d) -> p k g d", g=H, k=2)
                    steps.mark(v.tensor_tensor(brow[0:1, BQKV + D:BQKV + 2 * D].rearrange("p (g d) -> p g d", g=H),
                                               kvp[:, 0], kvb[:, 0], ALU.add))
                    steps.wait()
                    v.tensor_tensor(brow[0:1, BQKV + 2 * D:BQKV + 3 * D].rearrange("p (d g) -> p g d", g=H),
                                    kvp[:, 1], kvb[:, 1], ALU.add).then_inc(part_read, 1)

            def statistics(*tiles):
                for n in tiles:
                    at_least(dve, stats, n - TB + 1)
                    steps.mark(v.bn_stats(st6[:, n % TB, :], x[:, n % NT, :]))
                first = steps.n - len(tiles) + 1
                for k, n in enumerate(tiles):
                    steps.wait(first + k)
                    v.bn_aggr(mv[:, n, :], st6[:, n % TB, :]).then_inc(stats, 1)

            aggregate = {}

            def negative_mean(n):
                steps.wait(aggregate[n])
                v.tensor_scalar(negm[:, n - NT:n - NT + 1], mv[:, n, 0:1], -1.0, None, ALU.mult).then_inc(stats, 1)

            def normalise(n):
                t = n % NT
                dve.wait_ge(rstd_done, n + 1)
                at_least(dve, yT_ps, n - 1)
                v.tensor_scalar(y[:, n % 2, :], x[:, t, :], mv[:, n, 0:1], rstd[:, n:n + 1],
                                ALU.subtract, ALU.mult).then_inc(y_done, 1)

            def shifted_scores(l, t):
                n, k = 2 * l * NT + t, l * NT + t
                s3 = pS[n % 2][:, :].rearrange("p (h k) -> p h k", h=H)
                dve.wait_ge(proj_ps, n + 1)
                if l == 1:
                    if t == 0:
                        dve.wait_ge(ld_mask, 16)
                    steps.mark(v.copy_predicated(s3, maskt[:, t, :].unsqueeze(1).to_broadcast([P, H, C]),
                                                 neg[:, :].unsqueeze(2).to_broadcast([P, H, C])))
                    steps.wait()
                top = steps.mark(v.tensor_reduce(mx[:, k % 2, :], s3, AX.X, ALU.max))
                if l == 0 and POOL_Y <= t - 3:
                    negative_mean(NT + t - 3)
                steps.wait(top)
                at_least(dve, eT_ps, k - 1)
                v.tensor_tensor(e[:, k % 2, :].rearrange("p (h k) -> p h k", h=H), s3,
                                mx[:, k % 2, :].unsqueeze(2).to_broadcast([P, H, C]),
                                ALU.subtract).then_inc(e_shift, 1)

            def attention(l, i):
                base, k0 = 2 * l * NT, l * NT
                if 0 <= i < NT and not ahead(l, i):
                    shifted_scores(l, i)
                if (l, i) == (0, 0):
                    dve.wait_ge(consts, 2)
                    dve.wait_ge(setup_ps, 5)
                    for b in range(B):
                        masked_values(0, b, pW[:, b * D:(b + 1) * D])
                    dve.wait_ge(tg_done, 1)
                t = i - 1
                if 0 <= t < NT:
                    n, k = base + t, k0 + t
                    o9 = pO[:, 0:H * HC9].rearrange("p (h d) -> p h d", h=H)
                    dve.wait_ge(o_ps, k + 1)
                    if l == 0:
                        steps.mark(v.tensor_scalar(den[:, k % 2, :], o9[:, :, HD], 1e-10, None, ALU.add))
                        steps.wait()
                        steps.mark(v.reciprocal(rec[:, k % 2, :], den[:, k % 2, :]))
                    else:
                        steps.mark(v.reciprocal(rec[:, k % 2, :], o9[:, :, HD]))
                    steps.wait()
                    at_least(dve, oT_ps, n - 1)
                    v.tensor_tensor(o[:, n % 2, :].rearrange("p (h d) -> p h d", h=H), o9[:, :, 0:HD],
                                    rec[:, k % 2, :].unsqueeze(2).to_broadcast([P, H, HD]),
                                    ALU.mult).then_inc(o_done, 1)
                if l == 0 and 1 <= i <= PARTS:
                    weights_ready(i - 1)
                t = i - 2
                if 0 <= t < NT:
                    n = base + t
                    dve.wait_ge(w_ps, n + 1)
                    v.scalar_tensor_tensor(out=x[:, t, :], in0=pW[:, 0:D], scalar=tg[:, l:l + 1], in1=x[:, t, :],
                                           op0=ALU.mult, op1=ALU.add).then_inc(w_read, 1)
                    dve.wait_ge(w_read, n + 1)
                    moments = steps.mark(v.bn_stats(st6[:, t % TB, :], x[:, t, :]))
                if l == 0 and 0 <= i + 4 < NT:
                    normalise(base + i + 4)
                if 0 <= t < NT:
                    steps.wait(moments)
                    if l == 0 and t >= POOL_Y:
                        aggregate[n + NT] = steps.mark(v.bn_aggr(mv[:, n + NT, :], st6[:, t % TB, :]))
                        if t >= NT - 3:
                            negative_mean(n + NT)
                    else:
                        v.bn_aggr(mv[:, n + NT, :], st6[:, t % TB, :]).then_inc(stats, 1)

            def heads(i):
                if 0 <= i < NT:
                    dve.wait_ge(mulqk, i + 1)
                    v.tensor_reduce(sB[:, i % 2, :], prod[:, i % 2, :].rearrange("p (s d) -> p s d", d=HD),
                                    AX.X, ALU.add).then_inc(redqk, 1)
                if 0 <= i - 1 < NT:
                    dve.wait_ge(sumB, i)
                    v.reciprocal(rec[:, (i - 1) % 2, :], den[:, (i - 1) % 2, :]).then_inc(recB, 1)
                t = i - 2
                if 0 <= t < NT:
                    dve.wait_ge(w_ps, NT + t + 1)
                    dve.wait_ge(yB_done, t + 1)
                    if t > 0:
                        dve.wait_ge(gex_done, t)
                    at_least(dve, h2_done, t - 1)
                    v.tensor_tensor(xp[:, t % 2, :], pW[:, 0:D], yB[:, t, :], ALU.add).then_inc(w_read, 1)
                if 0 <= i < NT:
                    s3 = sB[:, i % 2, :].rearrange("p (h g) -> p h g", h=H)
                    dve.wait_ge(redqk, i + 1)
                    top = steps.mark(v.tensor_reduce(mx[:, i % 2, :], s3, AX.X, ALU.max))
                if 0 <= t < NT:
                    dve.wait_ge(w_read, NT + t + 1)
                    v.scalar_tensor_tensor(out=x[:, t, :], in0=xp[:, t % 2, :], scalar=tg[:, 2:3], in1=x[:, t, :],
                                           op0=ALU.mult, op1=ALU.add).then_inc(xp_done, 1)
                if 0 <= i < NT:
                    steps.wait(top)
                    v.tensor_tensor(s3, s3, mx[:, i % 2, :].unsqueeze(2).to_broadcast([P, H, H]),
                                    ALU.subtract).then_inc(sB_done, 1)
                t = i - 1
                if 0 <= t < NT:
                    n = NT + t
                    dve.wait_ge(mulav, t + 1)
                    dve.wait_ge(mulav_vec, t + 1)
                    v.tensor_reduce(oraw[:, :], prov[:, t % 2, :].rearrange("p (s g) -> p s g", g=H),
                                    AX.X, ALU.add).then_inc(redav, 1)
                    dve.wait_ge(recB, t + 1)
                    if i < NT:
                        dve.wait_ge(eB_done, i + 1)
                        v.tensor_reduce(den[:, i % 2, :], eB[:, i % 2, :].rearrange("p (h g) -> p h g", h=H),
                                        AX.X, ALU.add).then_inc(sumB, 1)
                    dve.wait_ge(redav, t + 1)
                    at_least(dve, oT_ps, n - 1)
                    v.tensor_tensor(o[:, n % 2, :].rearrange("p (h d) -> p h d", h=H),
                                    oraw[:, :].rearrange("p (h d) -> p h d", h=H),
                                    rec[:, t % 2, :].unsqueeze(2).to_broadcast([P, H, HD]),
                                    ALU.mult).then_inc(o_done, 1)
                t = i - 2
                if 0 <= t < NT:
                    dve.wait_ge(gl_ps, t + 1)
                    v.tensor_reduce(gmx[:, t:t + 1], pW[:, 256:256 + E0], AX.X, ALU.max, negate=True).then_inc(gmx_done, 1)
                if 0 <= i < NT:
                    dve.wait_ge(eB_done, i + 1)
                    w = eB[:, i % 2, :].rearrange("p (h g) -> p h g", h=H)
                    val = qkv[:, i % 4, 2 * D:3 * D].rearrange("p (d g) -> p d g", d=HD)
                    if i == 0:
                        v.tensor_reduce(den[:, i % 2, :], w, AX.X, ALU.add).then_inc(sumB, 1)
                    v.tensor_tensor(prov[:, i % 2, :].rearrange("p (h d g) -> p h d g", h=H, d=HD)[:, HP:H],
                                    w[:, HP:H].unsqueeze(2).to_broadcast([P, H - HP, HD, H]),
                                    val.unsqueeze(1).to_broadcast([P, H - HP, HD, H]), ALU.mult).then_inc(mulav_vec, 1)
                t = i - 2
                if GATES_VEC <= t < NT:
                    dve.wait_ge(gex_done, t + 1)
                    dve.wait_ge(hgT_ps, 2 * t)
                    v.tensor_tensor(hgate[:, E0 // 2:E0, :], h2[:, t % 2, :].unsqueeze(1).to_broadcast([P, E0 // 2, D]),
                                    gex[:, t % 2, E0 // 2:E0].unsqueeze(2).to_broadcast([P, E0 // 2, D]),
                                    ALU.mult).then_inc(hgate_done[1], 1)
                t = i - 3
                if 0 <= t < NT:
                    dve.wait_ge(gex_done, t + 1)
                    steps.mark(v.reciprocal(grec[:, t:t + 1], gsum[:, t:t + 1]))
                    dve.wait_ge(moe_ps, t + 1)
                    dve.wait_ge(xp_done, t + 1)
                    steps.wait()
                    v.scalar_tensor_tensor(out=x[:, t, :], in0=pO[:, P:2 * P], scalar=grec[:, t:t + 1], in1=x[:, t, :],
                                           op0=ALU.mult, op1=ALU.add).then_inc(moe_read, 1)
                    dve.wait_ge(moe_read, t + 1)
                    statistics(2 * NT + t)

            def router(i):
                if 0 <= i < NT:
                    dve.wait_ge(proj_ps, 3 * NT + i + 1)
                    v.tensor_reduce(rmx[:, i:i + 1], pS[i % 2][:, 0:E1], AX.X, ALU.max, negate=True).then_inc(rmx_done, 1)
                if 0 <= i + 3 < NT:
                    normalise(3 * NT + i + 3)
                t = i - 1
                if 0 <= t < NT:
                    dve.wait_ge(rex_done, t + 1)
                    steps.mark(v.reciprocal(rrec[:, t:t + 1], rsum[:, t:t + 1]))
                    steps.wait()
                    v.tensor_scalar(rsc[:, t % TB, t // TB, :], rex[:, t % 2, :], rrec[:, t:t + 1], None,
                                    ALU.mult).then_inc(rsc_done, 1)

            setup0()
            dve.wait_ge(ld_x[0], 16)
            statistics(*range(TB))
            dve.wait_ge(ld_b[0], 32)
            dve.wait_ge(setup_ps, 4)
            v.tensor_scalar(kT[0][:, :], pTA[:, 0:B * C], bcol[:, 1:2], None, ALU.add).then_inc(kT_done[0], 1)
            for stage, i in SCHEDULE:
                if (stage, i) == ("A", -2):
                    dve.wait_ge(ld_x[1], 16)
                    statistics(*range(TB, NT))
                if stage == "B" and ahead(1, i - NT - 1):
                    shifted_scores(1, i - NT - 1)
                {"A": lambda i: attention(0, i), "B": heads, "C": lambda i: attention(1, i), "D": router}[stage](i)

            dve.wait_ge(rT_done, 1)

            def exchange(src, dst, k, j):
                if j is None:
                    s = src[:, :].rearrange("p (b k) -> p b k", k=k)
                    d = dst[:, :].rearrange("p (b k) -> p b k", k=k)
                    lo, hi = s[:, :, 0:k // 2], s[:, :, k // 2:k]
                    lo_back = s[:, :, k // 2 - 1::-1]
                    hi_back = s[:, :, k - 1:k // 2 - 1:-1]
                    dlo, dhi = d[:, :, 0:k // 2], d[:, :, k // 2:k]
                else:
                    s = src[:, :].rearrange("p (b two j) -> p b two j", two=2, j=j)
                    d = dst[:, :].rearrange("p (b two j) -> p b two j", two=2, j=j)
                    lo, hi = s[:, :, 0, :], s[:, :, 1, :]
                    lo_back, hi_back = lo, hi
                    dlo, dhi = d[:, :, 0, :], d[:, :, 1, :]
                steps.mark(v.tensor_tensor(dlo, lo, hi_back, ALU.max))
                steps.mark(v.tensor_tensor(dhi, hi, lo_back, ALU.min))

            src = rT
            stage_no = 0
            for k, j in SORT:
                exchange(src, sort[stage_no % 2], k, j)
                src = sort[stage_no % 2]
                stage_no += 1
                steps.wait()
            lo, hi = slice(0, E1), slice(E1, P)
            dst = sort[stage_no % 2]
            steps.mark(v.tensor_copy(other[lo, :], src[hi, :]))
            steps.mark(v.tensor_copy(other[hi, :], src[lo, :]))
            steps.wait()
            steps.mark(v.tensor_tensor(dst[lo, :], src[lo, :], other[lo, ::-1], ALU.max))
            steps.mark(v.tensor_tensor(dst[hi, :], src[hi, :], other[hi, ::-1], ALU.min))
            src = dst
            stage_no += 1
            steps.wait()
            for k, j in MERGE:
                exchange(src, sort[stage_no % 2], k, j)
                src = sort[stage_no % 2]
                stage_no += 1
                steps.wait()
            groups = src[:, :].rearrange("p (c g) -> p c g", g=G)
            steps.mark(v.tensor_reduce(gs[:, :], groups, AX.X, ALU.add))
            steps.wait()
            v.tensor_tensor(diag, gs[:, :].unsqueeze(2).to_broadcast([P, GH, P]),
                            ident[:, :].unsqueeze(1).to_broadcast([P, GH, P]), ALU.mult).then_inc(pick_vec, 1)
            steps.mark(v.tensor_reduce(gmin[:, :], groups, AX.X, ALU.min))

            count, cand, tie, incl, key, pick, big, gsel = (small[:, k, :] for k in range(8))
            dve.wait_ge(allgs_done, 2)
            dve.wait_ge(hg_pool, len(UNITS))
            for c, adds in COUNTS:
                if adds:
                    k = COUNTED.index(c)
                    at_least(dve, counted, k - 2)
                    v.tensor_scalar(larger[:, k % 3, :], allgs[:, :], gs[:, c:c + 1], None, ALU.is_gt).then_inc(compared, 1)
                else:
                    steps.mark(v.tensor_scalar(junk[:, 0, :], allgs[:, :], gs[:, c:c + 1], None, ALU.is_gt, ALU.add,
                                               accum_out=count[:, c:c + 1]))
                    steps.wait()
            dve.wait_ge(counted, len(COUNTED))
            steps.mark(v.scalar_tensor_tensor(out=cand, in0=count, scalar=float(BUDGET), in1=count,
                                              op0=ALU.is_lt, op1=ALU.mult))
            steps.wait()
            v.tensor_reduce(st2[:, 0:1], cand, AX.X, ALU.max).then_inc(pick_vec, 1)
            dve.wait_ge(pick_ps, 2)
            v.tensor_reduce(lmax[0:1, 0:1], pO[0:1, 0:P], AX.X, ALU.max).then_inc(pick_vec, 1)
            dve.wait_ge(pick_ps, 3)
            steps.mark(v.tensor_scalar(tie, count, pO[:, 256:257], None, ALU.is_equal))
            steps.wait()
            v.tensor_tensor_scan(incl, ones[:, 0:GH], tie, 0.0, ALU.mult, ALU.add).then_inc(pick_vec, 1)
            dve.wait_ge(pick_ps, 4)
            steps.mark(v.scalar_tensor_tensor(out=key, in0=pW[:, 0:GH], scalar=-1.0, in1=tie, op0=ALU.add, op1=ALU.mult))
            steps.wait()
            steps.mark(v.tensor_tensor(key, key, count, ALU.add))
            steps.wait()
            steps.mark(v.tensor_scalar(pick, key, float(BUDGET), None, ALU.is_lt, ALU.add, accum_out=st2[:, 3:4]))
            steps.wait()
            steps.mark(v.tensor_scalar(big, pick, -2.0, 2.0, ALU.mult, ALU.add))
            steps.wait()
            steps.mark(v.tensor_tensor(gsel, big, gmin[:, :], ALU.max))
            steps.wait()
            v.tensor_reduce(st2[:, 2:3], gsel, AX.X, ALU.min).then_inc(pick_vec, 1)
            dve.wait_ge(pick_ps, 5)
            thr, room, need = st2[:, 6:7], st2[:, 7:8], st2[:, 1:2]
            steps.mark(v.tensor_tensor(thr, pO[:, 0:1], st2[:, 2:3], ALU.min))
            steps.mark(v.tensor_scalar(room, pO[:, 1:2], st2[:, 3:4], float(G), ALU.add, ALU.mult))
            steps.wait()

            steps.mark(v.tensor_scalar(eq[:, :], rT[:, :], thr, None, ALU.is_equal, ALU.add, accum_out=st2[:, 5:6]))
            v.tensor_scalar(gt[:, :], rT[:, :], thr, None, ALU.is_gt, ALU.add, accum_out=st2[:, 4:5]).then_inc(pick_vec, 1)
            steps.wait()
            steps.mark(v.tensor_tensor_scan(cum[:, :], ones[:, :], eq[:, :], 0.0, ALU.mult, ALU.add))
            dve.wait_ge(pick_vec, 6)
            dve.wait_ge(pick_ps, 6)
            steps.mark(v.tensor_scalar(need, pW[:, 0:1], st2[:, 4:5], -1.0, ALU.add, ALU.mult))
            steps.wait()
            steps.mark(v.tensor_tensor(need, need, room, ALU.add))
            steps.wait()
            steps.mark(v.tensor_tensor(room, pW[:, 1:2], high[:, :], ALU.mult))
            steps.wait()
            steps.mark(v.tensor_tensor(need, need, room, ALU.subtract))
            steps.wait()
            steps.mark(v.scalar_tensor_tensor(out=eq[:, :], in0=cum[:, :], scalar=need, in1=eq[:, :],
                                              op0=ALU.is_le, op1=ALU.mult))
            steps.wait()
            v.tensor_tensor(gt[:, :], gt[:, :], eq[:, :], ALU.add).then_inc(mask_done, 1)
            dve.wait_ge(mask_done, 1)
            dve.wait_ge(rT_low, 1)
            for part in range(2):
                v.tensor_tensor(fsr[:, part, :], gt[:, :], fsr[:, part, :].bitcast(F32), ALU.mult).then_inc(fs_done, 1)

            dve.wait_ge(hg_pool, len(UNITS))
            def low_part(u):
                if u > 0 and u % 2 == 1:
                    dve.wait_ge(h_high, u + 1)
                    v.tensor_tensor(hr[:, 1, u % 4, :], hidden_values(*TAIL[u]), hr[:, 0, u % 4, :].bitcast(F32),
                                    ALU.subtract).then_inc(h_low_vec, 1)

            def results(b):
                dve.wait_ge(res_ps, b + 1)
                for j in range(TB):
                    t = b * TB + j
                    v.scalar_tensor_tensor(out=res[:, t, :], in0=RESULT[b][:, j * P:(j + 1) * P],
                                           scalar=rden[:, b, j:j + 1], in1=x[:, t, :],
                                           op0=ALU.mult, op1=ALU.add).then_inc(res_done, 1)

            for u, (c, b) in enumerate(TAIL):
                dve.wait_ge(bc_ps, u + 1)
                part = hidden_values(c, b)
                v.tensor_tensor(part, BC[u % 4][:, :], part, ALU.mult).then_inc(h_done, 1)
                low_part(u - 1)
                if u == 7:
                    dve.wait_ge(den_ps, 1)
                    steps.mark(v.tensor_scalar(rden[:, :, :], pO[:, 0:2 * TB].rearrange("p (j b) -> p b j", b=2),
                                               1e-6, None, ALU.add))
                    steps.wait()
                    steps.mark(v.reciprocal(scale3[:, :, :], rden[:, :, :]))
                    steps.wait()
                    steps.mark(v.tensor_scalar(rden[:, :, :], scale3[:, :, :], tg[:, 3:4], None, ALU.mult))
                    steps.wait()
                if u == NC + 10:
                    results(0)
            low_part(len(TAIL) - 1)
            results(1)




def kernel(**inputs):
    import numpy as _np
    import concourse.bacc as _bacc
    from concourse import mybir as _mybir
    from concourse.bass_utils import run_bass_kernel_spmd as _run

    nc = _bacc.Bacc("TRN2", target_bir_lowering=False, num_devices=1)
    arrays, args = {}, {}
    for name, value in inputs.items():
        arr = _np.ascontiguousarray(value)
        arrays[f"in_{name}"] = arr
        args[name] = nc.dram_tensor(f"in_{name}", arr.shape, _mybir.dt.from_np(arr.dtype), kind="ExternalInput").ap()
    out = nc.dram_tensor("out_0", inputs["x"].shape, _mybir.dt.float32, kind="ExternalOutput").ap()
    gated_layers(nc, args, out)
    r = _run(nc, [arrays], core_ids=[0])
    return r.results[0]["out_0"]
```
